# Optimizing a Trainium2 kernel written in Bass

```python
import numpy as np
import jax
import jax.numpy as jnp

def _softmax(x, axis=-1):
    return jax.nn.softmax(x, axis=axis)

def _gelu(x):
    return jax.nn.gelu(x, approximate=True)

def _silu(x):
    return jax.nn.silu(x)

def _sigmoid(x):
    return jax.nn.sigmoid(x)

def _layernorm(x, axis=-1, eps=1e-05):
    m = jnp.mean(x, axis=axis, keepdims=True)
    v = jnp.var(x, axis=axis, keepdims=True)
    return (x - m) / jnp.sqrt(v + eps)

def _scatter_add(tgt, idx, src, axis=0):
    return tgt.at[idx].add(src)

def _segment_sum(src, seg, n):
    return jax.ops.segment_sum(src, seg, n)
kernel_name = 'mk_gnn_ffn_d1_gnn_r16_d79496'

def setup_inputs(seed: int=0):
    np.random.seed(seed)
    _w = jnp.asarray

    def _rec_inputs():
        import jax
        import jax.numpy as jnp
        _gk = jax.random.key(seed)
        x = 7.22e-05 + 1 * jax.random.normal(jax.random.fold_in(_gk, 1), (3125, 256), jnp.float32)
        src = jax.random.randint(jax.random.fold_in(_gk, 2), (100000,), 0, 3125, jnp.int32)
        dst = jnp.minimum((3125 * jax.random.uniform(jax.random.fold_in(_gk, 3), (100000,)) ** 2.0).astype(jnp.int32), 49999)
        _o = jnp.argsort(dst, stable=True)
        src = src[_o]
        dst = dst[_o]
        return (x, src, dst)
    x, src, dst = _rec_inputs()

    def _L0_gnn_setup():
        import jax, jax.numpy as jnp
        import numpy as np
        import math
        N = 2048
        E = N * 16
        D = 256
        H = 8
        DH = 32
        TD = H * DH
        FFN = 1024
        L = 2
        EPS = 1e-05

        def _layernorm(x, g, b):
            mu = jnp.mean(x, axis=-1, keepdims=True)
            var = jnp.mean(jnp.square(x - mu), axis=-1, keepdims=True)
            return (x - mu) * jax.lax.rsqrt(var + EPS) * g + b
        key = jax.random.key(seed)
        ks = jax.random.split(key, 16)
        w = lambda k, *s: jax.random.normal(k, s, dtype=jnp.float32) * 0.02
        return {'x': jax.random.normal(ks[0], (N, D), dtype=jnp.float32), 'edge_index': jax.random.randint(ks[1], (2, E), 0, N, dtype=jnp.int64).astype(jnp.int32), 'w_in': w(ks[2], D, D), 'b_in': jnp.zeros((D,), jnp.float32), 'ln1_g': jnp.ones((L, D), jnp.float32), 'ln1_b': jnp.zeros((L, D), jnp.float32), 'ln2_g': jnp.ones((L, D), jnp.float32), 'ln2_b': jnp.zeros((L, D), jnp.float32), 'wq': w(ks[3], L, D, TD), 'bq': jnp.zeros((L, TD), jnp.float32), 'wk': w(ks[4], L, D, TD), 'bk': jnp.zeros((L, TD), jnp.float32), 'wv': w(ks[5], L, D, TD), 'bv': jnp.zeros((L, TD), jnp.float32), 'wo': w(ks[6], L, TD, D), 'bo': jnp.zeros((L, D), jnp.float32), 'w1': w(ks[7], L, D, FFN), 'b1': jnp.zeros((L, FFN), jnp.float32), 'w2': w(ks[8], L, FFN, D), 'b2': jnp.zeros((L, D), jnp.float32)}
    _L0_gnn_all = _L0_gnn_setup()
    _L0_gnn_in = {k: v for k, v in _L0_gnn_all.items() if k in ('w_in', 'b_in', 'ln1_g', 'ln1_b', 'ln2_g', 'ln2_b', 'wq', 'bq', 'wk', 'bk', 'wv', 'bv', 'wo', 'bo', 'w1', 'b1', 'w2', 'b2')}
    del _L0_gnn_all

    def _L0_ffn_setup():
        import math
        import jax, jax.numpy as jnp
        import numpy as np
        CAPACITY_FACTOR = 1.25
        TOP_K = 2
        LN_EPS = 1e-05

        def _layer_norm(x, gamma, beta):
            mu = jnp.mean(x, axis=-1, keepdims=True)
            var = jnp.var(x, axis=-1, keepdims=True)
            return (x - mu) * jax.lax.rsqrt(var + LN_EPS) * gamma + beta
        key = jax.random.key(seed)
        ks = jax.random.split(key, 4)
        B, S, D, F, E = (8, 256, 256, 512, 8)
        x = jax.random.normal(ks[0], (B, S, D), dtype=jnp.float32)
        Wr = jax.random.normal(ks[1], (D, E), dtype=jnp.float32) / np.sqrt(D)
        br = jnp.zeros((E,), jnp.float32)
        W1 = jax.random.normal(ks[2], (E, D, F), dtype=jnp.float32) / np.sqrt(D)
        b1 = jnp.zeros((E, F), jnp.float32)
        W2 = jax.random.normal(ks[3], (E, F, D), dtype=jnp.float32) / np.sqrt(F)
        b2 = jnp.zeros((E, D), jnp.float32)
        gamma = jnp.ones((D,), jnp.float32)
        beta = jnp.zeros((D,), jnp.float32)
        return {'x': x, 'Wr': Wr, 'br': br, 'W1': W1, 'b1': b1, 'W2': W2, 'b2': b2, 'gamma': gamma, 'beta': beta}
    _L0_ffn_all = _L0_ffn_setup()
    _L0_ffn_in = {k: v for k, v in _L0_ffn_all.items() if k in ('Wr', 'br', 'W1', 'b1', 'W2', 'b2', 'gamma', 'beta')}
    del _L0_ffn_all
    return {'x': x, 'src': src, 'dst': dst, 'L0_gnn_w_in': _L0_gnn_in['w_in'], 'L0_gnn_b_in': _L0_gnn_in['b_in'], 'L0_gnn_ln1_g': _L0_gnn_in['ln1_g'], 'L0_gnn_ln1_b': _L0_gnn_in['ln1_b'], 'L0_gnn_ln2_g': _L0_gnn_in['ln2_g'], 'L0_gnn_ln2_b': _L0_gnn_in['ln2_b'], 'L0_gnn_wq': _L0_gnn_in['wq'], 'L0_gnn_bq': _L0_gnn_in['bq'], 'L0_gnn_wk': _L0_gnn_in['wk'], 'L0_gnn_bk': _L0_gnn_in['bk'], 'L0_gnn_wv': _L0_gnn_in['wv'], 'L0_gnn_bv': _L0_gnn_in['bv'], 'L0_gnn_wo': _L0_gnn_in['wo'], 'L0_gnn_bo': _L0_gnn_in['bo'], 'L0_gnn_w1': _L0_gnn_in['w1'], 'L0_gnn_b1': _L0_gnn_in['b1'], 'L0_gnn_w2': _L0_gnn_in['w2'], 'L0_gnn_b2': _L0_gnn_in['b2'], 'L0_ffn_Wr': _L0_ffn_in['Wr'], 'L0_ffn_br': _L0_ffn_in['br'], 'L0_ffn_W1': _L0_ffn_in['W1'], 'L0_ffn_b1': _L0_ffn_in['b1'], 'L0_ffn_W2': _L0_ffn_in['W2'], 'L0_ffn_b2': _L0_ffn_in['b2'], 'L0_ffn_gamma': _L0_ffn_in['gamma'], 'L0_ffn_beta': _L0_ffn_in['beta']}

def reference(x, src, dst, L0_gnn_w_in, L0_gnn_b_in, L0_gnn_ln1_g, L0_gnn_ln1_b, L0_gnn_ln2_g, L0_gnn_ln2_b, L0_gnn_wq, L0_gnn_bq, L0_gnn_wk, L0_gnn_bk, L0_gnn_wv, L0_gnn_bv, L0_gnn_wo, L0_gnn_bo, L0_gnn_w1, L0_gnn_b1, L0_gnn_w2, L0_gnn_b2, L0_ffn_Wr, L0_ffn_br, L0_ffn_W1, L0_ffn_b1, L0_ffn_W2, L0_ffn_b2, L0_ffn_gamma, L0_ffn_beta):
    import jax
    import jax.numpy as jnp

    def _L0_gnn_ref(x, edge_index, w_in, b_in, ln1_g, ln1_b, ln2_g, ln2_b, wq, bq, wk, bk, wv, bv, wo, bo, w1, b1, w2, b2):
        import jax, jax.numpy as jnp
        import numpy as np
        import math
        N = 2048
        E = N * 16
        D = 256
        H = 8
        DH = 32
        TD = H * DH
        FFN = 1024
        L = 2
        EPS = 1e-05

        def _layernorm(x, g, b):
            mu = jnp.mean(x, axis=-1, keepdims=True)
            var = jnp.mean(jnp.square(x - mu), axis=-1, keepdims=True)
            return (x - mu) * jax.lax.rsqrt(var + EPS) * g + b
        n = x.shape[0]
        src0, dst0 = (edge_index[0], edge_index[1])
        deg = jax.ops.segment_sum(jnp.ones_like(src0, jnp.float32), dst0, num_segments=n)
        ar = jnp.arange(n, dtype=src0.dtype)
        src = jnp.concatenate([src0, ar])
        dst = jnp.concatenate([dst0, ar])
        h = x @ w_in + b_in
        scale = 1.0 / math.sqrt(DH)
        for l in range(L):
            xn = _layernorm(h, ln1_g[l], ln1_b[l])
            q = (xn @ wq[l] + bq[l]).reshape(n, H, DH)
            k = (xn @ wk[l] + bk[l]).reshape(n, H, DH)
            v = (xn @ wv[l] + bv[l]).reshape(n, H, DH)
            scores = jnp.einsum('ehd,ehd->eh', q[dst], k[src]) * scale
            m = jax.ops.segment_max(scores, dst, num_segments=n)
            ex = jnp.exp(scores - m[dst])
            z = jax.ops.segment_sum(ex, dst, num_segments=n)
            attn = ex / z[dst]
            agg = jax.ops.segment_sum(attn[:, :, None] * v[src], dst, num_segments=n)
            agg = jnp.where((deg > 0)[:, None, None], agg, 0.0)
            h = h + agg.reshape(n, TD) @ wo[l] + bo[l] * jnp.where(deg > 0, 1.0, 1.0)[:, None] * 0 + agg.reshape(n, TD) @ wo[l] * 0
            h = h - agg.reshape(n, TD) @ wo[l]
            h = h + (agg.reshape(n, TD) @ wo[l] + bo[l]) - bo[l] * 0
            xn2 = _layernorm(h, ln2_g[l], ln2_b[l])
            ffn = jax.nn.gelu(xn2 @ w1[l] + b1[l], approximate=False) @ w2[l] + b2[l]
            h = h + ffn
        return h

    def _L0_ffn_ref(x, Wr, br, W1, b1, W2, b2, gamma, beta):
        import math
        import jax, jax.numpy as jnp
        import numpy as np
        CAPACITY_FACTOR = 1.25
        TOP_K = 2
        LN_EPS = 1e-05

        def _layer_norm(x, gamma, beta):
            mu = jnp.mean(x, axis=-1, keepdims=True)
            var = jnp.var(x, axis=-1, keepdims=True)
            return (x - mu) * jax.lax.rsqrt(var + LN_EPS) * gamma + beta
        B, S, D = x.shape
        E = Wr.shape[1]
        N = B * S
        K = TOP_K
        logits = jnp.mean(x, axis=1) @ Wr + br
        routing_weights = jax.nn.softmax(logits, axis=-1)
        capacity = float(math.ceil(N * CAPACITY_FACTOR / E))
        expected_loads = routing_weights.sum(axis=0) * (N / B)
        scale = jnp.where(expected_loads > capacity, capacity / expected_loads, 1.0)
        routing_weights = jax.nn.softmax(routing_weights * scale, axis=-1)
        rw_tok = jnp.broadcast_to(routing_weights[:, None, :], (B, S, E)).reshape(N, E)
        top_w, top_i = jax.lax.top_k(rw_tok, K)
        top_w = jax.nn.softmax(top_w, axis=-1)
        xf = x.reshape(N, D)
        h = jax.nn.gelu(jnp.einsum('nd,edf->enf', xf, W1) + b1[:, None, :], approximate=False)
        y = jnp.einsum('enf,efd->end', h, W2) + b2[:, None, :]
        w_dense = jnp.zeros((N, E), x.dtype).at[jnp.arange(N)[:, None], top_i].add(top_w)
        out = jnp.einsum('ne,end->nd', w_dense, y).reshape(B, S, D)
        out = _layer_norm(out + x, gamma, beta)
        return out
    edge_index = jnp.stack([src, dst])
    x = x + _L0_gnn_ref(_layernorm(x, axis=-1), edge_index, L0_gnn_w_in, L0_gnn_b_in, L0_gnn_ln1_g, L0_gnn_ln1_b, L0_gnn_ln2_g, L0_gnn_ln2_b, L0_gnn_wq, L0_gnn_bq, L0_gnn_wk, L0_gnn_bk, L0_gnn_wv, L0_gnn_bv, L0_gnn_wo, L0_gnn_bo, L0_gnn_w1, L0_gnn_b1, L0_gnn_w2, L0_gnn_b2)
    x = x + _L0_ffn_ref(_layernorm(x, axis=-1)[None], L0_ffn_Wr, L0_ffn_br, L0_ffn_W1, L0_ffn_b1, L0_ffn_W2, L0_ffn_b2, L0_ffn_gamma, L0_ffn_beta)[0]
    return x

_drawn_inputs = setup_inputs


def setup_inputs(seed=0):
    import zlib

    import numpy as np

    out = dict(_drawn_inputs(seed))
    spreads = {'L0_gnn_b_in': (0.0, 0.1),
     'L0_gnn_ln1_g': (1.0, 0.6),
     'L0_gnn_ln1_b': (0.0, 0.534),
     'L0_gnn_ln2_g': (1.0, 0.2),
     'L0_gnn_ln2_b': (0.0, 0.49),
     'L0_gnn_bq': (0.0, 0.8),
     'L0_gnn_bk': (0.0, 0.8),
     'L0_gnn_bv': (0.0, 0.1),
     'L0_gnn_bo': (0.0, 0.1),
     'L0_gnn_b1': (0.0, 0.1),
     'L0_gnn_b2': (0.0, 0.1),
     'L0_ffn_br': (0.0, 0.1),
     'L0_ffn_b1': (0.0, 0.372),
     'L0_ffn_b2': (0.0, 0.1),
     'L0_ffn_gamma': (1.0, 0.2),
     'L0_ffn_beta': (0.0, 0.1)}
    factors = {'L0_gnn_wq': 8.0, 'L0_gnn_wk': 8.0}
    for name, (base, spread) in spreads.items():
        noise = np.random.default_rng([zlib.crc32(name.encode()), seed]).standard_normal(out[name].shape)
        drawn = base * np.exp(spread * noise) if base else spread * noise
        out[name] = jnp.asarray(drawn.astype(out[name].dtype))
    for name, factor in factors.items():
        out[name] = (out[name] * factor).astype(out[name].dtype)
    return out
```

```python
from contextlib import ExitStack

import concourse.bass as bass
from concourse import mybir

ALU = mybir.AluOpType
ACT = mybir.ActivationFunctionType
AX = mybir.AxisListType
F32 = mybir.dt.float32
BF16 = mybir.dt.bfloat16
I32 = mybir.dt.int32
U32 = mybir.dt.uint32

N, D, E = 3125, 256, 100000
H, DH = 8, 32
LAYERS, FFN = 2, 1024
NEXP, FE, TOPK = 8, 512, 2
EPS = 1e-5
CAPACITY = float(-(-(N * 125) // (NEXP * 100)))

P = 128
TN = 125
NT = N // TN
BT = 5
NBATCH = NT // BT

BLK = 512
NBLK = -(-E // BLK)
CH = BLK // P
VG = 4
NG = -(-(NBLK + NT - 1) // VG)
NG += NG % 2
NV = NG * VG
GC = VG * CH
NC = NV * CH
HV = NV // 2
LB = NBLK // 2
BIG = 1e30

ROW = 2 * D
WOFF = D - 2 * H
WCOL = D + 2 * H
QC = D + H
RING = 2 * GC * ROW


def hold(eng, sem, value, passed):
    eng.wait_ge(sem, value)
    eng.sem_inc(passed, 1)


class Steps:

    def __init__(self, sem, base=0):
        self.sem, self.base, self.n = sem, base, 0

    def did(self, ins):
        ins.then_inc(self.sem, 1)
        self.n += 1
        return self.n

    def sync(self, eng, n=None):
        eng.wait_ge(self.sem, self.base + (self.n if n is None else n))


PASSES = {
    "in": ["norm", "turn", "proj", "norm", "turn", "qkv"],
    "mid": ["agg", "turn", "proj", "norm", "turn", "mlp", "norm", "turn", "qkv"],
    "last": ["agg", "turn", "proj", "norm", "turn", "mlp", "norm"],
    "moe": ["take", "turn", "mlp", "norm"],
}
def count(kind, *names):
    return sum(s in names for s in PASSES[kind])


PREP_IND = 15
C_SP, C_ENDS, C_XY, C_DM, C_ALPHA, C_MU, C_ARG, C_SELF = 1, 5, 8, 10, 13, 18, 22, 23
R_MEAN, R_E1, R_E2, R_E3, R_TOPW, R_WEIGHTS = 1, 4, 17, 38, 41, 46
W_STEPS = {"in": 7, "mid": 10, "last": 3}
D_STEPS = {"in": 21, "mid": 26, "last": 21, "moe": 25}


def program(nc, A, out):
    ctx = ExitStack()
    with ctx, nc.allow_non_contiguous_dma(reason="index tables and columns of vectors, once"):
        def sb(name, shape, dt=F32):
            return ctx.enter_context(nc.sbuf_tensor(name, shape, dt))

        def sem(name):
            return ctx.enter_context(nc.semaphore(name))

        def scratch(name, shape, dt=F32):
            return nc.dram_tensor(name, shape, dt, kind="Internal").ap()

        src_rows = scratch("src_rows", [NBLK + 1, BLK], I32)
        dst_rows = scratch("dst_rows", [NBLK + 1, BLK], I32)
        key_line = scratch("key_line", [1, NC * P + 2])
        dl_line = scratch("dl_line", [1, NC * P], BF16)
        pen_f = scratch("pen_f", [1, NC * P + P], BF16)
        pen_b = scratch("pen_b", [1, NC * P], BF16)
        kv_table = scratch("kv_table", [N, ROW])
        kv_table2 = scratch("kv_table2", [N, ROW])
        h_dram = scratch("h_dram", [N, D])

        ring = sb("ring", [P, RING])
        acc = sb("acc", [TN, NT * WCOL])
        qs = sb("qs", [TN, NT * 3 * QC], BF16)
        src_ix = sb("src_ix", [P, NC], U32)
        dl_col = sb("dl_col", [P, NC])
        last_col = sb("last_col", [P, NC])
        dt = sb("dt", [TN, 2, GC * P], BF16)
        pens = sb("pens", [P, 2, 2, P], BF16)
        stage_ix = sb("stage_ix", [P, 2, GC], U32)
        dhot = sb("dhot", [P, 2 * CH, TN])
        w_qkv = sb("w_qkv", [P, 2, 3 * D])
        w_sq = sb("w_sq", [P, 2, D])
        w_up = sb("w_up", [P, 2, FFN])
        w_down = sb("w_down", [P, FFN // P, D])
        row_qkv = sb("row_qkv", [1, 3 * D])
        row_sq = sb("row_sq", [1, D])
        row_down = sb("row_down", [1, D])
        up_bias = sb("up_bias", [P, FFN // P])
        g_col = sb("g_col", [P, 4, 2])
        ident = sb("ident", [P, P])
        iota_f = sb("iota_f", [P, P])
        iota_p = sb("iota_p", [P, 1])
        ones = sb("ones", [P, P])
        half = sb("half", [P, BT])
        lane_h = sb("lane_h", [P, H])
        lane_hT = sb("lane_hT", [H, P])
        lane_c = sb("lane_c", [P, 2, GC])
        t_row = sb("t_row", [1, NV], I32)
        kp = sb("kp", [H, NC + 1], BF16)
        a_f = sb("a_f", [H, NC], BF16)
        a_b = sb("a_b", [H, NC], BF16)
        dl0 = sb("dl0", [H, NG])
        s_e = sb("s_e", [P, H, GC])
        ss_e = sb("ss_e", [P, H, GC])
        sp_e = sb("sp_e", [P, H, GC])
        f_lane = sb("f_lane", [P, P])
        b_lane = sb("b_lane", [P, P])
        ends = sb("ends", [P, 2, GC])
        runs = sb("runs", [H, 2 * (GC + 2)])
        g_run, h_run = runs[:, 0:GC + 1], runs[:, GC + 1:2 * GC + 2]
        flows = runs[:, :].rearrange("p (a c) -> p a c", a=2)[:, :, 0:GC]
        xy_m = sb("xy_m", [P, 2, GC])
        xy_l = sb("xy_l", [P, 2])
        m_new = sb("m_new", [H, 4])
        r_diag = sb("r_diag", [H, H])
        delta = sb("delta", [H, TN])
        a_fac = sb("a_fac", [TN, H])
        arg = sb("arg", [P, 2, H * GC])
        small = sb("small", [P, 64])
        stat = sb("stat", [TN, BT, 6])
        mv = sb("mv", [TN, BT, 2])
        rs = sb("rs", [TN, BT])
        exp_ix = sb("exp_ix", [1, 2], I32)
        x_in = sb("x_in", [TN, BT, D])
        h_b = sb("h_b", [TN, BT, D])

        o = 0
        def part(n, p=P):
            nonlocal o
            v = ring[0:p, o:o + n]
            o += n
            return v
        up_T = part(FFN // P * BT * TN).rearrange("p (f n) -> p f n", f=FFN // P)
        kv_b = part(BT * ROW, TN).rearrange("p (j c) -> p j c", j=BT)
        tok = part(BT * D, TN).rearrange("p (j c) -> p j c", j=BT)
        tok_T = part(2 * BT * TN).rearrange("p (a n) -> p a n", a=2)
        qf = part(BT * QC, TN).rearrange("p (j c) -> p j c", j=BT)
        qr = part(BT * QC, TN).rearrange("p (j c) -> p j c", j=BT)
        assert o <= RING
        o = 0
        e_i = part(2 * 2 * BLK, HV).rearrange("p (a m e) -> p a m e", a=2, m=2)
        e_src = part(2 * BLK, HV).rearrange("p (m e) -> p m e", m=2)
        e_dst = part(2 * BLK, HV).rearrange("p (m e) -> p m e", m=2)
        e_val = part(2 * BLK, HV).rearrange("p (m e) -> p m e", m=2)
        e_key = part(2 * BLK, HV).rearrange("p (m e) -> p m e", m=2)
        e_dl = part(2 * BLK, HV).rearrange("p (m e) -> p m e", m=2)
        e_prev = part(2 * BLK, HV).rearrange("p (m e) -> p m e", m=2)
        e_next = part(2 * BLK, HV).rearrange("p (m e) -> p m e", m=2)
        o_load = part(E // TN, TN)
        o_load2 = part(E // TN, TN)
        k_first = part(NC, H)
        k_last = part(NC, H)
        fill_m1 = part(BLK, 1)
        fill_0 = part(BLK, 1)
        b_dl = part(BLK, HV).bitcast(BF16).rearrange("p (m e) -> p m e", m=2)
        b_pf = part(BLK, HV).bitcast(BF16).rearrange("p (m e) -> p m e", m=2)
        b_pb = part(BLK, HV).bitcast(BF16).rearrange("p (m e) -> p m e", m=2)
        assert o <= RING

        bank = [ctx.enter_context(nc.psum_tensor(f"bank{i}", [P, 512], F32)) for i in range(8)]
        b_q, b_ss, b_acc, b_ch, b_p, b_mu = bank[0:2], bank[2], bank[3:5], bank[5], bank[6], bank[7]

        chunk = ring[:, :].rearrange("p (g c w) -> p g c w", g=2, c=GC)
        acc_t = acc[:, :].rearrange("p (t w) -> p t w", t=NT)

        iota_v = part(NV)
        ind = part(2 * NV, LB).rearrange("p (a v) -> p a v", a=2)
        assert o <= RING

        S = {n: sem(n) for n in (
            "sp_passed", "pool_passed", "dve_passed", "pool_const", "pads", "edges_in", "edges_copied", "last_in", "prep", "prep_pe", "blocks", "keys", "penalties",
            "prep_done", "edges_over", "rows_in", "lines_out", "lines_in", "turned_rows",
            "w_in_dma", "w_pe", "w_dve", "w_step", "kv_out", "h_out", "out_done", "pass_over",
            "tab0", "tab1", "onehot", "q_ready", "q_used", "score", "ss_ready", "ss_copied",
            "ch_dve", "ch_pe", "ch_act", "ix_staged", "w_ready", "d_ready", "agg", "agg_used", "edge_step", "route",
            "route_dma", "route_pe", "route_act", "chosen")}
        gath = [[sem(f"gath{g}{q}") for q in range(VG)] for g in range(2)]
        PS = {k: {n: sem(f"{n}_{k}") for n in (
            "x_in", "stat", "rs_ready", "rs_step", "dve", "tok", "turned", "evac", "mm", "used", "up", "gelu", "qf", "kvc", "cast", "rest", "done")}
            for k in PASSES}

        CH_DVE, CH_PE, CH_ACT = 23, 5, 4
        W_TOTAL = {"in": 10, "mid": 26, "last": 34}
        PASS_NO = {"in": 0, "mid": 1, "last": 2, "moe": 3}
        b2_rows = x_in[0:1, 0:TOPK, :]
        MLP_CUT = ((0, 3 * TN), (3 * TN, 2 * TN))

        block = ctx.enter_context(nc.Block())
        vec, ten, sca, gps, syn = nc.vector, nc.tensor, nc.scalar, nc.gpsimd, nc.sync


        @block.sync
        def _(sp):
            sp.dma_start(o_load.bitcast(I32), A["src"].rearrange("(p c) -> p c", p=TN)).then_inc(S["edges_in"], 16)
            sp.dma_start(o_load2.bitcast(I32), A["dst"].rearrange("(p c) -> p c", p=TN)).then_inc(S["edges_in"], 16)
            li = small[:, 0:2].bitcast(I32)
            ends_of = A["dst"][0:(NBLK - 1) * BLK].rearrange("(b e) -> b e", e=BLK)
            sp.dma_start(li[0:LB, 0:1], ends_of[0:LB, BLK - 1:BLK]).then_inc(S["last_in"], 16)
            sp.dma_start(li[0:LB - 1, 1:2], ends_of[LB:2 * LB - 1, BLK - 1:BLK]).then_inc(S["last_in"], 16)
            sp.dma_start(li[LB - 1:LB, 1:2], A["dst"].rearrange("(a e) -> a e", a=1)[:, E - 1:E]).then_inc(S["last_in"], 16)
            sp.wait_ge(S["edges_in"], 32)
            sp.wait_ge(S["pads"], 3)
            for rows, col, pad in ((src_rows, o_load, fill_0), (dst_rows, o_load2, fill_m1)):
                line = rows.rearrange("b e -> (b e)")
                sp.dma_start(line[0:E].rearrange("(p c) -> p c", p=TN), col.bitcast(I32)).then_inc(S["edges_copied"], 16)
                n, k = (NBLK + 1) * BLK - E, BLK
                for at, k in ((E, n - BLK), (E + n - BLK, BLK)):
                    sp.dma_start(line[at:at + k].rearrange("(a e) -> a e", a=1), pad[:, 0:k].bitcast(I32)).then_inc(S["edges_copied"], 16)
            sp.wait_ge(S["keys"], 1)
            by_visit = "a (m p e) -> p (a m) e"
            sp.dma_start(key_line[:, 1:1 + NC * P].rearrange(by_visit, m=2, p=HV), e_key).then_inc(S["lines_out"], 16)
            sp.dma_start(key_line[:, 0:1], small[0:1, 10:11]).then_inc(S["lines_out"], 16)
            sp.dma_start(key_line[:, NC * P + 1:NC * P + 2], small[0:1, 10:11]).then_inc(S["lines_out"], 16)
            sp.dma_start(dl_line.rearrange(by_visit, m=2, p=HV), b_dl).then_inc(S["lines_out"], 16)
            sp.wait_ge(S["lines_out"], 64)
            for t, off in ((e_prev, 0), (e_next, 2)):
                sp.dma_start(t, key_line[:, off:off + NC * P].rearrange(by_visit, m=2, p=HV)).then_inc(S["lines_in"], 16)
            firsts = key_line[:, 1:1 + NC * P].rearrange("a (c e) -> (a e) c", e=P)
            for hh in range(H):
                sp.dma_start(k_first[hh:hh + 1, :], firsts[0:1, :]).then_inc(S["lines_in"], 16)
                sp.dma_start(k_last[hh:hh + 1, :], firsts[P - 1:P, :]).then_inc(S["lines_in"], 16)
                sp.dma_start(a_f[hh:hh + 1, 0:NG], dl_line.rearrange("a (g e) -> (a e) g", e=GC * P)[0:1, :]).then_inc(S["lines_in"], 16)
            sp.wait_ge(S["penalties"], 1)
            sp.dma_start(pen_f[:, 0:NC * P].rearrange(by_visit, m=2, p=HV), b_pf).then_inc(S["lines_out"], 16)
            sp.dma_start(pen_b.rearrange(by_visit, m=2, p=HV), b_pb).then_inc(S["lines_out"], 16)
            sp.dma_start(pen_f[:, NC * P:NC * P + P], b_pf[0:1, 0, 0:P]).then_inc(S["lines_out"], 16)
            sp.wait_ge(S["lines_out"], 64 + 48)
            for hh in range(H):
                sp.dma_start(kp[hh:hh + 1, :], pen_f.rearrange("a (c e) -> (a e) c", e=P)[0:1, :]).then_inc(S["lines_in"], 16)

            def load_w(kind, layer):
                todo = []
                if kind == "in":
                    todo += [(w_sq[:, :, :], A["L0_gnn_w_in"].rearrange("(a p) n -> p a n", p=P)),
                             (row_sq[:, :], A["L0_gnn_b_in"].rearrange("(a n) -> a n", a=1))]
                else:
                    todo += [(w_sq[:, :, :], A["L0_gnn_wo"][layer].rearrange("(a p) n -> p a n", p=P)),
                             (row_sq[:, :], A["L0_gnn_bo"][layer:layer + 1, :]),
                             (w_up[:, :, :], A["L0_gnn_w1"][layer].rearrange("(a p) n -> p a n", p=P)),
                             (up_bias[:, :], A["L0_gnn_b1"][layer].rearrange("(f p) -> p f", p=P)),
                             (w_down[:, :, :], A["L0_gnn_w2"][layer].rearrange("(f p) n -> p f n", p=P)),
                             (row_down[:, :], A["L0_gnn_b2"][layer:layer + 1, :]),
                             (g_col[:, 2, :], A["L0_gnn_ln2_g"][layer].rearrange("(a p) -> p a", p=P)),
                             (g_col[:, 3, :], A["L0_gnn_ln2_b"][layer].rearrange("(a p) -> p a", p=P))]
                if kind in ("in", "mid"):
                    nl = 0 if kind == "in" else layer + 1
                    for i, n in enumerate("qkv"):
                        todo += [(w_qkv[:, :, i * D:(i + 1) * D], A[f"L0_gnn_w{n}"][nl].rearrange("(a p) n -> p a n", p=P)),
                                 (row_qkv[:, i * D:(i + 1) * D], A[f"L0_gnn_b{n}"][nl:nl + 1, :])]
                    todo += [(g_col[:, 0, :], A["L0_gnn_ln1_g"][nl].rearrange("(a p) -> p a", p=P)),
                             (g_col[:, 1, :], A["L0_gnn_ln1_b"][nl].rearrange("(a p) -> p a", p=P))]
                for o_, i_ in todo:
                    sp.dma_start(o_, i_).then_inc(S["w_in_dma"], 16)

            def dense(kind):
                s, no = PS[kind], PASS_NO[kind]
                with sp.Fori(0, NBATCH) as it:
                    def rows(t, c0=0, c1=None):
                        return t.rearrange("(t p) c -> p t c", p=TN)[:, bass.ds(it * BT, BT), c0:c1]
                    if kind in ("in", "last"):
                        sp.dma_start(x_in[:, :, :], rows(A["x"])).then_inc(s["x_in"], 16)
                    if kind != "in":
                        sp.dma_start(h_b[:, :, :], rows(h_dram)).then_inc(s["x_in"], 16)
                    if kind in ("mid", "last"):
                        sp.dma_start(kv_b[:, :, D:ROW], rows(kv_in, D, ROW)).then_inc(s["x_in"], 16)
                    if kind in ("in", "mid"):
                        for j in range(BT):
                            hold(sp, s["kvc"], it * BT + j + 1, S["sp_passed"])
                            sp.dma_start(kv_out.rearrange("(t p) c -> p t c", p=TN)[:, bass.ds(it * BT + j, 1), :],
                                         kv_b[:, j:j + 1, :]).then_inc(S["kv_out"], 16)
                    hold(sp, s["done"], it + 1, S["sp_passed"])
                    if kind == "moe":
                        sp.dma_start(rows(out), h_b[:, :, :]).then_inc(S["out_done"], 16)
                        hold(sp, S["out_done"], it * 16 + 16, S["sp_passed"])
                    else:
                        sp.dma_start(rows(h_dram), h_b[:, :, :]).then_inc(S["h_out"], 16)
                        hold(sp, S["h_out"], it * 16 + (no * NBATCH + 1) * 16, S["sp_passed"])
                    if kind in ("in", "mid"):
                        hold(sp, S["kv_out"], it * (BT * 16) + (no * NBATCH + 1) * BT * 16, S["sp_passed"])

            def tables(layer):
                def group(i, par, first):
                    k = i * 2 + par
                    if not first:
                        hold(sp, S["agg"], k * VG + (layer * NV - VG), S["sp_passed"])
                    t = S[f"tab{par}"]
                    for hh in range(H):
                        for d, line in ((0, pen_f), (1, pen_b)):
                            sp.dma_start(pens[hh * GC:(hh + 1) * GC, par, d, :],
                                         line[:, bass.ds(k * (GC * P), GC * P)].rearrange("a (c e) -> (a c) e", e=P)).then_inc(t, 16)
                    sp.dma_start(dt[:, par, :], dl_line[:, bass.ds(k * (GC * P), GC * P)].to_broadcast([TN, GC * P])).then_inc(t, 16)
                group(0, 0, layer == 0)
                group(0, 1, layer == 0)
                with sp.Fori(1, NG // 2) as i:
                    group(i, 0, False)
                    group(i, 1, False)

            sp.wait_ge(S["prep_done"], 1)
            load_w("in", 0)
            kv_in = kv_out = kv_table
            dense("in")
            sp.wait_ge(S["pass_over"], 1)
            load_w("mid", 0)
            tables(0)
            sp.wait_ge(S["agg"], NV)
            sp.wait_ge(S["edges_over"], 1)
            kv_out = kv_table2
            dense("mid")
            kv_in = kv_table2
            sp.wait_ge(S["pass_over"], 2)
            load_w("last", 1)
            tables(1)
            sp.wait_ge(S["edges_over"], 2)
            dense("last")
            sp.wait_ge(S["pass_over"], 3)
            r = S["route_dma"]
            sp.dma_start(w_qkv[:, 0, 0:2 * NEXP].rearrange("p (a n) -> p a n", a=2), A["L0_ffn_Wr"].rearrange("(a p) n -> p a n", p=P)).then_inc(r, 16)
            sp.dma_start(row_qkv[:, 0:NEXP], A["L0_ffn_br"].rearrange("(a n) -> a n", a=1)).then_inc(r, 16)
            sp.dma_start(row_qkv[:, D:2 * D], A["L0_ffn_gamma"].rearrange("(a n) -> a n", a=1)).then_inc(r, 16)
            sp.dma_start(row_qkv[:, 2 * D:3 * D], A["L0_ffn_beta"].rearrange("(a n) -> a n", a=1)).then_inc(r, 16)
            sp.wait_ge(S["chosen"], 1)
            f = FE // P
            for i in range(TOPK):
                ex = sp.value_load(exp_ix[0:1, i:i + 1], min_val=0, max_val=NEXP - 1)
                sp.dma_start(w_up[:, :, i * FE:(i + 1) * FE], A["L0_ffn_W1"].rearrange("x (a p) n -> p (x a) n", p=P)[:, bass.ds(ex * 2, 2), :]).then_inc(r, 16)
                sp.dma_start(up_bias[:, i * f:(i + 1) * f], A["L0_ffn_b1"].rearrange("x (f p) -> p (x f)", p=P)[:, bass.ds(ex * f, f)]).then_inc(r, 16)
                sp.dma_start(w_down[:, i * f:(i + 1) * f, :], A["L0_ffn_W2"].rearrange("x (f p) n -> p (x f) n", p=P)[:, bass.ds(ex * f, f), :]).then_inc(r, 16)
                sp.dma_start(b2_rows[:, i, :], A["L0_ffn_b2"][bass.ds(ex, 1), :]).then_inc(r, 16)
            dense("moe")

        @block.gpsimd
        def _(pool):
            c = S["pool_const"]
            gps.iota(iota_f[:, :], pattern=[[1, P]], base=0, channel_multiplier=0, allow_small_or_imprecise_dtypes=True).then_inc(c, 1)
            gps.iota(iota_p[:, :], pattern=[[0, 1]], base=0, channel_multiplier=1, allow_small_or_imprecise_dtypes=True).then_inc(c, 1)
            gps.iota(iota_v, pattern=[[1, NV]], base=0, channel_multiplier=0, allow_small_or_imprecise_dtypes=True).then_inc(c, 1)
            gps.memset(ident[:, :], 0.0).then_inc(c, 1)
            pool.wait_ge(c, 4)
            gps.affine_select(out=ident[:, :], in_=ident[:, :], compare_op=ALU.not_equal, fill=1.0, base=0,
                              pattern=[[-1, P]], channel_multiplier=1).then_inc(c, 1)
            pool.wait_ge(S["blocks"], 1)
            pool.wait_ge(S["edges_copied"], 96)
            for a, rows in enumerate((src_rows, dst_rows)):
                for m in range(2):
                    gps.indirect_dma_start(out=e_i[:, a, m, :].bitcast(I32), out_offset=None, in_=rows,
                                           in_offset=bass.IndirectOffsetOnAxis(ap=small[0:HV, 12 + m:13 + m].bitcast(U32), axis=0)).then_inc(S["rows_in"], 16)

            def dense(kind):
                s, n_norm = PS[kind], count(kind, "norm")
                with pool.Fori(0, NBATCH) as it:
                    for k in range(n_norm):
                        hold(pool, s["stat"], it * (n_norm * BT) + (k + 1) * BT, S["pool_passed"])
                        gps.tensor_scalar(rs[:, :], mv[:, :, 1], EPS, 1.0, ALU.add, ALU.mult).then_inc(s["rs_step"], 1)
                        hold(pool, s["rs_step"], it * n_norm + k + 1, S["pool_passed"])
                        gps.tensor_tensor(rs[:, :], rs[:, :], half[0:TN, :], ALU.pow).then_inc(s["rs_ready"], 1)

            def gathers(layer):
                def group(i, par, first):
                    k = i * 2 + par
                    if not first:
                        hold(pool, S["agg"], k * VG + (layer * NV - VG), S["pool_passed"])
                    gps.tensor_copy(stage_ix[:, par, :], src_ix[:, bass.ds(k * GC, GC)]).then_inc(S["ix_staged"], 1)
                    hold(pool, S["ix_staged"], k + (layer * NG + 1), S["pool_passed"])
                    for cc in range(GC):
                        gps.indirect_dma_start(out=chunk[:, par, cc, :], out_offset=None, in_=table,
                                               in_offset=bass.IndirectOffsetOnAxis(ap=stage_ix[:, par, cc:cc + 1], axis=0)).then_inc(gath[par][cc // CH], 16)
                group(0, 0, layer == 0)
                group(0, 1, layer == 0)
                with pool.Fori(1, NG // 2) as i:
                    group(i, 0, False)
                    group(i, 1, False)

            dense("in")
            pool.wait_ge(S["kv_out"], NT * 16)
            pool.wait_ge(S["pass_over"], 1)
            table = kv_table
            gathers(0)
            dense("mid")
            pool.wait_ge(S["kv_out"], 2 * NT * 16)
            pool.wait_ge(S["pass_over"], 2)
            table = kv_table2
            gathers(1)
            dense("last")
            dense("moe")

        @block.tensor
        def _(pe):
            pe.wait_ge(S["prep"], PREP_IND)
            for j in range(2):
                ten.matmul(bank[0][:, 0:NV], ones[0:LB, :], ind[:, j, :], start=(j == 0), stop=(j == 1))
            for m in range(2):
                for j in range(2):
                    mm = ten.matmul(bank[1][0:HV, m:m + 1], ind[:, j, m * HV:(m + 1) * HV], ones[0:LB, 0:1], start=(j == 0), stop=(j == 1))
            mm.then_inc(S["prep_pe"], 1)
            pe.wait_ge(S["pool_const"], 5)
            pe.wait_ge(S["penalties"], 1)
            for a, t in enumerate((e_src, e_dl, e_next)):
                for m in range(2):
                    for j in range(CH):
                        mm = ten.transpose(bank[2 + 2 * a + m][:, j * HV:(j + 1) * HV], t[:, m, j * P:(j + 1) * P], ident[0:HV, 0:HV])
            mm.then_inc(S["turned_rows"], 1)
            ten.transpose(bank[0][0:H, 256:256 + P], lane_h[:, :], ident[:, :]).then_inc(S["turned_rows"], 1)

            def fold(kind):
                pe.wait_ge(S["w_in_dma"], 16 * W_TOTAL[kind])
                mm = None
                if kind in ("in", "mid"):
                    for c0, c1, b in ((0, 512, bank[4]), (512, 768, bank[5])):
                        for a in range(2):
                            mm = ten.matmul(b[0:1, 0:c1 - c0], g_col[:, 1, a:a + 1], w_qkv[:, a, c0:c1], start=(a == 0), stop=(a == 1))
                if kind in ("mid", "last"):
                    for f in range(FFN // P):
                        for a in range(2):
                            mm = ten.matmul(bank[6][:, f:f + 1], w_up[:, a, f * P:(f + 1) * P], g_col[:, 3, a:a + 1], start=(a == 0), stop=(a == 1))
                mm.then_inc(S["w_pe"], 1)

            def dense(kind):
                s = PS[kind]
                n_turn, n_mm = count(kind, "turn") * BT, count(kind, "proj", "mlp", "qkv") * BT
                n_used = count(kind, "proj", "mlp") * BT
                n_mlp = FFN // P * 2
                with pe.Fori(0, NBATCH) as it:
                    turn = used = kvc = 0
                    for stage in PASSES[kind]:
                        if stage == "turn":
                            for j in range(BT):
                                pe.wait_ge(s["tok"], it * n_turn + turn + j + 1)
                                if j >= 2:
                                    pe.wait_ge(s["evac"], it * n_turn + turn + j - 1)
                                for a in range(2):
                                    mm = ten.transpose(bank[j % 2][:, a * TN:(a + 1) * TN], tok[:, j, a * P:(a + 1) * P], ident[0:TN, 0:TN])
                                mm.then_inc(s["turned"], 1)
                            turn += BT
                        elif stage == "proj":
                            for j in range(BT):
                                pe.wait_ge(s["evac"], it * n_turn + turn - BT + j + 1)
                                if j >= 3:
                                    pe.wait_ge(s["used"], it * n_used + used + j - 2)
                                o_ = bank[4 + j % 3][0:TN, 0:D]
                                ten.matmul(o_, ones[0:1, 0:TN], row_sq[:, :], start=True, stop=False)
                                for a in range(2):
                                    mm = ten.matmul(o_, tok_T[:, a, j * TN:(j + 1) * TN], w_sq[:, a, :], start=False, stop=(a == 1))
                                mm.then_inc(s["mm"], 1)
                            used += BT
                        elif stage == "mlp":
                            pe.wait_ge(s["evac"], it * n_turn + turn)
                            for n in range(n_mlp):
                                f, (c0, cn) = n // 2, MLP_CUT[n % 2]
                                if n >= 4:
                                    pe.wait_ge(s["gelu"], it * n_mlp + n - 3)
                                for a in range(2):
                                    mm = ten.matmul(bank[n % 4][:, 0:cn], w_up[:, a, f * P:(f + 1) * P], tok_T[:, a, c0:c0 + cn], start=(a == 0), stop=(a == 1))
                                mm.then_inc(s["up"], 1)
                            pe.wait_ge(s["gelu"], it * n_mlp + n_mlp)
                            for j in range(BT):
                                if j >= 3:
                                    pe.wait_ge(s["used"], it * n_used + used + j - 2)
                                o_ = bank[4 + j % 3][0:TN, 0:D]
                                ten.matmul(o_, ones[0:1, 0:TN], row_down[:, :], start=True, stop=False)
                                for f in range(FFN // P):
                                    mm = ten.matmul(o_, up_T[:, f, j * TN:(j + 1) * TN], w_down[:, f, :], start=False, stop=(f == FFN // P - 1))
                                mm.then_inc(s["mm"], 1)
                            used += BT
                        elif stage == "qkv":
                            for j in range(BT):
                                pe.wait_ge(s["evac"], it * n_turn + turn - BT + j + 1)
                                if j >= 2:
                                    pe.wait_ge(s["kvc"], it * BT + j - 1)
                                for c0, c1, b in ((0, 512, bank[4 + 2 * (j % 2)]), (512, 768, bank[5 + 2 * (j % 2)])):
                                    ten.matmul(b[0:TN, 0:c1 - c0], ones[0:1, 0:TN], row_qkv[:, c0:c1], start=True, stop=False)
                                    for a in range(2):
                                        mm = ten.matmul(b[0:TN, 0:c1 - c0], tok_T[:, a, j * TN:(j + 1) * TN], w_qkv[:, a, c0:c1], start=False, stop=(a == 1))
                                mm.then_inc(s["mm"], 1)

            def edges(layer):
                def scores(i, par, t, first):
                    gk = i * 2 + (par + layer * NG)
                    pe.wait_ge(S["onehot"], gk + 1)
                    for b in range(GC // 2):
                        if not (first and b < 2):
                            pe.wait_ge(S["q_used"], gk * (GC // 2) + b - 1)
                        if b == 0 and not first:
                            pe.wait_ge(S["ss_copied"], gk)
                        for c2 in range(2):
                            cc = 2 * b + c2
                            hot = dt[:, par, cc * P:(cc + 1) * P]
                            for p3 in range(3):
                                qo = t[cc // CH] * (3 * QC) + p3 * QC
                                mm = ten.matmul(b_q[b % 2][:, c2 * D:(c2 + 1) * D], hot, qs[:, bass.ds(qo, D)], start=(p3 == 0), stop=(p3 == 2))
                            for p3 in range(3):
                                qo = t[cc // CH] * (3 * QC) + p3 * QC + D
                                ms = ten.matmul(b_ss[:, cc * H:(cc + 1) * H], hot, qs[:, bass.ds(qo, H)], start=(p3 == 0), stop=(p3 == 2))
                        ms.then_inc(S["q_ready"], 1)

                def maxima(i, par):
                    gk = i * 2 + (par + layer * NG)
                    st = Steps(S["ch_pe"], gk * CH_PE)
                    def dve(n):
                        pe.wait_ge(S["ch_dve"], gk * CH_DVE + n)
                    dve(C_SP)
                    st.did(ten.transpose(b_ch[:, 0:P], sp_e[:, :, :].rearrange("p h c -> p (h c)"), ident[:, :]))
                    dve(C_ENDS)
                    st.did(ten.matmul(b_ch[0:H, 128:160], lane_h[:, :], ends[:, :, :].rearrange("p a c -> p (a c)"), start=True, stop=True))
                    dve(C_XY)
                    st.did(ten.matmul(b_ch[:, 160:192], lane_hT[:, :], flows, start=True, stop=True))
                    dve(C_ALPHA)
                    st.did(ten.matmul(b_mu[0:TN, P:P + H], delta[:, :], r_diag[:, :], start=True, stop=True))
                    dve(C_MU)
                    st.did(ten.transpose(b_mu[:, 0:P], f_lane[:, :], ident[:, :]))
                    assert st.n == CH_PE

                def sums(i, par, first):
                    gk = i * 2 + (par + layer * NG)
                    pe.wait_ge(S["ch_dve"], gk * CH_DVE + C_SELF)
                    for v in range(VG):
                        pe.wait_ge(S["d_ready"], gk * VG + v + 1)
                        pe.wait_ge(S["w_ready"], gk * (GC // 2) + 2 * v + 2)
                        if not (first and v < 2):
                            pe.wait_ge(S["agg_used"], gk * VG + v - 1)
                        for c4 in range(CH):
                            mm = ten.matmul(b_acc[v % 2][0:TN, 0:WCOL], dhot[:, (v % 2) * CH + c4, :],
                                            chunk[:, par, v * CH + c4, WOFF:ROW], start=(c4 == 0), stop=(c4 == CH - 1))
                        mm.then_inc(S["agg"], 1)

                def group(i, par, first=False):
                    t = [pe.value_load(t_row[0:1, bass.ds((i * 2 + par) * VG + v, 1)], min_val=0, max_val=NT - 1) for v in range(VG)]
                    scores(i, par, t, first)
                    maxima(i, par)
                    sums(i, par, first)
                group(0, 0, layer == 0)
                group(0, 1)
                with pe.Fori(1, NG // 2) as i:
                    group(i, 0)
                    group(i, 1)

            pe.wait_ge(S["prep_done"], 1)
            fold("in")
            pe.wait_ge(S["w_dve"], 1)
            dense("in")
            pe.wait_ge(S["pass_over"], 1)
            fold("mid")
            pe.wait_ge(S["w_dve"], 2)
            edges(0)
            dense("mid")
            pe.wait_ge(S["pass_over"], 2)
            fold("last")
            pe.wait_ge(S["w_dve"], 3)
            edges(1)
            dense("last")
            pe.wait_ge(S["pass_over"], 3)
            for a in range(2):
                for t in range(NT):
                    mm = ten.matmul(bank[0][:, a:a + 1], acc_t[:, t, a * P:(a + 1) * P], ones[0:TN, 0:1], start=(t == 0), stop=(t == NT - 1))
            mm.then_inc(S["route_pe"], 1)
            pe.wait_ge(S["route_dma"], 64)
            pe.wait_ge(S["route"], R_MEAN)
            for a in range(2):
                mm = ten.matmul(bank[1][0:1, 0:NEXP], small[:, a:a + 1], w_qkv[:, 0, a * NEXP:(a + 1) * NEXP], start=(a == 0), stop=(a == 1))
            mm.then_inc(S["route_pe"], 1)
            ten.matmul(bank[7][0:TN, :], ones[0:1, 0:TN], row_qkv[:, D:3 * D], start=True, stop=True).then_inc(S["route_pe"], 1)
            pe.wait_ge(S["route"], R_TOPW)
            ten.matmul(bank[2][:, 0:TOPK], ones[0:1, :], small[0:1, 62:64], start=True, stop=True).then_inc(S["route_pe"], 1)
            pe.wait_ge(S["route"], R_WEIGHTS)
            dense("moe")

        @block.scalar
        def _(act):
            def dense(kind):
                s = PS[kind]
                n_turn, n_mm = count(kind, "turn") * BT, count(kind, "proj", "mlp", "qkv") * BT
                n_mlp = FFN // P * 2
                with act.Fori(0, NBATCH) as it:
                    turn = mm = 0
                    for stage in PASSES[kind]:
                        if stage == "turn":
                            for j in range(BT):
                                act.wait_ge(s["turned"], it * n_turn + turn + j + 1)
                                sca.activation(tok_T[:, :, j * TN:(j + 1) * TN], bank[j % 2][:, 0:2 * TN].rearrange("p (a n) -> p a n", a=2), ACT.Copy).then_inc(s["evac"], 1)
                            turn += BT
                        elif stage == "mlp":
                            for n in range(n_mlp):
                                f, (c0, cn) = n // 2, MLP_CUT[n % 2]
                                act.wait_ge(s["up"], it * n_mlp + n + 1)
                                sca.activation(up_T[:, f, c0:c0 + cn], bank[n % 4][:, 0:cn], ACT.Gelu, bias=up_bias[:, f:f + 1]).then_inc(s["gelu"], 1)
                        elif stage == "qkv":
                            for j in range(BT):
                                act.wait_ge(s["mm"], it * n_mm + mm + j + 1)
                                b0, b1 = bank[4 + 2 * (j % 2)], bank[5 + 2 * (j % 2)]
                                sca.activation(qf[:, j, 0:D], b0[0:TN, 0:D], ACT.Copy)
                                sca.activation(kv_b[:, j, 0:D], b0[0:TN, D:2 * D], ACT.Copy)
                                sca.activation(kv_b[:, j, D:ROW].rearrange("p (d h) -> p h d", h=H),
                                               b1[0:TN, 0:D].rearrange("p (h d) -> p h d", h=H), ACT.Copy).then_inc(s["kvc"], 1)
                            for r, src in ((0, qf), (1, qr)):
                                act.wait_ge(s["qf"], it * 2 + r + 1)
                                dst = qs[:, bass.ds(it * (BT * 3 * QC) , BT * 3 * QC)].rearrange("p (j r c) -> p j r c", j=BT, r=3)[:, :, r, :]
                                sca.activation(dst, src, ACT.Copy).then_inc(s["cast"], 1)
                        if stage in ("proj", "mlp"):
                            mm += BT

            def edges(layer):
                def group(i, par, first=False):
                    gk = i * 2 + (par + layer * NG)
                    st = Steps(S["ch_act"], gk * CH_ACT)
                    act.wait_ge(S["q_ready"], gk * (GC // 2) + GC // 2)
                    if not first:
                        act.wait_ge(S["ch_dve"], gk * CH_DVE)
                    sca.activation(ss_e[:, :, :].rearrange("p h c -> p c h"), b_ss[:, 0:P].rearrange("p (c h) -> p c h", h=H), ACT.Copy).then_inc(S["ss_copied"], 1)
                    act.wait_ge(S["ch_dve"], gk * CH_DVE + C_DM)
                    st.did(sca.activation(m_new[:, 2:3], m_new[:, 1:2], ACT.Exp))
                    act.wait_ge(S["ch_dve"], gk * CH_DVE + C_ARG)
                    a0 = arg[:, 0, :].rearrange("p (h c) -> p c h", h=H)
                    st.did(sca.activation(chunk[:, par, :, WOFF:WOFF + H], a0, ACT.Exp))
                    if not first:
                        act.wait_ge(S["w_ready"], gk * (GC // 2))
                    st.did(sca.activation(b_p[:, 0:P].rearrange("p (c h) -> p c h", h=H), a0, ACT.Exp))
                    st.did(sca.activation(sp_e[:, :, :].rearrange("p h c -> p (h c)"), arg[:, 1, :], ACT.Exp))
                    assert st.n == CH_ACT
                group(0, 0, layer == 0)
                group(0, 1)
                with act.Fori(1, NG // 2) as i:
                    group(i, 0)
                    group(i, 1)

            dense("in")
            edges(0)
            dense("mid")
            edges(1)
            dense("last")
            for n, (at, i_, w, b_) in enumerate(((R_E1, 8, NEXP, 58), (R_E2, 16, NEXP, 58), (R_E3, 60, TOPK, 58))):
                act.wait_ge(S["route"], at)
                sca.activation(small[0:1, i_:i_ + w], small[0:1, i_:i_ + w], ACT.Exp, bias=small[0:1, b_:b_ + 1]).then_inc(S["route_act"], 1)
            dense("moe")

        @block.vector
        def _(v):
            tt, ts = vec.tensor_tensor, vec.tensor_scalar
            vec.memset(fill_m1.bitcast(I32), -1).then_inc(S["pads"], 1)
            vec.memset(fill_0.bitcast(I32), 0).then_inc(S["pads"], 1)
            vec.memset(small[0:1, 10:11], -2.0).then_inc(S["pads"], 1)
            st = Steps(S["prep"])

            def do(ins):
                st.did(ins)
                st.sync(v)

            vec.memset(half[:, :], -0.5)
            st.did(vec.memset(ones[:, :], 1.0))
            vec.memset(g_run[:, :], -BIG)
            do(vec.memset(h_run[:, :], -BIG))
            v.wait_ge(S["pool_const"], 5)
            by_lane = ident[:, :].rearrange("p (h c) -> p h c", h=H)
            do(vec.tensor_reduce(lane_h[:, :], by_lane, AX.X, ALU.add))
            for a in range(2):
                do(vec.tensor_reduce(lane_c[:, a, :], by_lane.rearrange("p h c -> p c h"), AX.X, ALU.add))
            v.wait_ge(S["last_in"], 48)
            do(vec.tensor_copy(small[0:LB, 2:4], small[0:LB, 0:2].bitcast(I32)))
            do(ts(small[:, 20:20 + NT - 1], iota_f[:, 1:NT], float(TN), None, ALU.mult))
            for j in range(2):
                do(ts(e_src[0:LB, 0, 0:NT - 1], small[0:LB, 20:20 + NT - 1], small[0:LB, 2 + j:3 + j], None, ALU.is_le))
                do(vec.tensor_reduce(small[0:LB, 4 + j:5 + j], e_src[0:LB, 0, 0:NT - 1], AX.X, ALU.add))
                do(ts(small[0:LB, 6 + j:7 + j], small[0:LB, 4 + j:5 + j], iota_p[0:LB, :], float(j * LB), ALU.add, ALU.add))
                do(ts(ind[:, j, :], iota_v[0:LB, :], small[0:LB, 6 + j:7 + j], None, ALU.is_gt))
            assert st.n == PREP_IND, st.n
            v.wait_ge(S["prep_pe"], 1)
            do(vec.tensor_copy(small[0:HV, 16:18], bank[1][0:HV, 0:2]))
            vec.tensor_copy(small[0:HV, 12:14].bitcast(U32), small[0:HV, 16:18]).then_inc(S["blocks"], 1)
            for m in range(2):
                do(ts(small[0:HV, 18 + m:19 + m], small[0:HV, 16 + m:17 + m], iota_p[0:HV, :], -1.0, ALU.subtract, ALU.mult))
                do(ts(small[0:HV, 18 + m:19 + m], small[0:HV, 18 + m:19 + m], float(m * HV), float(NT - 1), ALU.add, ALU.min))
                do(ts(small[0:HV, 18 + m:19 + m], small[0:HV, 18 + m:19 + m], float(TN), None, ALU.mult))
            do(tt(iota_v[0:1, :], iota_v[0:1, :], bank[0][0:1, 0:NV], ALU.subtract))
            do(ts(iota_v[0:1, :], iota_v[0:1, :], float(NT - 1), None, ALU.min))
            do(vec.tensor_copy(t_row[:, :], iota_v[0:1, :]))
            v.wait_ge(S["rows_in"], 64)
            st.did(vec.tensor_copy(e_src, e_i[:, 0, :, :].bitcast(I32)))
            do(vec.tensor_copy(e_dst, e_i[:, 1, :, :].bitcast(I32)))
            for m in range(2):
                do(ts(e_dl[:, m, :], e_dst[:, m, :], small[0:HV, 18 + m:19 + m], None, ALU.subtract))
            do(ts(e_val, e_dl, 0.0, None, ALU.is_ge))
            do(ts(e_key, e_dl, float(TN), None, ALU.is_lt))
            do(tt(e_val, e_val, e_key, ALU.mult))
            for t, s_ in ((e_key, e_dst), (e_dl, e_dl)):
                do(vec.scalar_tensor_tensor(out=t, in0=s_, scalar=1.0, in1=e_val, op0=ALU.add, op1=ALU.mult))
                do(ts(t, t, -1.0, None, ALU.add))
            vec.tensor_copy(b_dl, e_dl).then_inc(S["keys"], 1)
            v.wait_ge(S["lines_in"], 16 * (2 + 3 * H))
            st.did(tt(e_prev, e_key, e_prev, ALU.is_equal))
            do(tt(e_next, e_key, e_next, ALU.is_equal))
            st.did(ts(b_pf, e_prev, BIG, -BIG, ALU.mult, ALU.add))
            do(ts(b_pb, e_next, BIG, -BIG, ALU.mult, ALU.add))
            do(ts(e_next, e_next, -1.0, 1.0, ALU.mult, ALU.add))
            tt(e_next, e_next, e_val, ALU.mult).then_inc(S["penalties"], 1)
            v.wait_ge(S["turned_rows"], 2)
            for a, (t, dst) in enumerate(((e_src, src_ix), (e_dl, dl_col), (e_next, last_col))):
                for m in range(2):
                    st.did(vec.tensor_copy(dst[:, :].rearrange("p (v j) -> p j v", j=CH)[:, :, m * HV:(m + 1) * HV],
                                           bank[2 + 2 * a + m][:, 0:CH * HV].rearrange("p (j v) -> p j v", j=CH)))
            st.did(vec.tensor_copy(lane_hT[:, :], bank[0][0:H, 256:256 + P]))
            v.wait_ge(S["lines_in"], 16 * (2 + 4 * H))
            do(tt(k_first, k_first, k_last, ALU.is_equal))
            do(ts(k_first, k_first, BIG, -BIG, ALU.mult, ALU.add))
            at_group = kp[:, 0:NC].rearrange("p (g c) -> p g c", c=GC)[:, :, 0]
            do(ts(dl0[:, :], at_group, 0.0, None, ALU.is_equal))
            do(ts(k_last[:, 0:NG], a_f[:, 0:NG], 1.0, None, ALU.add))
            do(tt(dl0[:, :], dl0[:, :], k_last[:, 0:NG], ALU.mult))
            do(ts(dl0[:, :], dl0[:, :], -1.0, None, ALU.add))
            do(tt(a_f[:, :], k_first, kp[:, 0:NC], ALU.min))
            do(tt(a_b[:, :].rearrange("p (g c) -> p g c", c=GC)[:, :, ::-1], k_first.rearrange("p (g c) -> p g c", c=GC),
                  kp[:, 1:NC + 1].rearrange("p (g c) -> p g c", c=GC), ALU.min))
            v.sem_inc(S["prep_done"], 1)

            def fold(kind):
                w = S["w_step"]
                n0 = {"in": 0, "mid": W_STEPS["in"], "last": W_STEPS["in"] + W_STEPS["mid"]}[kind]
                ws = Steps(w, n0)
                v.wait_ge(S["w_pe"], PASS_NO[kind] + 1)
                sc = DH ** -0.5
                if kind in ("in", "mid"):
                    ws.did(tt(row_qkv[:, 0:512], row_qkv[:, 0:512], bank[4][0:1, 0:512], ALU.add))
                    ws.did(tt(row_qkv[:, 512:768], row_qkv[:, 512:768], bank[5][0:1, 0:256], ALU.add))
                    for a in range(2):
                        ws.did(ts(w_qkv[:, a, 0:D], w_qkv[:, a, 0:D], g_col[:, 0, a:a + 1], sc, ALU.mult, ALU.mult))
                        ws.did(ts(w_qkv[:, a, D:3 * D], w_qkv[:, a, D:3 * D], g_col[:, 0, a:a + 1], None, ALU.mult))
                    ws.sync(v)
                    ws.did(ts(row_qkv[:, 0:D], row_qkv[:, 0:D], sc, None, ALU.mult))
                if kind in ("mid", "last"):
                    ws.did(tt(up_bias[:, :], up_bias[:, :], bank[6][:, 0:FFN // P], ALU.add))
                    for a in range(2):
                        ws.did(ts(w_up[:, a, :], w_up[:, a, :], g_col[:, 2, a:a + 1], None, ALU.mult))
                ws.sync(v)
                assert ws.n == W_STEPS[kind], ws.n
                v.sem_inc(S["w_dve"], 1)

            def dense(kind):
                s = PS[kind]
                n_tok, n_mm = count(kind, "turn") * BT, count(kind, "proj", "mlp", "qkv") * BT
                n_used = count(kind, "proj", "mlp") * BT
                n_norm = count(kind, "norm")
                n_x = {"in": 16, "mid": 32, "last": 48, "moe": 16}[kind]
                with v.Fori(0, NBATCH) as it:
                    st = Steps(s["dve"], it * D_STEPS[kind])
                    mm = used = norm = tokn = 0
                    v.wait_ge(s["x_in"], it * n_x + n_x)
                    tiles = acc[:, bass.ds(it * (BT * WCOL), BT * WCOL)].rearrange("p (j w) -> p j w", j=BT)
                    for k, stage in enumerate(PASSES[kind]):
                        if stage == "agg":
                            z, own = tiles[:, :, 0:H], tiles[:, :, H:2 * H]
                            val = tiles[:, :, 2 * H:WCOL].rearrange("p j (d h) -> p j d h", h=H)
                            den = small[0:TN, 0:BT * H].rearrange("p (j h) -> p j h", h=H)
                            st.did(tt(den, z, own, ALU.add)); st.sync(v)
                            st.did(ts(den, den, 1e-30, None, ALU.max)); st.sync(v)
                            st.did(vec.reciprocal(den, den)); st.sync(v)
                            mine = kv_b[:, :, D:ROW].rearrange("p j (d h) -> p j d h", h=H)
                            def over_d(x):
                                return x.rearrange("p j (a h) -> p j a h", a=1).to_broadcast([TN, BT, DH, H])
                            st.did(tt(mine, mine, over_d(own), ALU.mult)); st.sync(v)
                            st.did(tt(mine, mine, val, ALU.add)); st.sync(v)
                            for j in range(BT):
                                tt(tok[:, j, :].rearrange("p (h d) -> p d h", h=H), kv_b[:, j, D:ROW].rearrange("p (d h) -> p d h", h=H),
                                   den[:, j:j + 1, :].to_broadcast([TN, DH, H]), ALU.mult).then_inc(s["tok"], 1)
                            tokn += BT
                        elif stage == "take":
                            for j in range(BT):
                                vec.tensor_copy(tok[:, j, :], tiles[:, j, 0:D]).then_inc(s["tok"], 1)
                            tokn += BT
                        elif stage in ("proj", "mlp"):
                            for j in range(BT):
                                v.wait_ge(s["mm"], it * n_mm + mm + j + 1)
                                r = bank[4 + j % 3][0:TN, 0:D]
                                if kind == "in":
                                    vec.tensor_copy(h_b[:, j, :], r).then_inc(s["used"], 1)
                                elif kind == "moe":
                                    tt(tok[:, j, :], tok[:, j, :], r, ALU.add).then_inc(s["used"], 1)
                                else:
                                    tt(h_b[:, j, :], h_b[:, j, :], r, ALU.add).then_inc(s["used"], 1)
                            mm += BT
                            used += BT
                            v.wait_ge(s["used"], it * n_used + used)
                            if kind == "last" and stage == "mlp":
                                st.did(tt(h_b[:, :, :], h_b[:, :, :], x_in[:, :, :], ALU.add)); st.sync(v)
                        elif stage == "norm":
                            src = x_in[:, :, :] if kind == "in" and norm == 0 else tok if kind == "moe" else h_b[:, :, :]
                            for j in range(BT):
                                st.did(vec.bn_stats(stat[:, j, :], src[:, j, :]))
                            hold(v, s["dve"], st.base + st.n, S["dve_passed"])
                            for j in range(BT):
                                vec.bn_aggr(mv[:, j, :], stat[:, j, :]).then_inc(s["stat"], 1)
                            norm += 1
                            v.wait_ge(s["stat"], it * (n_norm * BT) + norm * BT)
                            v.wait_ge(s["rs_ready"], it * n_norm + norm)
                            feeds = k + 1 < len(PASSES[kind])
                            for j in range(BT):
                                dst = tok[:, j, :] if kind != "last" or feeds else tiles[:, j, 0:D]
                                ins = ts(dst, src[:, j, :], mv[:, j, 0:1], rs[:, j:j + 1], ALU.subtract, ALU.mult)
                                if feeds:
                                    ins.then_inc(s["tok"], 1)
                                else:
                                    st.did(ins)
                            if feeds:
                                tokn += BT
                            else:
                                st.sync(v)
                            if kind == "moe":
                                for j in range(BT):
                                    st.did(tt(tok[:, j, :], tok[:, j, :], bank[7][0:TN, 0:D], ALU.mult)); st.sync(v)
                                    st.did(tt(tok[:, j, :], tok[:, j, :], bank[7][0:TN, D:2 * D], ALU.add)); st.sync(v)
                                    st.did(tt(h_b[:, j, :], h_b[:, j, :], tok[:, j, :], ALU.add))
                                st.sync(v)
                        elif stage == "qkv":
                            for j in range(BT):
                                v.wait_ge(s["kvc"], it * BT + j + 1)
                                st.did(tt(qr[:, j, 0:D], qf[:, j, 0:D], kv_b[:, j, 0:D], ALU.mult)); st.sync(v)
                                ins = vec.tensor_reduce(qf[:, j, D:QC], qr[:, j, 0:D].rearrange("p (h d) -> p h d", h=H), AX.X, ALU.add)
                                st.did(ins)
                            st.sync(v)
                            v.sem_inc(s["qf"], 1)
                            q3 = qs[:, bass.ds(it * (BT * 3 * QC), BT * 3 * QC)].rearrange("p (j r c) -> p j r c", j=BT, r=3)
                            v.wait_ge(s["cast"], it * 2 + 1)
                            tt(qr, qf, q3[:, :, 0, :], ALU.subtract).then_inc(s["qf"], 1)
                            v.wait_ge(s["cast"], it * 2 + 2)
                            st.did(tt(q3[:, :, 2, :], qr, q3[:, :, 1, :], ALU.subtract))
                            st.sync(v)
                    assert st.n == D_STEPS[kind], (kind, st.n)
                    v.sem_inc(s["done"], 1)
                v.sem_inc(S["pass_over"], 1)

            def edges(layer):
                es = Steps(S["edge_step"], layer * 2)
                es.did(vec.memset(acc[:, :], 0.0))
                es.did(vec.memset(g_run[:, GC:GC + 1], -BIG))
                es.sync(v)

                def scores(i, par):
                    gk = i * 2 + (par + layer * NG)
                    v.wait_ge(S[f"tab{par}"], i * (17 * 16) + (layer * (NG // 2) + 1) * 17 * 16)
                    ts(dt[:, par, :], dt[:, par, :], iota_p[0:TN, :], None, ALU.is_equal).then_inc(S["onehot"], 1)
                    ready = i * (CH * 16) + (layer * (NG // 2) + 1) * CH * 16
                    for b in range(GC // 2):
                        if b % 2 == 0:
                            v.wait_ge(gath[par][b // 2], ready)
                        v.wait_ge(S["q_ready"], gk * (GC // 2) + b + 1)
                        pair = chunk[:, par, 2 * b:2 * b + 2, 0:D]
                        tt(pair, pair, b_q[b % 2][:, :].rearrange("p (c w) -> p c w", c=2), ALU.mult).then_inc(S["q_used"], 1)
                        v.wait_ge(S["q_used"], gk * (GC // 2) + b + 1)
                        vec.tensor_reduce(s_e[:, :, 2 * b:2 * b + 2].rearrange("p h c -> p c h"),
                                          pair.rearrange("p c (h d) -> p c h d", h=H), AX.X, ALU.add).then_inc(S["score"], 1)

                def maxima(i, par, t0):
                    k = i * 2 + par
                    gk = k + layer * NG
                    st = Steps(S["ch_dve"], gk * CH_DVE)

                    def do(ins):
                        st.did(ins)
                        st.sync(v)

                    def pe(n):
                        v.wait_ge(S["ch_pe"], gk * CH_PE + n)
                    v.wait_ge(S["score"], gk * (GC // 2) + GC // 2)
                    v.wait_ge(S["ss_copied"], gk + 1)
                    do(tt(sp_e[:, :, :], s_e[:, :, :], ss_e[:, :, :], ALU.max))
                    assert st.n == C_SP
                    pf, pb = pens[:, par, 0, :], pens[:, par, 1, :]
                    pe(1)
                    sT = b_ch[:, 0:P]
                    st.did(vec.tensor_tensor_scan(f_lane[:, 1:P], pf[:, 1:P], sT[:, 1:P], sT[:, 0:1], ALU.add, ALU.max))
                    do(vec.tensor_tensor_scan(b_lane[:, ::-1][:, 1:P], pb[:, ::-1][:, 1:P], sT[:, ::-1][:, 1:P], sT[:, P - 1:P], ALU.add, ALU.max))
                    st.did(ts(ends[:, 0, :], lane_c[:, 0, :], f_lane[:, P - 1:P], None, ALU.mult))
                    do(ts(ends[:, 1, :], lane_c[:, 0, :], b_lane[:, 0:1], None, ALU.mult))
                    assert st.n == C_ENDS
                    do(vec.tensor_copy(g_run[:, 0:1], g_run[:, GC:GC + 1]))
                    pe(2)
                    c0 = k * GC
                    st.did(vec.tensor_tensor_scan(g_run[:, 1:GC + 1], a_f[:, bass.ds(c0, GC)], b_ch[0:H, 128:128 + GC], g_run[:, 0:1], ALU.add, ALU.max))
                    do(vec.tensor_tensor_scan(h_run[:, 0:GC][:, ::-1], a_b[:, bass.ds(c0, GC)], b_ch[0:H, 128 + GC:128 + 2 * GC][:, ::-1], -BIG, ALU.add, ALU.max))
                    assert st.n == C_XY
                    do(tt(m_new[:, 0:1], h_run[:, 0:1], g_run[:, 0:1], ALU.max))
                    do(tt(m_new[:, 1:2], g_run[:, 0:1], m_new[:, 0:1], ALU.subtract))
                    assert st.n == C_DM
                    do(ts(delta[:, :], iota_f[0:H, 0:TN], dl0[:, bass.ds(k, 1)], None, ALU.is_equal))
                    v.wait_ge(S["ch_act"], gk * CH_ACT + 1)
                    do(ts(m_new[:, 3:4], m_new[:, 2:3], -1.0, None, ALU.add))
                    do(ts(r_diag[:, :], ident[0:H, 0:H], m_new[:, 3:4], None, ALU.mult))
                    assert st.n == C_ALPHA
                    pe(3)
                    do(tt(xy_m[:, :, :], lane_c[:, :, :], b_ch[:, 160:192].rearrange("p (a c) -> p a c", a=2), ALU.mult))
                    do(vec.tensor_reduce(xy_l[:, :], xy_m[:, :, :], AX.X, ALU.add))
                    st.did(vec.tensor_tensor_scan(f_lane[:, :], pf, sT, xy_l[:, 0:1], ALU.add, ALU.max))
                    do(vec.tensor_tensor_scan(b_lane[:, ::-1], pb[:, ::-1], sT[:, ::-1], xy_l[:, 1:2], ALU.add, ALU.max))
                    do(tt(f_lane[:, :], f_lane[:, :], b_lane[:, :], ALU.max))
                    assert st.n == C_MU
                    pe(5)
                    do(ts(a_fac[:, :], b_mu[0:TN, P:P + H], 1.0, None, ALU.add))
                    at = acc[:, bass.ds(t0 * WCOL, WCOL)].rearrange("p (x h) -> p x h", h=H)
                    do(tt(at, at, a_fac[:, :].rearrange("p (a h) -> p a h", a=1).to_broadcast([TN, WCOL // H, H]), ALU.mult))
                    mu = b_mu[:, 0:P]
                    st.did(tt(arg[:, 0, :], s_e[:, :, :].rearrange("p h c -> p (h c)"), mu, ALU.subtract))
                    st.did(tt(arg[:, 1, :], ss_e[:, :, :].rearrange("p h c -> p (h c)"), mu, ALU.subtract))
                    assert st.n == C_ARG
                    v.wait_ge(S["ch_act"], gk * CH_ACT + CH_ACT)
                    st.did(tt(chunk[:, par, :, WOFF + H:WOFF + 2 * H], sp_e[:, :, :].rearrange("p h c -> p c h"),
                              last_col[:, bass.ds(k * GC, GC)].rearrange("p (c a) -> p c a", a=1).to_broadcast([P, GC, H]), ALU.mult))
                    assert st.n == C_SELF == CH_DVE

                def sums(i, par, t, first):
                    k = i * 2 + par
                    gk = k + layer * NG

                    def add(q):
                        v.wait_ge(S["agg"], gk * VG + q + 1)
                        at = acc[:, bass.ds(t[q] * WCOL, WCOL)]
                        tt(at, at, b_acc[q % 2][0:TN, 0:WCOL], ALU.add).then_inc(S["agg_used"], 1)

                    for q in range(VG):
                        if not (first and q < 2):
                            v.wait_ge(S["agg"], gk * VG + q - 1)
                        for c4 in range(CH):
                            ins = ts(dhot[:, (q % 2) * CH + c4, :], iota_f[:, 0:TN], dl_col[:, bass.ds(k * GC + q * CH + c4, 1)], None, ALU.is_equal)
                        ins.then_inc(S["d_ready"], 1)
                        for b in (2 * q, 2 * q + 1):
                            val = chunk[:, par, 2 * b:2 * b + 2, D:ROW].rearrange("p c (d h) -> p c d h", h=H)
                            w = b_p[:, 2 * b * H:(2 * b + 2) * H].rearrange("p (c a h) -> p c a h", c=2, a=1).to_broadcast([P, 2, DH, H])
                            tt(val, val, w, ALU.mult).then_inc(S["w_ready"], 1)
                        if q:
                            if q > 1:
                                v.wait_ge(S["agg_used"], gk * VG + q - 1)
                            add(q - 1)
                    v.wait_ge(S["agg_used"], gk * VG + VG - 1)
                    add(VG - 1)
                    v.wait_ge(S["agg_used"], gk * VG + VG)

                def group(i, par, first=False):
                    t = [v.value_load(t_row[0:1, bass.ds((i * 2 + par) * VG + q, 1)], min_val=0, max_val=NT - 1) for q in range(VG)]
                    scores(i, par)
                    maxima(i, par, t[0])
                    sums(i, par, t, first)
                group(0, 0, layer == 0)
                group(0, 1)
                with v.Fori(1, NG // 2) as i:
                    group(i, 0)
                    group(i, 1)
                v.sem_inc(S["edges_over"], 1)

            fold("in")
            dense("in")
            fold("mid")
            edges(0)
            dense("mid")
            fold("last")
            edges(1)
            dense("last")

            st = Steps(S["route"])

            def col(c, n=NEXP):
                return small[0:1, c:c + n]

            def softmax_top(x, e_no, n=NEXP):
                do(vec.tensor_reduce(col(58, 1), col(x, n), AX.X, ALU.max))
                do(ts(col(58, 1), col(58, 1), -1.0, None, ALU.mult))
                assert st.n == (R_E1, R_E2, R_E3)[e_no], (e_no, st.n)
                v.wait_ge(S["route_act"], e_no + 1)
                do(vec.tensor_reduce(col(59, 1), col(x, n), AX.X, ALU.add))
                do(vec.reciprocal(col(59, 1), col(59, 1)))

            v.wait_ge(S["route_pe"], 1)
            do(ts(small[:, 0:2], bank[0][:, 0:2], 1.0 / N, None, ALU.mult))
            assert st.n == R_MEAN
            v.wait_ge(S["route_pe"], 2)
            do(tt(col(8), bank[1][0:1, 0:NEXP], row_qkv[:, 0:NEXP], ALU.add))
            softmax_top(8, 0)
            do(ts(col(8), col(8), col(59, 1), None, ALU.mult))
            do(ts(col(16), col(8), float(N), None, ALU.mult))
            do(ts(col(24), col(16), CAPACITY, None, ALU.is_gt))
            do(ts(col(16), col(16), CAPACITY, None, ALU.max))
            do(vec.reciprocal(col(16), col(16)))
            do(ts(col(16), col(16), CAPACITY, -1.0, ALU.mult, ALU.add))
            do(tt(col(16), col(16), col(24), ALU.mult))
            do(ts(col(16), col(16), 1.0, None, ALU.add))
            do(tt(col(16), col(16), col(8), ALU.mult))
            softmax_top(16, 1)
            do(ts(col(16), col(16), col(59, 1), None, ALU.mult))
            for i in range(TOPK):
                do(vec.tensor_reduce(col(60 + i, 1), col(16), AX.X, ALU.max))
                do(ts(col(24), col(16), col(60 + i, 1), None, ALU.is_equal))
                do(ts(col(32), col(24), -99.0, 99.0, ALU.mult, ALU.add))
                do(tt(col(24), col(24), iota_f[0:1, 0:NEXP], ALU.mult))
                do(tt(col(32), col(32), col(24), ALU.add))
                do(vec.tensor_reduce(col(40 + i, 1), col(32), AX.X, ALU.min))
                do(ts(col(24), iota_f[0:1, 0:NEXP], col(40 + i, 1), -10.0, ALU.is_equal, ALU.mult))
                do(tt(col(16), col(16), col(24), ALU.add))
            vec.tensor_copy(exp_ix[:, :], col(40, TOPK)).then_inc(S["chosen"], 1)
            softmax_top(60, 2, TOPK)
            do(ts(col(62, TOPK), col(60, TOPK), col(59, 1), None, ALU.mult))
            assert st.n == R_TOPW, st.n
            v.wait_ge(S["route_pe"], 4)
            do(vec.tensor_copy(small[:, 4:6], bank[2][:, 0:TOPK]))
            v.wait_ge(S["route_dma"], 16 * (4 + 4 * TOPK))
            f = FE // P
            for i in range(TOPK):
                st.did(ts(w_down[:, i * f:(i + 1) * f, :], w_down[:, i * f:(i + 1) * f, :], small[:, 4 + i:5 + i], None, ALU.mult))
            do(ts(row_down[:, :], b2_rows[:, 0, :], col(4, 1), None, ALU.mult))
            do(vec.scalar_tensor_tensor(out=row_down[:, :], in0=b2_rows[:, 1, :], scalar=col(5, 1), in1=row_down[:, :], op0=ALU.mult, op1=ALU.add))
            assert st.n == R_WEIGHTS, st.n
            dense("moe")


_INS = ["x", "src", "dst"] + [f"L0_gnn_{n}" for n in (
    "w_in", "b_in", "ln1_g", "ln1_b", "ln2_g", "ln2_b", "wq", "bq", "wk", "bk", "wv", "bv", "wo", "bo", "w1", "b1", "w2", "b2")] + [
    f"L0_ffn_{n}" for n in ("Wr", "br", "W1", "b1", "W2", "b2", "gamma", "beta")]


def kernel(**inputs):
    import numpy as _np
    import concourse.bacc as _bacc
    from concourse import mybir as _mybir
    from concourse.bass_utils import run_bass_kernel_spmd as _run

    nc = _bacc.Bacc("TRN2", target_bir_lowering=False, num_devices=1)
    arrays, args = {}, {}
    for name in _INS:
        a = _np.ascontiguousarray(inputs[name])
        arrays[f"in_{name}_dram"] = a
        args[name] = nc.dram_tensor(f"in_{name}_dram", a.shape, _mybir.dt.from_np(a.dtype), kind="ExternalInput").ap()
    out = nc.dram_tensor("out_0_dram", (N, D), _mybir.dt.float32, kind="ExternalOutput").ap()
    program(nc, args, out)
    r = _run(nc, [arrays], core_ids=[0])
    return r.results[0]["out_0_dram"]
```

```python
from contextlib import ExitStack

import concourse.bass as bass
from concourse import mybir

ALU = mybir.AluOpType
ACT = mybir.ActivationFunctionType
AX = mybir.AxisListType
F32 = mybir.dt.float32
BF16 = mybir.dt.bfloat16
I32 = mybir.dt.int32
U32 = mybir.dt.uint32

N, D, E = 3125, 256, 100000
H, DH = 8, 32
LAYERS, FFN = 2, 1024
NEXP, FE, TOPK = 8, 512, 2
EPS = 1e-5
CAPACITY = float(-(-(N * 125) // (NEXP * 100)))

P = 128
TN = 125
NT = N // TN
BT = 5
NBATCH = NT // BT

BLK = 512
NBLK = -(-E // BLK)
CH = BLK // P
VG = 4
NG = -(-(NBLK + NT - 1) // VG)
NG += -(NG - 2) % 3
NV = NG * VG
GC = VG * CH
NC = NV * CH
HV = NV // 2
LB = NBLK // 2
BIG = 1e30

ROW = 2 * D
WOFF = D - 2 * H
WCOL = D + 2 * H
QC = D + H
SLOTS = 3
RING = SLOTS * GC * ROW
STEADY = (NG - 2) // SLOTS
USES = [len(range(s, NG, SLOTS)) for s in range(SLOTS)]
assert STEADY * SLOTS + 2 == NG


def hold(eng, sem, value, passed):
    eng.wait_ge(sem, value)
    eng.sem_inc(passed, 1)


class Steps:

    def __init__(self, sem, base=0):
        self.sem, self.base, self.n = sem, base, 0

    def did(self, ins):
        ins.then_inc(self.sem, 1)
        self.n += 1
        return self.n

    def sync(self, eng, n=None):
        eng.wait_ge(self.sem, self.base + (self.n if n is None else n))


PASSES = {
    "in": ["norm", "turn", "proj", "norm", "turn", "qkv"],
    "mid": ["agg", "turn", "proj", "norm", "turn", "mlp", "norm", "turn", "qkv"],
    "last": ["agg", "turn", "proj", "norm", "turn", "mlp", "norm"],
    "moe": ["take", "turn", "mlp", "norm"],
}
def count(kind, *names):
    return sum(s in names for s in PASSES[kind])


PREP_IND = 16
C_SP, C_ENDS, C_XY, C_DM, C_MU, C_ARG, C_SELF = 1, 5, 8, 10, 18, 21, 23
R_MEAN, R_E1, R_E2, R_E3, R_TOPW, R_WEIGHTS = 1, 4, 17, 38, 41, 46
W_STEPS = {"in": 7, "mid": 10, "last": 3}
D_STEPS = {"in": 21, "mid": 26, "last": 21, "moe": 25}


def program(nc, A, out):
    ctx = ExitStack()
    with ctx, nc.allow_non_contiguous_dma(reason="index tables and columns of vectors, once"):
        def sb(name, shape, dt=F32):
            return ctx.enter_context(nc.sbuf_tensor(name, shape, dt))

        def sem(name):
            return ctx.enter_context(nc.semaphore(name))

        def scratch(name, shape, dt=F32):
            return nc.dram_tensor(name, shape, dt, kind="Internal").ap()

        src_rows = scratch("src_rows", [NBLK + 1, BLK], I32)
        dst_rows = scratch("dst_rows", [NBLK + 1, BLK], I32)
        key_line = scratch("key_line", [1, NC * P + 2])
        dl_line = scratch("dl_line", [1, NC * P], BF16)
        pen_f = scratch("pen_f", [1, NC * P + P], BF16)
        pen_b = scratch("pen_b", [1, NC * P], BF16)
        kv_table = scratch("kv_table", [N, ROW])
        kv_table2 = scratch("kv_table2", [N, ROW])
        h_dram = scratch("h_dram", [N, D])

        ring = sb("ring", [P, RING])
        acc = sb("acc", [TN, NT * WCOL])
        qs = sb("qs", [TN, NT * 3 * QC], BF16)
        src_ix = sb("src_ix", [P, NC], U32)
        last_col = sb("last_col", [P, NC])
        dt = sb("dt", [TN, SLOTS, GC * P], BF16)
        pens = sb("pens", [P, SLOTS, 2, P], BF16)
        stage_ix = sb("stage_ix", [P, SLOTS, GC], U32)
        dhot = sb("dhot", [P, GC, TN])
        up_bias = sb("up_bias", [P, FFN // P])
        g_col = sb("g_col", [P, 4, 2])
        ident = sb("ident", [P, P])
        ident_b = sb("ident_b", [P, P], BF16)
        iota_f = sb("iota_f", [P, P])
        iota_p = sb("iota_p", [P, 1])
        ones = sb("ones", [P, P])
        half = sb("half", [P, BT])
        lane_h = sb("lane_h", [P, H])
        lane_hT = sb("lane_hT", [H, P])
        lane_c = sb("lane_c", [P, 2, GC])
        t_row = sb("t_row", [1, NV], I32)
        a_f = sb("a_f", [H, NC], BF16)
        a_b = sb("a_b", [H, NC], BF16)
        dl0 = sb("dl0", [H, NG])
        s_e = sb("s_e", [P, SLOTS, H, GC])
        ss_e = sb("ss_e", [P, SLOTS, H, GC])
        sp_e = sb("sp_e", [P, H, GC])
        own_e = sb("own_e", [P, H * GC])
        f_lane = sb("f_lane", [P, P])
        b_lane = sb("b_lane", [P, P])
        ends = sb("ends", [P, 2, GC])
        runs = sb("runs", [H, 2 * (GC + 2)])
        g_run, h_run = runs[:, 0:GC + 1], runs[:, GC + 1:2 * GC + 2]
        flows = runs[:, :].rearrange("p (a c) -> p a c", a=2)[:, :, 0:GC]
        xy_m = sb("xy_m", [P, 2, GC])
        xy_l = sb("xy_l", [P, 2])
        m_new = sb("m_new", [H, 4])
        r_diag = sb("r_diag", [H, H])
        delta = sb("delta", [H, TN])
        a_fac = sb("a_fac", [TN, H])
        arg = sb("arg", [P, 2, H * GC])
        small = sb("small", [P, 64])
        stat = sb("stat", [TN, BT, 6])
        mv = sb("mv", [TN, BT, 2])
        rs = sb("rs", [TN, BT])
        exp_ix = sb("exp_ix", [1, 2], I32)

        o = 0
        def part(n, p=P):
            nonlocal o
            v = ring[0:p, o:o + n]
            o += n
            return v
        up_T = part(FFN // P * BT * TN).rearrange("p (f n) -> p f n", f=FFN // P)
        kv_b = part(BT * ROW, TN).rearrange("p (j c) -> p j c", j=BT)
        tok = part(BT * D, TN).rearrange("p (j c) -> p j c", j=BT)
        tok_T = part(2 * BT * TN).rearrange("p (a n) -> p a n", a=2)
        qf = part(BT * QC, TN).rearrange("p (j c) -> p j c", j=BT)
        qr = part(BT * QC, TN).rearrange("p (j c) -> p j c", j=BT)
        x_in = part(BT * D, TN).rearrange("p (j c) -> p j c", j=BT)
        h_b = part(BT * D, TN).rearrange("p (j c) -> p j c", j=BT)
        w_qkv = part(2 * 3 * D).rearrange("p (a n) -> p a n", a=2)
        w_sq = part(2 * D).rearrange("p (a n) -> p a n", a=2)
        w_up = part(2 * FFN).rearrange("p (a n) -> p a n", a=2)
        w_down = part(FFN // P * D).rearrange("p (f n) -> p f n", f=FFN // P)
        row_qkv, row_sq, row_down = part(3 * D, 1), part(D, 1), part(D, 1)
        assert o <= RING
        o = 0
        e_i = part(2 * 2 * BLK, HV).rearrange("p (a m e) -> p a m e", a=2, m=2)
        e_src = part(2 * BLK, HV).rearrange("p (m e) -> p m e", m=2)
        e_dst = part(2 * BLK, HV).rearrange("p (m e) -> p m e", m=2)
        e_val = part(2 * BLK, HV).rearrange("p (m e) -> p m e", m=2)
        e_key = part(2 * BLK, HV).rearrange("p (m e) -> p m e", m=2)
        e_dl = part(2 * BLK, HV).rearrange("p (m e) -> p m e", m=2)
        e_prev = part(2 * BLK, HV).rearrange("p (m e) -> p m e", m=2)
        e_next = part(2 * BLK, HV).rearrange("p (m e) -> p m e", m=2)
        o_load = part(E // TN, TN)
        o_load2 = part(E // TN, TN)
        k_first = part(NC, H)
        k_last = part(NC, H)
        kp = part(NC + 2, H).bitcast(BF16)[:, 0:NC + 1]
        fill_m1 = part(BLK, 1)
        fill_0 = part(BLK, 1)
        b_dl = part(BLK, HV).bitcast(BF16).rearrange("p (m e) -> p m e", m=2)
        b_pf = part(BLK, HV).bitcast(BF16).rearrange("p (m e) -> p m e", m=2)
        b_pb = part(BLK, HV).bitcast(BF16).rearrange("p (m e) -> p m e", m=2)
        assert o <= RING

        bank = [ctx.enter_context(nc.psum_tensor(f"bank{i}", [P, 512], F32)) for i in range(8)]
        b_q, b_ss, b_acc, b_ch, b_p, b_hot = bank[0:2], bank[2], bank[3:5], bank[5], bank[6], bank[7]
        hot_T = b_hot[:, 0:CH * P // 2].bitcast(BF16).rearrange("p (c e) -> p c e", c=CH)

        chunk = ring[:, :].rearrange("p (g c w) -> p g c w", g=SLOTS, c=GC)
        acc_t = acc[:, :].rearrange("p (t w) -> p t w", t=NT)

        iota_v = part(NV)
        ind = part(2 * NV, LB).rearrange("p (a v) -> p a v", a=2)
        assert o <= RING

        S = {n: sem(n) for n in (
            "sp_passed", "pool_passed", "dve_passed", "pool_const", "pads", "edges_in", "edges_copied", "last_in", "prep", "prep_pe", "blocks", "keys", "penalties",
            "prep_done", "edges_over", "rows_in", "lines_out", "lines_in", "turned_rows",
            "w_in_dma", "w_pe", "w_dve", "w_step", "kv_out", "h_out", "out_done", "pass_over",
            "tab0", "tab1", "tab2", "hot_turned", "hot_copied", "onehot", "q_ready", "q_used", "score", "ss_ready", "ss_copied",
            "ch_dve", "ch_pe", "ch_act", "ix_staged", "w_ready", "d_ready", "agg", "agg_used", "edge_step", "route",
            "route_dma", "route_pe", "route_act", "chosen")}
        gath = [[sem(f"gath{g}{q}") for q in range(VG)] for g in range(SLOTS)]
        PS = {k: {n: sem(f"{n}_{k}") for n in (
            "x_in", "stat", "rs_ready", "rs_step", "dve", "tok", "turned", "evac", "mm", "used", "up", "gelu", "qf", "kvc", "cast", "rest", "done")}
            for k in PASSES}

        CH_DVE, CH_PE, CH_ACT = 23, 5, 4
        W_TOTAL = {"in": 10, "mid": 26, "last": 34}
        PASS_NO = {"in": 0, "mid": 1, "last": 2, "moe": 3}
        b2_rows = x_in[0:1, 0:TOPK, :]
        MLP_CUT = ((0, 3 * TN), (3 * TN, 2 * TN))

        def tiles_of(engine, visit, n):
            _, t = nc.values_load_multi_w_load_instructions(
                t_row[0:1, bass.ds(visit, n)], engines=[engine], min_val=0, max_val=NT - 1,
                skip_runtime_bounds_check_because="t_row is a count cut off at NT - 1")
            return t

        def in_slots(eng, group):
            for k in range(SLOTS):
                group(k, k, True)
            with eng.Fori(1, STEADY) as i:
                for u in range(SLOTS):
                    group(i * SLOTS + u, u, False)
            for k in (NG - 2, NG - 1):
                group(k, k % SLOTS, False)

        def in_steps(eng, step):
            def fixed(k):
                step(k, k % SLOTS, lambda j: (k + j) // SLOTS, k == 0, min(NG - 1 - k, 2))
            fixed(0)
            with eng.Fori(0, STEADY - 1) as i:
                for u in range(1, SLOTS + 1):
                    step(i * SLOTS + u, u % SLOTS, lambda j, u=u: i + (u + j) // SLOTS, False, 2)
            for k in range(NG - 1 - SLOTS, NG):
                fixed(k)

        block = ctx.enter_context(nc.Block())
        vec, ten, sca, gps, syn = nc.vector, nc.tensor, nc.scalar, nc.gpsimd, nc.sync


        @block.sync
        def _(sp):
            sp.dma_start(o_load.bitcast(I32), A["src"].rearrange("(p c) -> p c", p=TN)).then_inc(S["edges_in"], 16)
            sp.dma_start(o_load2.bitcast(I32), A["dst"].rearrange("(p c) -> p c", p=TN)).then_inc(S["edges_in"], 16)
            li = small[:, 0:2].bitcast(I32)
            ends_of = A["dst"][0:(NBLK - 1) * BLK].rearrange("(b e) -> b e", e=BLK)
            sp.dma_start(li[0:LB, 0:1], ends_of[0:LB, BLK - 1:BLK]).then_inc(S["last_in"], 16)
            sp.dma_start(li[0:LB - 1, 1:2], ends_of[LB:2 * LB - 1, BLK - 1:BLK]).then_inc(S["last_in"], 16)
            sp.dma_start(li[LB - 1:LB, 1:2], A["dst"].rearrange("(a e) -> a e", a=1)[:, E - 1:E]).then_inc(S["last_in"], 16)
            sp.wait_ge(S["edges_in"], 32)
            sp.wait_ge(S["pads"], 3)
            for rows, col, pad in ((src_rows, o_load, fill_0), (dst_rows, o_load2, fill_m1)):
                line = rows.rearrange("b e -> (b e)")
                sp.dma_start(line[0:E].rearrange("(p c) -> p c", p=TN), col.bitcast(I32)).then_inc(S["edges_copied"], 16)
                n, k = (NBLK + 1) * BLK - E, BLK
                for at, k in ((E, n - BLK), (E + n - BLK, BLK)):
                    sp.dma_start(line[at:at + k].rearrange("(a e) -> a e", a=1), pad[:, 0:k].bitcast(I32)).then_inc(S["edges_copied"], 16)
            sp.wait_ge(S["keys"], 1)
            by_visit = "a (m p e) -> p (a m) e"
            sp.dma_start(key_line[:, 1:1 + NC * P].rearrange(by_visit, m=2, p=HV), e_key).then_inc(S["lines_out"], 16)
            sp.dma_start(key_line[:, 0:1], small[0:1, 10:11]).then_inc(S["lines_out"], 16)
            sp.dma_start(key_line[:, NC * P + 1:NC * P + 2], small[0:1, 10:11]).then_inc(S["lines_out"], 16)
            sp.dma_start(dl_line.rearrange(by_visit, m=2, p=HV), b_dl).then_inc(S["lines_out"], 16)
            sp.wait_ge(S["lines_out"], 64)
            for t, off in ((e_prev, 0), (e_next, 2)):
                sp.dma_start(t, key_line[:, off:off + NC * P].rearrange(by_visit, m=2, p=HV)).then_inc(S["lines_in"], 16)
            firsts = key_line[:, 1:1 + NC * P].rearrange("a (c e) -> (a e) c", e=P)
            for hh in range(H):
                sp.dma_start(k_first[hh:hh + 1, :], firsts[0:1, :]).then_inc(S["lines_in"], 16)
                sp.dma_start(k_last[hh:hh + 1, :], firsts[P - 1:P, :]).then_inc(S["lines_in"], 16)
                sp.dma_start(a_f[hh:hh + 1, 0:NG], dl_line.rearrange("a (g e) -> (a e) g", e=GC * P)[0:1, :]).then_inc(S["lines_in"], 16)
            sp.wait_ge(S["penalties"], 1)
            sp.dma_start(pen_f[:, 0:NC * P].rearrange(by_visit, m=2, p=HV), b_pf).then_inc(S["lines_out"], 16)
            sp.dma_start(pen_b.rearrange(by_visit, m=2, p=HV), b_pb).then_inc(S["lines_out"], 16)
            sp.dma_start(pen_f[:, NC * P:NC * P + P], b_pf[0:1, 0, 0:P]).then_inc(S["lines_out"], 16)
            sp.wait_ge(S["lines_out"], 64 + 48)
            for hh in range(H):
                sp.dma_start(kp[hh:hh + 1, :], pen_f.rearrange("a (c e) -> (a e) c", e=P)[0:1, :]).then_inc(S["lines_in"], 16)

            def load_w(kind, layer):
                todo = []
                if kind == "in":
                    todo += [(w_sq[:, :, :], A["L0_gnn_w_in"].rearrange("(a p) n -> p a n", p=P)),
                             (row_sq[:, :], A["L0_gnn_b_in"].rearrange("(a n) -> a n", a=1))]
                else:
                    todo += [(w_sq[:, :, :], A["L0_gnn_wo"][layer].rearrange("(a p) n -> p a n", p=P)),
                             (row_sq[:, :], A["L0_gnn_bo"][layer:layer + 1, :]),
                             (w_up[:, :, :], A["L0_gnn_w1"][layer].rearrange("(a p) n -> p a n", p=P)),
                             (up_bias[:, :], A["L0_gnn_b1"][layer].rearrange("(f p) -> p f", p=P)),
                             (w_down[:, :, :], A["L0_gnn_w2"][layer].rearrange("(f p) n -> p f n", p=P)),
                             (row_down[:, :], A["L0_gnn_b2"][layer:layer + 1, :]),
                             (g_col[:, 2, :], A["L0_gnn_ln2_g"][layer].rearrange("(a p) -> p a", p=P)),
                             (g_col[:, 3, :], A["L0_gnn_ln2_b"][layer].rearrange("(a p) -> p a", p=P))]
                if kind in ("in", "mid"):
                    nl = 0 if kind == "in" else layer + 1
                    for i, n in enumerate("qkv"):
                        todo += [(w_qkv[:, :, i * D:(i + 1) * D], A[f"L0_gnn_w{n}"][nl].rearrange("(a p) n -> p a n", p=P)),
                                 (row_qkv[:, i * D:(i + 1) * D], A[f"L0_gnn_b{n}"][nl:nl + 1, :])]
                    todo += [(g_col[:, 0, :], A["L0_gnn_ln1_g"][nl].rearrange("(a p) -> p a", p=P)),
                             (g_col[:, 1, :], A["L0_gnn_ln1_b"][nl].rearrange("(a p) -> p a", p=P))]
                for o_, i_ in todo:
                    sp.dma_start(o_, i_).then_inc(S["w_in_dma"], 16)

            def dense(kind):
                s, no = PS[kind], PASS_NO[kind]
                with sp.Fori(0, NBATCH) as it:
                    def rows(t, c0=0, c1=None):
                        return t.rearrange("(t p) c -> p t c", p=TN)[:, bass.ds(it * BT, BT), c0:c1]
                    if kind in ("in", "last"):
                        sp.dma_start(x_in[:, :, :], rows(A["x"])).then_inc(s["x_in"], 16)
                    if kind != "in":
                        sp.dma_start(h_b[:, :, :], rows(h_dram)).then_inc(s["x_in"], 16)
                    if kind in ("mid", "last"):
                        sp.dma_start(kv_b[:, :, D:ROW], rows(kv_in, D, ROW)).then_inc(s["x_in"], 16)
                    if kind in ("in", "mid"):
                        for j in range(BT):
                            hold(sp, s["kvc"], it * BT + j + 1, S["sp_passed"])
                            sp.dma_start(kv_out.rearrange("(t p) c -> p t c", p=TN)[:, bass.ds(it * BT + j, 1), :],
                                         kv_b[:, j:j + 1, :]).then_inc(S["kv_out"], 16)
                    hold(sp, s["done"], it + 1, S["sp_passed"])
                    if kind == "moe":
                        sp.dma_start(rows(out), h_b[:, :, :]).then_inc(S["out_done"], 16)
                        hold(sp, S["out_done"], it * 16 + 16, S["sp_passed"])
                    else:
                        sp.dma_start(rows(h_dram), h_b[:, :, :]).then_inc(S["h_out"], 16)
                        hold(sp, S["h_out"], it * 16 + (no * NBATCH + 1) * 16, S["sp_passed"])
                    if kind in ("in", "mid"):
                        hold(sp, S["kv_out"], it * (BT * 16) + (no * NBATCH + 1) * BT * 16, S["sp_passed"])

            def tables(layer):
                def group(k, slot, first):
                    if not first:
                        hold(sp, S["agg"], k * VG + (layer * NV - (SLOTS - 1) * VG), S["sp_passed"])
                    t = S[f"tab{slot}"]
                    for hh in range(H):
                        for d, line in ((0, pen_f), (1, pen_b)):
                            sp.dma_start(pens[hh * GC:(hh + 1) * GC, slot, d, :],
                                         line[:, bass.ds(k * (GC * P), GC * P)].rearrange("a (c e) -> (a c) e", e=P)).then_inc(t, 16)
                    sp.dma_start(dt[:, slot, :], dl_line[:, bass.ds(k * (GC * P), GC * P)].to_broadcast([TN, GC * P])).then_inc(t, 16)
                in_slots(sp, group)

            sp.wait_ge(S["prep_done"], 1)
            load_w("in", 0)
            kv_in = kv_out = kv_table
            dense("in")
            sp.wait_ge(S["pass_over"], 1)
            tables(0)
            sp.wait_ge(S["edges_over"], 1)
            load_w("mid", 0)
            kv_out = kv_table2
            dense("mid")
            kv_in = kv_table2
            sp.wait_ge(S["pass_over"], 2)
            tables(1)
            sp.wait_ge(S["edges_over"], 2)
            load_w("last", 1)
            dense("last")
            sp.wait_ge(S["pass_over"], 3)
            r = S["route_dma"]
            sp.dma_start(w_qkv[:, 0, 0:2 * NEXP].rearrange("p (a n) -> p a n", a=2), A["L0_ffn_Wr"].rearrange("(a p) n -> p a n", p=P)).then_inc(r, 16)
            sp.dma_start(row_qkv[:, 0:NEXP], A["L0_ffn_br"].rearrange("(a n) -> a n", a=1)).then_inc(r, 16)
            sp.dma_start(row_qkv[:, D:2 * D], A["L0_ffn_gamma"].rearrange("(a n) -> a n", a=1)).then_inc(r, 16)
            sp.dma_start(row_qkv[:, 2 * D:3 * D], A["L0_ffn_beta"].rearrange("(a n) -> a n", a=1)).then_inc(r, 16)
            sp.wait_ge(S["chosen"], 1)
            f = FE // P
            for i in range(TOPK):
                ex = sp.value_load(exp_ix[0:1, i:i + 1], min_val=0, max_val=NEXP - 1)
                sp.dma_start(w_up[:, :, i * FE:(i + 1) * FE], A["L0_ffn_W1"].rearrange("x (a p) n -> p (x a) n", p=P)[:, bass.ds(ex * 2, 2), :]).then_inc(r, 16)
                sp.dma_start(up_bias[:, i * f:(i + 1) * f], A["L0_ffn_b1"].rearrange("x (f p) -> p (x f)", p=P)[:, bass.ds(ex * f, f)]).then_inc(r, 16)
                sp.dma_start(w_down[:, i * f:(i + 1) * f, :], A["L0_ffn_W2"].rearrange("x (f p) n -> p (x f) n", p=P)[:, bass.ds(ex * f, f), :]).then_inc(r, 16)
                sp.dma_start(b2_rows[:, i, :], A["L0_ffn_b2"][bass.ds(ex, 1), :]).then_inc(r, 16)
            dense("moe")

        @block.gpsimd
        def _(pool):
            c = S["pool_const"]
            gps.iota(iota_f[:, :], pattern=[[1, P]], base=0, channel_multiplier=0, allow_small_or_imprecise_dtypes=True).then_inc(c, 1)
            gps.iota(iota_p[:, :], pattern=[[0, 1]], base=0, channel_multiplier=1, allow_small_or_imprecise_dtypes=True).then_inc(c, 1)
            gps.iota(iota_v, pattern=[[1, NV]], base=0, channel_multiplier=0, allow_small_or_imprecise_dtypes=True).then_inc(c, 1)
            gps.memset(ident[:, :], 0.0).then_inc(c, 1)
            pool.wait_ge(c, 4)
            gps.affine_select(out=ident[:, :], in_=ident[:, :], compare_op=ALU.not_equal, fill=1.0, base=0,
                              pattern=[[-1, P]], channel_multiplier=1).then_inc(c, 1)
            pool.wait_ge(S["blocks"], 1)
            pool.wait_ge(S["edges_copied"], 96)
            for a, rows in enumerate((src_rows, dst_rows)):
                for m in range(2):
                    gps.indirect_dma_start(out=e_i[:, a, m, :].bitcast(I32), out_offset=None, in_=rows,
                                           in_offset=bass.IndirectOffsetOnAxis(ap=small[0:HV, 12 + m:13 + m].bitcast(U32), axis=0)).then_inc(S["rows_in"], 16)

            def dense(kind):
                s, n_norm = PS[kind], count(kind, "norm")
                with pool.Fori(0, NBATCH) as it:
                    for k in range(n_norm):
                        hold(pool, s["stat"], it * (n_norm * BT) + (k + 1) * BT, S["pool_passed"])
                        gps.tensor_scalar(rs[:, :], mv[:, :, 1], EPS, 1.0, ALU.add, ALU.mult).then_inc(s["rs_step"], 1)
                        hold(pool, s["rs_step"], it * n_norm + k + 1, S["pool_passed"])
                        gps.tensor_tensor(rs[:, :], rs[:, :], half[0:TN, :], ALU.pow).then_inc(s["rs_ready"], 1)

            def gathers(layer):
                def group(k, slot, first):
                    if not first:
                        hold(pool, S["agg"], k * VG + (layer * NV - (SLOTS - 1) * VG - VG + 1), S["pool_passed"])
                    gps.tensor_copy(stage_ix[:, slot, :], src_ix[:, bass.ds(k * GC, GC)]).then_inc(S["ix_staged"], 1)
                    hold(pool, S["ix_staged"], k + (layer * NG + 1), S["pool_passed"])
                    for cc in range(GC):
                        if cc and cc % CH == 0 and not first:
                            hold(pool, S["agg"], k * VG + (layer * NV - SLOTS * VG + cc // CH + 1), S["pool_passed"])
                        gps.indirect_dma_start(out=chunk[:, slot, cc, :], out_offset=None, in_=table,
                                               in_offset=bass.IndirectOffsetOnAxis(ap=stage_ix[:, slot, cc:cc + 1], axis=0)).then_inc(gath[slot][cc // CH], 16)
                in_slots(pool, group)

            dense("in")
            pool.wait_ge(S["kv_out"], NT * 16)
            pool.wait_ge(S["pass_over"], 1)
            pool.wait_ge(S["h_out"], NBATCH * 16)
            table = kv_table
            gathers(0)
            dense("mid")
            pool.wait_ge(S["kv_out"], 2 * NT * 16)
            pool.wait_ge(S["pass_over"], 2)
            pool.wait_ge(S["h_out"], 2 * NBATCH * 16)
            table = kv_table2
            gathers(1)
            dense("last")
            dense("moe")

        @block.tensor
        def _(pe):
            pe.wait_ge(S["prep"], PREP_IND)
            for j in range(2):
                ten.matmul(bank[0][:, 0:NV], ones[0:LB, :], ind[:, j, :], start=(j == 0), stop=(j == 1))
            for m in range(2):
                for j in range(2):
                    mm = ten.matmul(bank[1][0:HV, m:m + 1], ind[:, j, m * HV:(m + 1) * HV], ones[0:LB, 0:1], start=(j == 0), stop=(j == 1))
            mm.then_inc(S["prep_pe"], 1)
            pe.wait_ge(S["pool_const"], 5)
            pe.wait_ge(S["penalties"], 1)
            for a, t in enumerate((e_src, e_next)):
                for m in range(2):
                    for j in range(CH):
                        mm = ten.transpose(bank[2 + 2 * a + m][:, j * HV:(j + 1) * HV], t[:, m, j * P:(j + 1) * P], ident[0:HV, 0:HV])
            mm.then_inc(S["turned_rows"], 1)
            ten.transpose(bank[0][0:H, 256:256 + P], lane_h[:, :], ident[:, :]).then_inc(S["turned_rows"], 1)

            def fold(kind):
                pe.wait_ge(S["w_in_dma"], 16 * W_TOTAL[kind])
                mm = None
                if kind in ("in", "mid"):
                    for c0, c1, b in ((0, 512, bank[4]), (512, 768, bank[5])):
                        for a in range(2):
                            mm = ten.matmul(b[0:1, 0:c1 - c0], g_col[:, 1, a:a + 1], w_qkv[:, a, c0:c1], start=(a == 0), stop=(a == 1))
                if kind in ("mid", "last"):
                    for f in range(FFN // P):
                        for a in range(2):
                            mm = ten.matmul(bank[6][:, f:f + 1], w_up[:, a, f * P:(f + 1) * P], g_col[:, 3, a:a + 1], start=(a == 0), stop=(a == 1))
                mm.then_inc(S["w_pe"], 1)

            def dense(kind):
                s = PS[kind]
                n_turn, n_mm = count(kind, "turn") * BT, count(kind, "proj", "mlp", "qkv") * BT
                n_used = count(kind, "proj", "mlp") * BT
                n_mlp = FFN // P * 2
                with pe.Fori(0, NBATCH) as it:
                    turn = used = kvc = 0
                    for stage in PASSES[kind]:
                        if stage == "turn":
                            for j in range(BT):
                                pe.wait_ge(s["tok"], it * n_turn + turn + j + 1)
                                if j >= 2:
                                    pe.wait_ge(s["evac"], it * n_turn + turn + j - 1)
                                for a in range(2):
                                    mm = ten.transpose(bank[j % 2][:, a * TN:(a + 1) * TN], tok[:, j, a * P:(a + 1) * P], ident[0:TN, 0:TN])
                                mm.then_inc(s["turned"], 1)
                            turn += BT
                        elif stage == "proj":
                            for j in range(BT):
                                pe.wait_ge(s["evac"], it * n_turn + turn - BT + j + 1)
                                if j >= 3:
                                    pe.wait_ge(s["used"], it * n_used + used + j - 2)
                                o_ = bank[4 + j % 3][0:TN, 0:D]
                                ten.matmul(o_, ones[0:1, 0:TN], row_sq[:, :], start=True, stop=False)
                                for a in range(2):
                                    mm = ten.matmul(o_, tok_T[:, a, j * TN:(j + 1) * TN], w_sq[:, a, :], start=False, stop=(a == 1))
                                mm.then_inc(s["mm"], 1)
                            used += BT
                        elif stage == "mlp":
                            pe.wait_ge(s["evac"], it * n_turn + turn)
                            for n in range(n_mlp):
                                f, (c0, cn) = n // 2, MLP_CUT[n % 2]
                                if n >= 4:
                                    pe.wait_ge(s["gelu"], it * n_mlp + n - 3)
                                for a in range(2):
                                    mm = ten.matmul(bank[n % 4][:, 0:cn], w_up[:, a, f * P:(f + 1) * P], tok_T[:, a, c0:c0 + cn], start=(a == 0), stop=(a == 1))
                                mm.then_inc(s["up"], 1)
                            pe.wait_ge(s["gelu"], it * n_mlp + n_mlp)
                            for j in range(BT):
                                if j >= 3:
                                    pe.wait_ge(s["used"], it * n_used + used + j - 2)
                                o_ = bank[4 + j % 3][0:TN, 0:D]
                                ten.matmul(o_, ones[0:1, 0:TN], row_down[:, :], start=True, stop=False)
                                for f in range(FFN // P):
                                    mm = ten.matmul(o_, up_T[:, f, j * TN:(j + 1) * TN], w_down[:, f, :], start=False, stop=(f == FFN // P - 1))
                                mm.then_inc(s["mm"], 1)
                            used += BT
                        elif stage == "qkv":
                            for j in range(BT):
                                pe.wait_ge(s["evac"], it * n_turn + turn - BT + j + 1)
                                if j >= 2:
                                    pe.wait_ge(s["kvc"], it * BT + j - 1)
                                for c0, c1, b in ((0, 512, bank[4 + 2 * (j % 2)]), (512, 768, bank[5 + 2 * (j % 2)])):
                                    ten.matmul(b[0:TN, 0:c1 - c0], ones[0:1, 0:TN], row_qkv[:, c0:c1], start=True, stop=False)
                                    for a in range(2):
                                        mm = ten.matmul(b[0:TN, 0:c1 - c0], tok_T[:, a, j * TN:(j + 1) * TN], w_qkv[:, a, c0:c1], start=False, stop=(a == 1))
                                mm.then_inc(s["mm"], 1)

            def edges(layer):
                def queries(k, slot, t, pairs, first=False):
                    gk = k + layer * NG
                    if 0 in pairs:
                        pe.wait_ge(S["onehot"], gk + 1)
                        if not first:
                            pe.wait_ge(S["ss_copied"], gk)
                    for b in pairs:
                        if not (first and b < 2):
                            pe.wait_ge(S["q_used"], gk * (GC // 2) + b - 1)
                        for cc in (2 * b, 2 * b + 1):
                            hot = dt[:, slot, cc * P:(cc + 1) * P]
                            for p3 in range(3):
                                mm = ten.matmul(b_q[b % 2][:, cc % 2 * D:(cc % 2 + 1) * D], hot, qs[:, bass.ds(t[b // 2] * (3 * QC) + p3 * QC, D)], start=(p3 == 0), stop=(p3 == 2))
                            for p3 in range(3):
                                mm = ten.matmul(b_ss[:, cc * H:(cc + 1) * H], hot, qs[:, bass.ds(t[b // 2] * (3 * QC) + (p3 * QC + D), H)], start=(p3 == 0), stop=(p3 == 2))
                        mm.then_inc(S["q_ready"], 1)

                def turn_hot(k, slot, v, first):
                    if not (first and v == 0):
                        pe.wait_ge(S["hot_copied"], k * VG + (layer * NV + v))
                    for c4 in range(CH):
                        cc = v * CH + c4
                        mm = ten.transpose(hot_T[:, c4, 0:TN], dt[:, slot, cc * P:(cc + 1) * P], ident_b[0:TN, 0:TN])
                    mm.then_inc(S["hot_turned"], 1)

                def maxima(k, n):
                    pe.wait_ge(S["ch_dve"], (k + layer * NG) * CH_DVE + {1: C_SP, 2: C_ENDS, 3: C_XY}[n])
                    if n == 1:
                        mm = ten.transpose(b_ch[:, 0:P], sp_e[:, :, :].rearrange("p h c -> p (h c)"), ident[:, :])
                    elif n == 2:
                        mm = ten.matmul(b_ch[0:H, 128:160], lane_h[:, :], ends[:, :, :].rearrange("p a c -> p (a c)"), start=True, stop=True)
                    else:
                        mm = ten.matmul(b_ch[:, 160:192], lane_hT[:, :], flows, start=True, stop=True)
                    mm.then_inc(S["ch_pe"], 1)

                def step(k, slot, turn, first, left):
                    gk = k + layer * NG
                    first = first and layer == 0
                    if left:
                        t = tiles_of(mybir.EngineType.PE, (k + 1) * VG + 1, VG if left == 2 else VG - 1)
                        t1, t2 = (None,) + t[:VG - 1], t[VG - 1:]

                    def ahead(b):
                        if left:
                            queries(k + 1, (slot + 1) % SLOTS, t1, (b,))

                    def sums(v):
                        pe.wait_ge(S["hot_copied"], gk * VG + v + 1)
                        pe.wait_ge(S["w_ready"], gk * VG + v + 1)
                        if not (first and v < 2):
                            pe.wait_ge(S["agg_used"], gk * VG + v - 1)
                        for c4 in range(CH):
                            cc = v * CH + c4
                            mm = ten.matmul(b_acc[v % 2][0:TN, 0:WCOL], dhot[:, cc, :], chunk[:, slot, cc, WOFF:ROW], start=(c4 == 0), stop=(c4 == CH - 1))
                        mm.then_inc(S["agg"], 1)
                    turn_hot(k, slot, 0, first)
                    ahead(2)
                    pe.wait_ge(S["ch_dve"], gk * CH_DVE + C_MU)
                    ten.matmul(b_ch[0:TN, 192:192 + H], delta[:, :], r_diag[:, :], start=True, stop=True).then_inc(S["ch_pe"], 1)
                    ten.transpose(b_ch[:, 256:256 + P], f_lane[:, :], ident[:, :]).then_inc(S["ch_pe"], 1)
                    turn_hot(k, slot, 1, False)
                    ahead(3)
                    turn_hot(k, slot, 2, False)
                    ahead(4)
                    turn_hot(k, slot, 3, False)
                    ahead(5)
                    pe.wait_ge(S["ch_dve"], gk * CH_DVE + C_SELF)
                    sums(0)
                    ahead(6)
                    sums(1)
                    ahead(7)
                    sums(2)
                    if left == 2:
                        queries(k + 2, (slot + 2) % SLOTS, t2, (0,))
                    sums(3)
                    if left:
                        maxima(k + 1, 1)
                    if left == 2:
                        queries(k + 2, (slot + 2) % SLOTS, t2, (1,))
                    if left:
                        maxima(k + 1, 2)
                        maxima(k + 1, 3)

                queries(0, 0, tiles_of(mybir.EngineType.PE, 0, VG), range(GC // 2), layer == 0)
                maxima(0, 1)
                queries(1, 1, tiles_of(mybir.EngineType.PE, VG, 1), (0, 1))
                maxima(0, 2)
                maxima(0, 3)
                in_steps(pe, step)

            pe.wait_ge(S["prep_done"], 1)
            fold("in")
            pe.wait_ge(S["w_dve"], 1)
            dense("in")
            pe.wait_ge(S["pass_over"], 1)
            edges(0)
            fold("mid")
            pe.wait_ge(S["w_dve"], 2)
            dense("mid")
            pe.wait_ge(S["pass_over"], 2)
            edges(1)
            fold("last")
            pe.wait_ge(S["w_dve"], 3)
            dense("last")
            pe.wait_ge(S["pass_over"], 3)
            for a in range(2):
                for t in range(NT):
                    mm = ten.matmul(bank[0][:, a:a + 1], acc_t[:, t, a * P:(a + 1) * P], ones[0:TN, 0:1], start=(t == 0), stop=(t == NT - 1))
            mm.then_inc(S["route_pe"], 1)
            pe.wait_ge(S["route_dma"], 64)
            pe.wait_ge(S["route"], R_MEAN)
            for a in range(2):
                mm = ten.matmul(bank[1][0:1, 0:NEXP], small[:, a:a + 1], w_qkv[:, 0, a * NEXP:(a + 1) * NEXP], start=(a == 0), stop=(a == 1))
            mm.then_inc(S["route_pe"], 1)
            ten.matmul(bank[7][0:TN, :], ones[0:1, 0:TN], row_qkv[:, D:3 * D], start=True, stop=True).then_inc(S["route_pe"], 1)
            pe.wait_ge(S["route"], R_TOPW)
            ten.matmul(bank[2][:, 0:TOPK], ones[0:1, :], small[0:1, 62:64], start=True, stop=True).then_inc(S["route_pe"], 1)
            pe.wait_ge(S["route"], R_WEIGHTS)
            dense("moe")

        @block.scalar
        def _(act):
            def dense(kind):
                s = PS[kind]
                n_turn, n_mm = count(kind, "turn") * BT, count(kind, "proj", "mlp", "qkv") * BT
                n_mlp = FFN // P * 2
                with act.Fori(0, NBATCH) as it:
                    turn = mm = 0
                    for stage in PASSES[kind]:
                        if stage == "turn":
                            for j in range(BT):
                                act.wait_ge(s["turned"], it * n_turn + turn + j + 1)
                                sca.activation(tok_T[:, :, j * TN:(j + 1) * TN], bank[j % 2][:, 0:2 * TN].rearrange("p (a n) -> p a n", a=2), ACT.Copy).then_inc(s["evac"], 1)
                            turn += BT
                        elif stage == "mlp":
                            for n in range(n_mlp):
                                f, (c0, cn) = n // 2, MLP_CUT[n % 2]
                                act.wait_ge(s["up"], it * n_mlp + n + 1)
                                sca.activation(up_T[:, f, c0:c0 + cn], bank[n % 4][:, 0:cn], ACT.Gelu, bias=up_bias[:, f:f + 1]).then_inc(s["gelu"], 1)
                        elif stage == "qkv":
                            for j in range(BT):
                                act.wait_ge(s["mm"], it * n_mm + mm + j + 1)
                                b0, b1 = bank[4 + 2 * (j % 2)], bank[5 + 2 * (j % 2)]
                                sca.activation(qf[:, j, 0:D], b0[0:TN, 0:D], ACT.Copy)
                                sca.activation(kv_b[:, j, 0:D], b0[0:TN, D:2 * D], ACT.Copy)
                                sca.activation(kv_b[:, j, D:ROW].rearrange("p (d h) -> p h d", h=H),
                                               b1[0:TN, 0:D].rearrange("p (h d) -> p h d", h=H), ACT.Copy).then_inc(s["kvc"], 1)
                            for r, src in ((0, qf), (1, qr)):
                                act.wait_ge(s["qf"], it * 2 + r + 1)
                                dst = qs[:, bass.ds(it * (BT * 3 * QC) , BT * 3 * QC)].rearrange("p (j r c) -> p j r c", j=BT, r=3)[:, :, r, :]
                                sca.activation(dst, src, ACT.Copy).then_inc(s["cast"], 1)
                        if stage in ("proj", "mlp"):
                            mm += BT

            def edges(layer):
                def copy_self(k, slot):
                    act.wait_ge(S["q_ready"], (k + layer * NG) * (GC // 2) + GC // 2)
                    sca.activation(ss_e[:, slot, :, :].rearrange("p h c -> p c h"), b_ss[:, 0:P].rearrange("p (c h) -> p c h", h=H), ACT.Copy).then_inc(S["ss_copied"], 1)

                def step(k, slot, turn, first, left):
                    gk = k + layer * NG

                    def copy_hot(v):
                        act.wait_ge(S["hot_turned"], gk * VG + v + 1)
                        sca.activation(dhot[:, v * CH:(v + 1) * CH, :], hot_T[:, :, 0:TN], ACT.Copy).then_inc(S["hot_copied"], 1)
                    c = S["ch_act"]
                    act.wait_ge(S["ch_dve"], gk * CH_DVE + C_DM)
                    sca.activation(m_new[:, 2:3], m_new[:, 1:2], ACT.Exp).then_inc(c, 1)
                    copy_hot(0)
                    copy_hot(1)
                    act.wait_ge(S["ch_dve"], gk * CH_DVE + C_ARG)
                    a0 = arg[:, 0, :].rearrange("p (h c) -> p c h", h=H)
                    if not (first and layer == 0):
                        act.wait_ge(S["w_ready"], gk * VG)
                    sca.activation(b_p[:, 0:P].rearrange("p (c h) -> p c h", h=H), a0, ACT.Exp).then_inc(c, 1)
                    sca.activation(chunk[:, slot, :, WOFF:WOFF + H], a0, ACT.Exp).then_inc(c, 1)
                    sca.activation(own_e[:, :], arg[:, 1, :], ACT.Exp).then_inc(c, 1)
                    copy_hot(2)
                    copy_hot(3)
                    if left:
                        copy_self(k + 1, (slot + 1) % SLOTS)

                copy_self(0, 0)
                in_steps(act, step)

            dense("in")
            edges(0)
            dense("mid")
            edges(1)
            dense("last")
            for n, (at, i_, w, b_) in enumerate(((R_E1, 8, NEXP, 58), (R_E2, 16, NEXP, 58), (R_E3, 60, TOPK, 58))):
                act.wait_ge(S["route"], at)
                sca.activation(small[0:1, i_:i_ + w], small[0:1, i_:i_ + w], ACT.Exp, bias=small[0:1, b_:b_ + 1]).then_inc(S["route_act"], 1)
            dense("moe")

        @block.vector
        def _(v):
            tt, ts = vec.tensor_tensor, vec.tensor_scalar
            vec.memset(fill_m1.bitcast(I32), -1).then_inc(S["pads"], 1)
            vec.memset(fill_0.bitcast(I32), 0).then_inc(S["pads"], 1)
            vec.memset(small[0:1, 10:11], -2.0).then_inc(S["pads"], 1)
            st = Steps(S["prep"])

            def do(ins):
                st.did(ins)
                st.sync(v)

            vec.memset(half[:, :], -0.5)
            st.did(vec.memset(ones[:, :], 1.0))
            vec.memset(g_run[:, :], -BIG)
            do(vec.memset(h_run[:, :], -BIG))
            v.wait_ge(S["pool_const"], 5)
            do(vec.tensor_copy(ident_b[:, :], ident[:, :]))
            by_lane = ident[:, :].rearrange("p (h c) -> p h c", h=H)
            do(vec.tensor_reduce(lane_h[:, :], by_lane, AX.X, ALU.add))
            for a in range(2):
                do(vec.tensor_reduce(lane_c[:, a, :], by_lane.rearrange("p h c -> p c h"), AX.X, ALU.add))
            v.wait_ge(S["last_in"], 48)
            do(vec.tensor_copy(small[0:LB, 2:4], small[0:LB, 0:2].bitcast(I32)))
            do(ts(small[:, 20:20 + NT - 1], iota_f[:, 1:NT], float(TN), None, ALU.mult))
            for j in range(2):
                do(ts(e_src[0:LB, 0, 0:NT - 1], small[0:LB, 20:20 + NT - 1], small[0:LB, 2 + j:3 + j], None, ALU.is_le))
                do(vec.tensor_reduce(small[0:LB, 4 + j:5 + j], e_src[0:LB, 0, 0:NT - 1], AX.X, ALU.add))
                do(ts(small[0:LB, 6 + j:7 + j], small[0:LB, 4 + j:5 + j], iota_p[0:LB, :], float(j * LB), ALU.add, ALU.add))
                do(ts(ind[:, j, :], iota_v[0:LB, :], small[0:LB, 6 + j:7 + j], None, ALU.is_gt))
            assert st.n == PREP_IND, st.n
            v.wait_ge(S["prep_pe"], 1)
            do(vec.tensor_copy(small[0:HV, 16:18], bank[1][0:HV, 0:2]))
            vec.tensor_copy(small[0:HV, 12:14].bitcast(U32), small[0:HV, 16:18]).then_inc(S["blocks"], 1)
            for m in range(2):
                do(ts(small[0:HV, 18 + m:19 + m], small[0:HV, 16 + m:17 + m], iota_p[0:HV, :], -1.0, ALU.subtract, ALU.mult))
                do(ts(small[0:HV, 18 + m:19 + m], small[0:HV, 18 + m:19 + m], float(m * HV), float(NT - 1), ALU.add, ALU.min))
                do(ts(small[0:HV, 18 + m:19 + m], small[0:HV, 18 + m:19 + m], float(TN), None, ALU.mult))
            do(tt(iota_v[0:1, :], iota_v[0:1, :], bank[0][0:1, 0:NV], ALU.subtract))
            do(ts(iota_v[0:1, :], iota_v[0:1, :], float(NT - 1), None, ALU.min))
            do(vec.tensor_copy(t_row[:, :], iota_v[0:1, :]))
            v.wait_ge(S["rows_in"], 64)
            st.did(vec.tensor_copy(e_src, e_i[:, 0, :, :].bitcast(I32)))
            do(vec.tensor_copy(e_dst, e_i[:, 1, :, :].bitcast(I32)))
            for m in range(2):
                do(ts(e_dl[:, m, :], e_dst[:, m, :], small[0:HV, 18 + m:19 + m], None, ALU.subtract))
            do(ts(e_val, e_dl, 0.0, None, ALU.is_ge))
            do(ts(e_key, e_dl, float(TN), None, ALU.is_lt))
            do(tt(e_val, e_val, e_key, ALU.mult))
            for t, s_ in ((e_key, e_dst), (e_dl, e_dl)):
                do(vec.scalar_tensor_tensor(out=t, in0=s_, scalar=1.0, in1=e_val, op0=ALU.add, op1=ALU.mult))
                do(ts(t, t, -1.0, None, ALU.add))
            vec.tensor_copy(b_dl, e_dl).then_inc(S["keys"], 1)
            v.wait_ge(S["lines_in"], 16 * (2 + 3 * H))
            st.did(tt(e_prev, e_key, e_prev, ALU.is_equal))
            do(tt(e_next, e_key, e_next, ALU.is_equal))
            st.did(ts(b_pf, e_prev, BIG, -BIG, ALU.mult, ALU.add))
            do(ts(b_pb, e_next, BIG, -BIG, ALU.mult, ALU.add))
            do(ts(e_next, e_next, -1.0, 1.0, ALU.mult, ALU.add))
            tt(e_next, e_next, e_val, ALU.mult).then_inc(S["penalties"], 1)
            v.wait_ge(S["turned_rows"], 2)
            for a, (t, dst) in enumerate(((e_src, src_ix), (e_next, last_col))):
                for m in range(2):
                    st.did(vec.tensor_copy(dst[:, :].rearrange("p (v j) -> p j v", j=CH)[:, :, m * HV:(m + 1) * HV],
                                           bank[2 + 2 * a + m][:, 0:CH * HV].rearrange("p (j v) -> p j v", j=CH)))
            st.did(vec.tensor_copy(lane_hT[:, :], bank[0][0:H, 256:256 + P]))
            v.wait_ge(S["lines_in"], 16 * (2 + 4 * H))
            do(tt(k_first, k_first, k_last, ALU.is_equal))
            do(ts(k_first, k_first, BIG, -BIG, ALU.mult, ALU.add))
            at_group = kp[:, 0:NC].rearrange("p (g c) -> p g c", c=GC)[:, :, 0]
            do(ts(dl0[:, :], at_group, 0.0, None, ALU.is_equal))
            do(ts(k_last[:, 0:NG], a_f[:, 0:NG], 1.0, None, ALU.add))
            do(tt(dl0[:, :], dl0[:, :], k_last[:, 0:NG], ALU.mult))
            do(ts(dl0[:, :], dl0[:, :], -1.0, None, ALU.add))
            do(tt(a_f[:, :], k_first, kp[:, 0:NC], ALU.min))
            do(tt(a_b[:, :].rearrange("p (g c) -> p g c", c=GC)[:, :, ::-1], k_first.rearrange("p (g c) -> p g c", c=GC),
                  kp[:, 1:NC + 1].rearrange("p (g c) -> p g c", c=GC), ALU.min))
            v.sem_inc(S["prep_done"], 1)

            def fold(kind):
                w = S["w_step"]
                n0 = {"in": 0, "mid": W_STEPS["in"], "last": W_STEPS["in"] + W_STEPS["mid"]}[kind]
                ws = Steps(w, n0)
                v.wait_ge(S["w_pe"], PASS_NO[kind] + 1)
                sc = DH ** -0.5
                if kind in ("in", "mid"):
                    ws.did(tt(row_qkv[:, 0:512], row_qkv[:, 0:512], bank[4][0:1, 0:512], ALU.add))
                    ws.did(tt(row_qkv[:, 512:768], row_qkv[:, 512:768], bank[5][0:1, 0:256], ALU.add))
                    for a in range(2):
                        ws.did(ts(w_qkv[:, a, 0:D], w_qkv[:, a, 0:D], g_col[:, 0, a:a + 1], sc, ALU.mult, ALU.mult))
                        ws.did(ts(w_qkv[:, a, D:3 * D], w_qkv[:, a, D:3 * D], g_col[:, 0, a:a + 1], None, ALU.mult))
                    ws.sync(v)
                    ws.did(ts(row_qkv[:, 0:D], row_qkv[:, 0:D], sc, None, ALU.mult))
                if kind in ("mid", "last"):
                    ws.did(tt(up_bias[:, :], up_bias[:, :], bank[6][:, 0:FFN // P], ALU.add))
                    for a in range(2):
                        ws.did(ts(w_up[:, a, :], w_up[:, a, :], g_col[:, 2, a:a + 1], None, ALU.mult))
                ws.sync(v)
                assert ws.n == W_STEPS[kind], ws.n
                v.sem_inc(S["w_dve"], 1)

            def dense(kind):
                s = PS[kind]
                n_tok, n_mm = count(kind, "turn") * BT, count(kind, "proj", "mlp", "qkv") * BT
                n_used = count(kind, "proj", "mlp") * BT
                n_norm = count(kind, "norm")
                n_x = {"in": 16, "mid": 32, "last": 48, "moe": 16}[kind]
                with v.Fori(0, NBATCH) as it:
                    st = Steps(s["dve"], it * D_STEPS[kind])
                    mm = used = norm = tokn = 0
                    v.wait_ge(s["x_in"], it * n_x + n_x)
                    tiles = acc[:, bass.ds(it * (BT * WCOL), BT * WCOL)].rearrange("p (j w) -> p j w", j=BT)
                    for k, stage in enumerate(PASSES[kind]):
                        if stage == "agg":
                            z, own = tiles[:, :, 0:H], tiles[:, :, H:2 * H]
                            val = tiles[:, :, 2 * H:WCOL].rearrange("p j (d h) -> p j d h", h=H)
                            den = small[0:TN, 0:BT * H].rearrange("p (j h) -> p j h", h=H)
                            st.did(tt(den, z, own, ALU.add)); st.sync(v)
                            st.did(ts(den, den, 1e-30, None, ALU.max)); st.sync(v)
                            st.did(vec.reciprocal(den, den)); st.sync(v)
                            mine = kv_b[:, :, D:ROW].rearrange("p j (d h) -> p j d h", h=H)
                            def over_d(x):
                                return x.rearrange("p j (a h) -> p j a h", a=1).to_broadcast([TN, BT, DH, H])
                            st.did(tt(mine, mine, over_d(own), ALU.mult)); st.sync(v)
                            st.did(tt(mine, mine, val, ALU.add)); st.sync(v)
                            for j in range(BT):
                                tt(tok[:, j, :].rearrange("p (h d) -> p d h", h=H), kv_b[:, j, D:ROW].rearrange("p (d h) -> p d h", h=H),
                                   den[:, j:j + 1, :].to_broadcast([TN, DH, H]), ALU.mult).then_inc(s["tok"], 1)
                            tokn += BT
                        elif stage == "take":
                            for j in range(BT):
                                vec.tensor_copy(tok[:, j, :], tiles[:, j, 0:D]).then_inc(s["tok"], 1)
                            tokn += BT
                        elif stage in ("proj", "mlp"):
                            for j in range(BT):
                                v.wait_ge(s["mm"], it * n_mm + mm + j + 1)
                                r = bank[4 + j % 3][0:TN, 0:D]
                                if kind == "in":
                                    vec.tensor_copy(h_b[:, j, :], r).then_inc(s["used"], 1)
                                elif kind == "moe":
                                    tt(tok[:, j, :], tok[:, j, :], r, ALU.add).then_inc(s["used"], 1)
                                else:
                                    tt(h_b[:, j, :], h_b[:, j, :], r, ALU.add).then_inc(s["used"], 1)
                            mm += BT
                            used += BT
                            v.wait_ge(s["used"], it * n_used + used)
                            if kind == "last" and stage == "mlp":
                                st.did(tt(h_b[:, :, :], h_b[:, :, :], x_in[:, :, :], ALU.add)); st.sync(v)
                        elif stage == "norm":
                            src = x_in[:, :, :] if kind == "in" and norm == 0 else tok if kind == "moe" else h_b[:, :, :]
                            for j in range(BT):
                                st.did(vec.bn_stats(stat[:, j, :], src[:, j, :]))
                            hold(v, s["dve"], st.base + st.n, S["dve_passed"])
                            for j in range(BT):
                                vec.bn_aggr(mv[:, j, :], stat[:, j, :]).then_inc(s["stat"], 1)
                            norm += 1
                            v.wait_ge(s["stat"], it * (n_norm * BT) + norm * BT)
                            v.wait_ge(s["rs_ready"], it * n_norm + norm)
                            feeds = k + 1 < len(PASSES[kind])
                            for j in range(BT):
                                dst = tok[:, j, :] if kind != "last" or feeds else tiles[:, j, 0:D]
                                ins = ts(dst, src[:, j, :], mv[:, j, 0:1], rs[:, j:j + 1], ALU.subtract, ALU.mult)
                                if feeds:
                                    ins.then_inc(s["tok"], 1)
                                else:
                                    st.did(ins)
                            if feeds:
                                tokn += BT
                            else:
                                st.sync(v)
                            if kind == "moe":
                                for j in range(BT):
                                    st.did(tt(tok[:, j, :], tok[:, j, :], bank[7][0:TN, 0:D], ALU.mult)); st.sync(v)
                                    st.did(tt(tok[:, j, :], tok[:, j, :], bank[7][0:TN, D:2 * D], ALU.add)); st.sync(v)
                                    st.did(tt(h_b[:, j, :], h_b[:, j, :], tok[:, j, :], ALU.add))
                                st.sync(v)
                        elif stage == "qkv":
                            for j in range(BT):
                                v.wait_ge(s["kvc"], it * BT + j + 1)
                                st.did(tt(qr[:, j, 0:D], qf[:, j, 0:D], kv_b[:, j, 0:D], ALU.mult)); st.sync(v)
                                ins = vec.tensor_reduce(qf[:, j, D:QC], qr[:, j, 0:D].rearrange("p (h d) -> p h d", h=H), AX.X, ALU.add)
                                st.did(ins)
                            st.sync(v)
                            v.sem_inc(s["qf"], 1)
                            q3 = qs[:, bass.ds(it * (BT * 3 * QC), BT * 3 * QC)].rearrange("p (j r c) -> p j r c", j=BT, r=3)
                            v.wait_ge(s["cast"], it * 2 + 1)
                            tt(qr, qf, q3[:, :, 0, :], ALU.subtract).then_inc(s["qf"], 1)
                            v.wait_ge(s["cast"], it * 2 + 2)
                            st.did(tt(q3[:, :, 2, :], qr, q3[:, :, 1, :], ALU.subtract))
                            st.sync(v)
                    assert st.n == D_STEPS[kind], (kind, st.n)
                    v.sem_inc(s["done"], 1)
                v.sem_inc(S["pass_over"], 1)

            def edges(layer):
                es = Steps(S["edge_step"], layer * 2)
                es.did(vec.memset(acc[:, :], 0.0))
                es.did(vec.memset(g_run[:, GC:GC + 1], -BIG))
                es.sync(v)

                def onehot(k, slot, turn):
                    v.wait_ge(S[f"tab{slot}"], turn * (17 * 16) + (layer * USES[slot] + 1) * 17 * 16)
                    ts(dt[:, slot, :], dt[:, slot, :], iota_p[0:TN, :], None, ALU.is_equal).then_inc(S["onehot"], 1)

                def scores(k, slot, turn, b):
                    gk = k + layer * NG
                    if b % 2 == 0:
                        v.wait_ge(gath[slot][b // 2], turn * (CH * 16) + (layer * USES[slot] + 1) * CH * 16)
                    v.wait_ge(S["q_ready"], gk * (GC // 2) + b + 1)
                    pair = chunk[:, slot, 2 * b:2 * b + 2, 0:D]
                    tt(pair, pair, b_q[b % 2][:, :].rearrange("p (c w) -> p c w", c=2), ALU.mult).then_inc(S["q_used"], 1)
                    if b % 2:
                        v.wait_ge(S["q_used"], gk * (GC // 2) + b + 1)
                        c0 = 2 * b - 2
                        vec.tensor_reduce(s_e[:, slot, :, c0:c0 + CH].rearrange("p h c -> p c h"),
                                          chunk[:, slot, c0:c0 + CH, 0:D].rearrange("p c (h d) -> p c h d", h=H), AX.X, ALU.add).then_inc(S["score"], 1)

                def pe(k, n):
                    v.wait_ge(S["ch_pe"], (k + layer * NG) * CH_PE + n)

                def scores_max(k, slot, st):
                    v.wait_ge(S["score"], (k + layer * NG) * VG + VG)
                    v.wait_ge(S["ss_copied"], k + (layer * NG + 1))
                    st.did(tt(sp_e[:, :, :], s_e[:, slot, :, :], ss_e[:, slot, :, :], ALU.max))
                    assert st.n == C_SP

                def in_chunks(k, slot, st):
                    pf, pb, sT = pens[:, slot, 0, :], pens[:, slot, 1, :], b_ch[:, 0:P]
                    pe(k, 1)
                    st.did(vec.tensor_tensor_scan(f_lane[:, 1:P], pf[:, 1:P], sT[:, 1:P], sT[:, 0:1], ALU.add, ALU.max))
                    st.did(vec.tensor_tensor_scan(b_lane[:, ::-1][:, 1:P], pb[:, ::-1][:, 1:P], sT[:, ::-1][:, 1:P], sT[:, P - 1:P], ALU.add, ALU.max))
                    st.sync(v)
                    st.did(ts(ends[:, 0, :], lane_c[:, 0, :], f_lane[:, P - 1:P], None, ALU.mult))
                    st.did(ts(ends[:, 1, :], lane_c[:, 0, :], b_lane[:, 0:1], None, ALU.mult))
                    assert st.n == C_ENDS
                    st.did(vec.tensor_copy(g_run[:, 0:1], g_run[:, GC:GC + 1]))

                def over_chunks(k, st):
                    st.sync(v)
                    pe(k, 2)
                    c0 = k * GC
                    st.did(vec.tensor_tensor_scan(g_run[:, 1:GC + 1], a_f[:, bass.ds(c0, GC)], b_ch[0:H, 128:128 + GC], g_run[:, 0:1], ALU.add, ALU.max))
                    st.did(vec.tensor_tensor_scan(h_run[:, 0:GC][:, ::-1], a_b[:, bass.ds(c0, GC)], b_ch[0:H, 128 + GC:128 + 2 * GC][:, ::-1], -BIG, ALU.add, ALU.max))
                    assert st.n == C_XY
                    st.sync(v)
                    st.did(tt(m_new[:, 0:1], h_run[:, 0:1], g_run[:, 0:1], ALU.max))
                    st.sync(v)
                    st.did(tt(m_new[:, 1:2], g_run[:, 0:1], m_new[:, 0:1], ALU.subtract))
                    assert st.n == C_DM

                def step(k, slot, turn, first, left):
                    gk = k + layer * NG
                    nxt = (slot + 1) % SLOTS
                    st = Steps(S["ch_dve"], gk * CH_DVE)
                    st.n = C_DM
                    head = Steps(S["ch_dve"], (gk + 1) * CH_DVE)
                    t = tiles_of(mybir.EngineType.DVE, k * VG, VG)

                    def do(ins):
                        st.did(ins)
                        st.sync(v)

                    def ahead(b):
                        if left:
                            scores(k + 1, nxt, turn(1), b)

                    def weigh(q):
                        val = chunk[:, slot, q * CH:(q + 1) * CH, D:ROW].rearrange("p c (d h) -> p c d h", h=H)
                        w = b_p[:, q * CH * H:(q + 1) * CH * H].rearrange("p (c a h) -> p c a h", c=CH, a=1).to_broadcast([P, CH, DH, H])
                        tt(val, val, w, ALU.mult).then_inc(S["w_ready"], 1)

                    def add(q):
                        v.wait_ge(S["agg"], gk * VG + q + 1)
                        if q == 0:
                            st.sync(v)
                        else:
                            v.wait_ge(S["agg_used"], gk * VG + q)
                        at = acc[:, bass.ds(t[q] * WCOL, WCOL)]
                        tt(at, at, b_acc[q % 2][0:TN, 0:WCOL], ALU.add).then_inc(S["agg_used"], 1)

                    pf, pb, sT = pens[:, slot, 0, :], pens[:, slot, 1, :], b_ch[:, 0:P]
                    st.did(ts(delta[:, :], iota_f[0:H, 0:TN], dl0[:, bass.ds(k, 1)], None, ALU.is_equal))
                    ahead(0)
                    pe(k, 3)
                    do(tt(xy_m[:, :, :], lane_c[:, :, :], b_ch[:, 160:192].rearrange("p (a c) -> p a c", a=2), ALU.mult))
                    do(vec.tensor_reduce(xy_l[:, :], xy_m[:, :, :], AX.X, ALU.add))
                    st.did(vec.tensor_tensor_scan(f_lane[:, :], pf, sT, xy_l[:, 0:1], ALU.add, ALU.max))
                    st.did(vec.tensor_tensor_scan(b_lane[:, ::-1], pb[:, ::-1], sT[:, ::-1], xy_l[:, 1:2], ALU.add, ALU.max))
                    v.wait_ge(S["ch_act"], gk * CH_ACT + 1)
                    do(ts(m_new[:, 3:4], m_new[:, 2:3], -1.0, None, ALU.add))
                    st.did(ts(r_diag[:, :], ident[0:H, 0:H], m_new[:, 3:4], None, ALU.mult))
                    st.did(tt(f_lane[:, :], f_lane[:, :], b_lane[:, :], ALU.max))
                    assert st.n == C_MU
                    ahead(1)
                    pe(k, 5)
                    st.did(ts(a_fac[:, :], b_ch[0:TN, 192:192 + H], 1.0, None, ALU.add))
                    mu = b_ch[:, 256:256 + P]
                    st.did(tt(arg[:, 0, :], s_e[:, slot, :, :].rearrange("p h c -> p (h c)"), mu, ALU.subtract))
                    st.did(tt(arg[:, 1, :], ss_e[:, slot, :, :].rearrange("p h c -> p (h c)"), mu, ALU.subtract))
                    assert st.n == C_ARG
                    st.sync(v, C_ARG - 2)
                    if not first:
                        v.wait_ge(S["agg_used"], gk * VG)
                    at = acc[:, bass.ds(t[0] * WCOL, WCOL)].rearrange("p (x h) -> p x h", h=H)
                    st.did(tt(at, at, a_fac[:, :].rearrange("p (a h) -> p a h", a=1).to_broadcast([TN, WCOL // H, H]), ALU.mult))
                    ahead(2)
                    ahead(3)
                    v.wait_ge(S["ch_act"], gk * CH_ACT + CH_ACT)
                    st.did(tt(chunk[:, slot, :, WOFF + H:WOFF + 2 * H], own_e[:, :].rearrange("p (h c) -> p c h", h=H),
                              last_col[:, bass.ds(k * GC, GC)].rearrange("p (c a) -> p c a", a=1).to_broadcast([P, GC, H]), ALU.mult))
                    assert st.n == C_SELF == CH_DVE
                    weigh(0)
                    ahead(4)
                    weigh(1)
                    ahead(5)
                    add(0)
                    weigh(2)
                    if left == 2:
                        onehot(k + 2, (slot + 2) % SLOTS, turn(2))
                    ahead(6)
                    add(1)
                    weigh(3)
                    ahead(7)
                    if left:
                        scores_max(k + 1, nxt, head)
                    add(2)
                    if left:
                        in_chunks(k + 1, nxt, head)
                    add(3)
                    if left:
                        over_chunks(k + 1, head)
                    else:
                        v.wait_ge(S["agg_used"], gk * VG + VG)

                onehot(0, 0, 0)
                onehot(1, 1, 0)
                for b in range(GC // 2):
                    scores(0, 0, 0, b)
                head = Steps(S["ch_dve"], layer * NG * CH_DVE)
                scores_max(0, 0, head)
                in_chunks(0, 0, head)
                over_chunks(0, head)
                in_steps(v, step)
                v.sem_inc(S["edges_over"], 1)

            fold("in")
            dense("in")
            edges(0)
            fold("mid")
            dense("mid")
            edges(1)
            fold("last")
            dense("last")

            st = Steps(S["route"])

            def col(c, n=NEXP):
                return small[0:1, c:c + n]

            def softmax_top(x, e_no, n=NEXP):
                do(vec.tensor_reduce(col(58, 1), col(x, n), AX.X, ALU.max))
                do(ts(col(58, 1), col(58, 1), -1.0, None, ALU.mult))
                assert st.n == (R_E1, R_E2, R_E3)[e_no], (e_no, st.n)
                v.wait_ge(S["route_act"], e_no + 1)
                do(vec.tensor_reduce(col(59, 1), col(x, n), AX.X, ALU.add))
                do(vec.reciprocal(col(59, 1), col(59, 1)))

            v.wait_ge(S["route_pe"], 1)
            do(ts(small[:, 0:2], bank[0][:, 0:2], 1.0 / N, None, ALU.mult))
            assert st.n == R_MEAN
            v.wait_ge(S["route_pe"], 2)
            do(tt(col(8), bank[1][0:1, 0:NEXP], row_qkv[:, 0:NEXP], ALU.add))
            softmax_top(8, 0)
            do(ts(col(8), col(8), col(59, 1), None, ALU.mult))
            do(ts(col(16), col(8), float(N), None, ALU.mult))
            do(ts(col(24), col(16), CAPACITY, None, ALU.is_gt))
            do(ts(col(16), col(16), CAPACITY, None, ALU.max))
            do(vec.reciprocal(col(16), col(16)))
            do(ts(col(16), col(16), CAPACITY, -1.0, ALU.mult, ALU.add))
            do(tt(col(16), col(16), col(24), ALU.mult))
            do(ts(col(16), col(16), 1.0, None, ALU.add))
            do(tt(col(16), col(16), col(8), ALU.mult))
            softmax_top(16, 1)
            do(ts(col(16), col(16), col(59, 1), None, ALU.mult))
            for i in range(TOPK):
                do(vec.tensor_reduce(col(60 + i, 1), col(16), AX.X, ALU.max))
                do(ts(col(24), col(16), col(60 + i, 1), None, ALU.is_equal))
                do(ts(col(32), col(24), -99.0, 99.0, ALU.mult, ALU.add))
                do(tt(col(24), col(24), iota_f[0:1, 0:NEXP], ALU.mult))
                do(tt(col(32), col(32), col(24), ALU.add))
                do(vec.tensor_reduce(col(40 + i, 1), col(32), AX.X, ALU.min))
                do(ts(col(24), iota_f[0:1, 0:NEXP], col(40 + i, 1), -10.0, ALU.is_equal, ALU.mult))
                do(tt(col(16), col(16), col(24), ALU.add))
            vec.tensor_copy(exp_ix[:, :], col(40, TOPK)).then_inc(S["chosen"], 1)
            softmax_top(60, 2, TOPK)
            do(ts(col(62, TOPK), col(60, TOPK), col(59, 1), None, ALU.mult))
            assert st.n == R_TOPW, st.n
            v.wait_ge(S["route_pe"], 4)
            do(vec.tensor_copy(small[:, 4:6], bank[2][:, 0:TOPK]))
            v.wait_ge(S["route_dma"], 16 * (4 + 4 * TOPK))
            f = FE // P
            for i in range(TOPK):
                st.did(ts(w_down[:, i * f:(i + 1) * f, :], w_down[:, i * f:(i + 1) * f, :], small[:, 4 + i:5 + i], None, ALU.mult))
            do(ts(row_down[:, :], b2_rows[:, 0, :], col(4, 1), None, ALU.mult))
            do(vec.scalar_tensor_tensor(out=row_down[:, :], in0=b2_rows[:, 1, :], scalar=col(5, 1), in1=row_down[:, :], op0=ALU.mult, op1=ALU.add))
            assert st.n == R_WEIGHTS, st.n
            dense("moe")


_INS = ["x", "src", "dst"] + [f"L0_gnn_{n}" for n in (
    "w_in", "b_in", "ln1_g", "ln1_b", "ln2_g", "ln2_b", "wq", "bq", "wk", "bk", "wv", "bv", "wo", "bo", "w1", "b1", "w2", "b2")] + [
    f"L0_ffn_{n}" for n in ("Wr", "br", "W1", "b1", "W2", "b2", "gamma", "beta")]


def kernel(**inputs):
    import numpy as _np
    import concourse.bacc as _bacc
    from concourse import mybir as _mybir
    from concourse.bass_utils import run_bass_kernel_spmd as _run

    nc = _bacc.Bacc("TRN2", target_bir_lowering=False, num_devices=1)
    arrays, args = {}, {}
    for name in _INS:
        a = _np.ascontiguousarray(inputs[name])
        arrays[f"in_{name}_dram"] = a
        args[name] = nc.dram_tensor(f"in_{name}_dram", a.shape, _mybir.dt.from_np(a.dtype), kind="ExternalInput").ap()
    out = nc.dram_tensor("out_0_dram", (N, D), _mybir.dt.float32, kind="ExternalOutput").ap()
    program(nc, args, out)
    r = _run(nc, [arrays], core_ids=[0])
    return r.results[0]["out_0_dram"]
```

```python
from contextlib import ExitStack

import concourse.bass as bass
from concourse import mybir

ALU = mybir.AluOpType
ACT = mybir.ActivationFunctionType
AX = mybir.AxisListType
F32 = mybir.dt.float32
BF16 = mybir.dt.bfloat16
I32 = mybir.dt.int32
U32 = mybir.dt.uint32

N, D, E = 3125, 256, 100000
H, DH = 8, 32
LAYERS, FFN = 2, 1024
NEXP, FE, TOPK = 8, 512, 2
EPS = 1e-5
CAPACITY = float(-(-(N * 125) // (NEXP * 100)))

P = 128
TN = 125
NT = N // TN
BT = 5
NBATCH = NT // BT

BLK = 512
NBLK = -(-E // BLK)
CH = BLK // P
VG = 4
NG = -(-(NBLK + NT - 1) // VG)
NG += -(NG - 2) % 3
NV = NG * VG
GC = VG * CH
NC = NV * CH
HV = NV // 2
LB = NBLK // 2
BIG = 1e30

ROW = 2 * D
WOFF = D - 2 * H
WCOL = D + 2 * H
QC = D + H
SLOTS = 3
RING = SLOTS * GC * ROW
STEADY = (NG - 2) // SLOTS
USES = [len(range(s, NG, SLOTS)) for s in range(SLOTS)]
assert STEADY * SLOTS + 2 == NG


def hold(eng, sem, value, passed):
    eng.wait_ge(sem, value)
    eng.sem_inc(passed, 1)


class Steps:

    def __init__(self, sem, base=0):
        self.sem, self.base, self.n = sem, base, 0

    def did(self, ins):
        ins.then_inc(self.sem, 1)
        self.n += 1
        return self.n

    def sync(self, eng, n=None):
        eng.wait_ge(self.sem, self.base + (self.n if n is None else n))


PASSES = {
    "in": ["norm", "turn", "proj", "norm", "turn", "qkv"],
    "mid": ["agg", "turn", "proj", "norm", "turn", "mlp", "norm", "turn", "qkv"],
    "last": ["agg", "turn", "proj", "norm", "turn", "mlp", "norm"],
    "moe": ["take", "turn", "mlp", "norm"],
}
def count(kind, *names):
    return sum(s in names for s in PASSES[kind])


PREP_IND = 17
C_SP, C_ENDS, C_XY, C_DM, C_MU, C_ARG, C_SELF = 1, 6, 8, 10, 18, 21, 23
R_MEAN, R_E1, R_E2, R_E3, R_TOPW, R_WEIGHTS = 1, 4, 17, 38, 41, 46
W_STEPS = {"in": 7, "mid": 10, "last": 3}
H_STEPS = {"in": 5, "mid": 6, "last": 6, "moe": 1}
D_STEPS = {"in": 19, "mid": 25, "last": 17, "moe": 21}


def program(nc, A, out):
    ctx = ExitStack()
    with ctx, nc.allow_non_contiguous_dma(reason="index tables and columns of vectors, once"):
        def sb(name, shape, dt=F32):
            return ctx.enter_context(nc.sbuf_tensor(name, shape, dt))

        def sem(name):
            return ctx.enter_context(nc.semaphore(name))

        def scratch(name, shape, dt=F32):
            return nc.dram_tensor(name, shape, dt, kind="Internal").ap()

        src_rows = scratch("src_rows", [NBLK + 1, BLK], I32)
        dst_rows = scratch("dst_rows", [NBLK + 1, BLK], I32)
        key_line = scratch("key_line", [1, NC * P + 2])
        dl_line = scratch("dl_line", [1, NC * P], BF16)
        pen_lines = scratch("pen_lines", [2, NC * P + P], BF16)
        pen_f, pen_b = pen_lines[0:1, :], pen_lines[1:2, 0:NC * P]
        kv_table = scratch("kv_table", [N, ROW])
        kv_table2 = scratch("kv_table2", [N, ROW])
        h_dram = scratch("h_dram", [N, D])

        ring = sb("ring", [P, RING])
        acc = sb("acc", [TN, NT * WCOL])
        qs = sb("qs", [TN, NT * 3 * QC], BF16)
        src_ix = sb("src_ix", [P, NC], U32)
        last_col = sb("last_col", [P, NC])
        dt = sb("dt", [TN, SLOTS, GC * P], BF16)
        pens = sb("pens", [P, SLOTS, 2, P], BF16)
        stage_ix = sb("stage_ix", [P, SLOTS, GC], U32)
        dhot = sb("dhot", [P, GC, TN])
        up_bias = sb("up_bias", [P, FFN // P])
        g_col = sb("g_col", [P, 4, 2])
        ident = sb("ident", [P, P])
        ident_b = sb("ident_b", [P, P], BF16)
        iota_f = sb("iota_f", [P, P])
        iota_p = sb("iota_p", [P, 1])
        minus_p = sb("minus_p", [P, 1])
        ones = sb("ones", [P, P])
        half = sb("half", [P, BT])
        lane_h = sb("lane_h", [P, H])
        lane_hT = sb("lane_hT", [H, P])
        lane_c = sb("lane_c", [P, 2, GC])
        t_row = sb("t_row", [1, NV], I32)
        a_f = sb("a_f", [H, NC], BF16)
        a_b = sb("a_b", [H, NC], BF16)
        dl0 = sb("dl0", [H, NG])
        s_e = sb("s_e", [P, SLOTS, H, GC])
        ss_e = sb("ss_e", [P, SLOTS, H, GC])
        sp_e = sb("sp_e", [P, H, GC])
        own_e = sb("own_e", [P, H * GC])
        f_lane = sb("f_lane", [P, P])
        b_lane = sb("b_lane", [P, P])
        ends = sb("ends", [P, 2, GC])
        runs = sb("runs", [H, 2 * (GC + 2)])
        g_run, h_run = runs[:, 0:GC + 1], runs[:, GC + 1:2 * GC + 2]
        flows = runs[:, :].rearrange("p (a c) -> p a c", a=2)[:, :, 0:GC]
        xy_m = sb("xy_m", [P, 2, GC])
        xy_l = sb("xy_l", [P, 2])
        m_new = sb("m_new", [H, 4])
        r_diag = sb("r_diag", [H, H])
        delta = sb("delta", [H, TN])
        a_fac = sb("a_fac", [TN, H])
        arg = sb("arg", [P, 2, H * GC])
        small = sb("small", [P, 64])
        stat = sb("stat", [TN, BT, 6])
        mv = sb("mv", [TN, BT, 2])
        rs = sb("rs", [TN, BT])
        exp_ix = sb("exp_ix", [1, 2], I32)

        o = 0
        def part(n, p=P):
            nonlocal o
            v = ring[0:p, o:o + n]
            o += n
            return v
        up_T = part(FFN // P * BT * TN).rearrange("p (f n) -> p f n", f=FFN // P)
        kv_b = part(BT * ROW, TN).rearrange("p (j c) -> p j c", j=BT)
        tok = part(BT * D, TN).rearrange("p (j c) -> p j c", j=BT)
        tok_T = part(2 * BT * TN).rearrange("p (a n) -> p a n", a=2)
        qf = part(BT * QC, TN).rearrange("p (j c) -> p j c", j=BT)
        qr = part(BT * QC, TN).rearrange("p (j c) -> p j c", j=BT)
        x_in = part(BT * D, TN).rearrange("p (j c) -> p j c", j=BT)
        h_b = part(BT * D, TN).rearrange("p (j c) -> p j c", j=BT)
        own_v = part(BT * D, TN).rearrange("p (j c) -> p j c", j=BT)
        h_spare = kv_b.rearrange("p j c -> p (j c)")[:, 0:BT * D].rearrange("p (j c) -> p j c", j=BT)
        h_n = {"mid": x_in, "last": h_spare, "moe": h_spare}
        w_qkv = part(2 * 3 * D).rearrange("p (a n) -> p a n", a=2)
        w_sq = part(2 * D).rearrange("p (a n) -> p a n", a=2)
        w_up = part(2 * FFN).rearrange("p (a n) -> p a n", a=2)
        w_down = part(FFN // P * D).rearrange("p (f n) -> p f n", f=FFN // P)
        row_qkv = part(3 * D, 1)
        bias_sq, bias_down = part(D, TN), part(D, TN)
        assert o <= RING
        o = 0
        e_i = part(2 * 2 * BLK, HV).rearrange("p (a m e) -> p a m e", a=2, m=2)
        e_src = part(2 * BLK, HV).rearrange("p (m e) -> p m e", m=2)
        e_dst = part(2 * BLK, HV).rearrange("p (m e) -> p m e", m=2)
        e_val = part(2 * BLK, HV).rearrange("p (m e) -> p m e", m=2)
        e_key = part(2 * BLK, HV).rearrange("p (m e) -> p m e", m=2)
        e_dl = part(2 * BLK, HV).rearrange("p (m e) -> p m e", m=2)
        e_prev = part(2 * BLK, HV).rearrange("p (m e) -> p m e", m=2)
        e_next = part(2 * BLK, HV).rearrange("p (m e) -> p m e", m=2)
        o_load = part(E // TN, TN)
        o_load2 = part(E // TN, TN)
        k_first = part(NC, H)
        k_last = part(NC, H)
        kp = part(NC + 2, H).bitcast(BF16)[:, 0:NC + 1]
        fill_m1 = part(BLK, 1)
        fill_0 = part(BLK, 1)
        b_dl = part(BLK, HV).bitcast(BF16).rearrange("p (m e) -> p m e", m=2)
        b_pf = part(BLK, HV).bitcast(BF16).rearrange("p (m e) -> p m e", m=2)
        b_pb = part(BLK, HV).bitcast(BF16).rearrange("p (m e) -> p m e", m=2)
        assert o <= RING

        bank = [ctx.enter_context(nc.psum_tensor(f"bank{i}", [P, 512], F32)) for i in range(8)]
        b_q, b_ss, b_acc, b_ch, b_p, b_hot = bank[0:2], bank[2], bank[3:5], bank[5], bank[6], bank[7]
        hot_T = b_hot[:, 0:CH * P // 2].bitcast(BF16).rearrange("p (c e) -> p c e", c=CH)

        chunk = ring[:, :].rearrange("p (g c w) -> p g c w", g=SLOTS, c=GC)
        acc_t = acc[:, :].rearrange("p (t w) -> p t w", t=NT)

        iota_v = part(NV)
        ind = part(2 * NV, LB).rearrange("p (a v) -> p a v", a=2)
        assert o <= RING

        S = {n: sem(n) for n in (
            "sp_passed", "pool_passed", "dve_passed", "pool_const", "pads", "edges_in", "edges_copied", "last_in", "prep", "prep_pe", "blocks", "keys", "penalties",
            "prep_done", "edges_over", "rows_in", "lines_out", "lines_in", "turned_rows",
            "w_in_dma", "w_pe", "w_dve", "w_step", "kv_out", "h_out", "out_done", "pass_over",
            "tab0", "tab1", "tab2", "dl_abs", "hot_turned", "hot_copied", "onehot", "q_ready", "q_used", "score", "ss_copied",
            "ch_dve", "ch_pe", "ch_act", "ix_staged", "w_ready", "agg", "agg_used", "edge_step", "route",
            "route_dma", "route_pe", "route_act", "chosen")}
        gath = [[sem(f"gath{g}{q}") for q in range(VG)] for g in range(SLOTS)]
        PS = {k: {n: sem(f"{n}_{k}") for n in (
            "x_in", "x_late", "out_free", "head", "stat", "rs_ready", "rs_step", "dve", "tok", "turned", "evac", "mm", "bank_free", "up", "gelu", "kvc", "done")}
            for k in PASSES}

        CH_DVE, CH_PE, CH_ACT = 23, 5, 4
        W_TOTAL = {"in": 10, "mid": 26, "last": 34}
        PASS_NO = {"in": 0, "mid": 1, "last": 2, "moe": 3}
        b2_rows = x_in[:, 0:TOPK, :]
        MLP_CUT = ((0, 3 * TN), (3 * TN, 2 * TN))

        def tiles_of(engine, visit, n):
            _, t = nc.values_load_multi_w_load_instructions(
                t_row[0:1, bass.ds(visit, n)], engines=[engine], min_val=0, max_val=NT - 1,
                skip_runtime_bounds_check_because="t_row is a count cut off at NT - 1")
            return t

        def in_slots(eng, group, begun=False):
            if not begun:
                for k in range(SLOTS):
                    group(k, k, True)
            with eng.Fori(1, STEADY) as i:
                for u in range(SLOTS):
                    group(i * SLOTS + u, u, False)
            for k in (NG - 2, NG - 1):
                group(k, k % SLOTS, False)

        def in_steps(eng, step):
            def fixed(k):
                step(k, k % SLOTS, lambda j: (k + j) // SLOTS, k == 0, min(NG - 1 - k, 2))
            fixed(0)
            with eng.Fori(0, STEADY - 1) as i:
                for u in range(1, SLOTS + 1):
                    step(i * SLOTS + u, u % SLOTS, lambda j, u=u: i + (u + j) // SLOTS, False, 2)
            for k in range(NG - 1 - SLOTS, NG):
                fixed(k)

        block = ctx.enter_context(nc.Block())
        vec, ten, sca, gps, syn = nc.vector, nc.tensor, nc.scalar, nc.gpsimd, nc.sync


        @block.sync
        def _(sp):
            sp.dma_start(o_load.bitcast(I32), A["src"].rearrange("(p c) -> p c", p=TN)).then_inc(S["edges_in"], 16)
            sp.dma_start(o_load2.bitcast(I32), A["dst"].rearrange("(p c) -> p c", p=TN)).then_inc(S["edges_in"], 16)
            li = small[:, 0:2].bitcast(I32)
            ends_of = A["dst"][0:(NBLK - 1) * BLK].rearrange("(b e) -> b e", e=BLK)
            sp.dma_start(li[0:LB, 0:1], ends_of[0:LB, BLK - 1:BLK]).then_inc(S["last_in"], 16)
            sp.dma_start(li[0:LB - 1, 1:2], ends_of[LB:2 * LB - 1, BLK - 1:BLK]).then_inc(S["last_in"], 16)
            sp.dma_start(li[LB - 1:LB, 1:2], A["dst"].rearrange("(a e) -> a e", a=1)[:, E - 1:E]).then_inc(S["last_in"], 16)
            sp.wait_ge(S["edges_in"], 32)
            sp.wait_ge(S["pads"], 3)
            for rows, col, pad in ((src_rows, o_load, fill_0), (dst_rows, o_load2, fill_m1)):
                line = rows.rearrange("b e -> (b e)")
                sp.dma_start(line[0:E].rearrange("(p c) -> p c", p=TN), col.bitcast(I32)).then_inc(S["edges_copied"], 16)
                n, k = (NBLK + 1) * BLK - E, BLK
                for at, k in ((E, n - BLK), (E + n - BLK, BLK)):
                    sp.dma_start(line[at:at + k].rearrange("(a e) -> a e", a=1), pad[:, 0:k].bitcast(I32)).then_inc(S["edges_copied"], 16)
            sp.wait_ge(S["keys"], 1)
            by_visit = "a (m p e) -> p (a m) e"
            sp.dma_start(key_line[:, 1:1 + NC * P].rearrange(by_visit, m=2, p=HV), e_key).then_inc(S["lines_out"], 16)
            sp.dma_start(key_line[:, 0:1], small[0:1, 10:11]).then_inc(S["lines_out"], 16)
            sp.dma_start(key_line[:, NC * P + 1:NC * P + 2], small[0:1, 10:11]).then_inc(S["lines_out"], 16)
            sp.dma_start(dl_line.rearrange(by_visit, m=2, p=HV), b_dl).then_inc(S["lines_out"], 16)
            sp.wait_ge(S["lines_out"], 64)
            for t, off in ((e_prev, 0), (e_next, 2)):
                sp.dma_start(t, key_line[:, off:off + NC * P].rearrange(by_visit, m=2, p=HV)).then_inc(S["lines_in"], 16)
            firsts = key_line[:, 1:1 + NC * P].rearrange("a (c e) -> (a e) c", e=P)
            for hh in range(H):
                sp.dma_start(k_first[hh:hh + 1, :], firsts[0:1, :]).then_inc(S["lines_in"], 16)
                sp.dma_start(k_last[hh:hh + 1, :], firsts[P - 1:P, :]).then_inc(S["lines_in"], 16)
                sp.dma_start(a_f[hh:hh + 1, 0:NG], dl_line.rearrange("a (g e) -> (a e) g", e=GC * P)[0:1, :]).then_inc(S["lines_in"], 16)
            sp.wait_ge(S["penalties"], 1)
            sp.dma_start(pen_f[:, 0:NC * P].rearrange(by_visit, m=2, p=HV), b_pf).then_inc(S["lines_out"], 16)
            sp.dma_start(pen_b.rearrange(by_visit, m=2, p=HV), b_pb).then_inc(S["lines_out"], 16)
            sp.dma_start(pen_f[:, NC * P:NC * P + P], b_pf[0:1, 0, 0:P]).then_inc(S["lines_out"], 16)
            sp.wait_ge(S["lines_out"], 64 + 48)
            for hh in range(H):
                sp.dma_start(kp[hh:hh + 1, :], pen_f.rearrange("a (c e) -> (a e) c", e=P)[0:1, :]).then_inc(S["lines_in"], 16)

            def load_w(kind, layer):
                todo = []
                if kind == "in":
                    todo += [(w_sq[:, :, :], A["L0_gnn_w_in"].rearrange("(a p) n -> p a n", p=P)),
                             (bias_sq[:, :], A["L0_gnn_b_in"].rearrange("(a n) -> a n", a=1).to_broadcast([TN, D]))]
                else:
                    todo += [(w_sq[:, :, :], A["L0_gnn_wo"][layer].rearrange("(a p) n -> p a n", p=P)),
                             (bias_sq[:, :], A["L0_gnn_bo"][layer:layer + 1, :].to_broadcast([TN, D])),
                             (w_up[:, :, :], A["L0_gnn_w1"][layer].rearrange("(a p) n -> p a n", p=P)),
                             (up_bias[:, :], A["L0_gnn_b1"][layer].rearrange("(f p) -> p f", p=P)),
                             (w_down[:, :, :], A["L0_gnn_w2"][layer].rearrange("(f p) n -> p f n", p=P)),
                             (bias_down[:, :], A["L0_gnn_b2"][layer:layer + 1, :].to_broadcast([TN, D])),
                             (g_col[:, 2, :], A["L0_gnn_ln2_g"][layer].rearrange("(a p) -> p a", p=P)),
                             (g_col[:, 3, :], A["L0_gnn_ln2_b"][layer].rearrange("(a p) -> p a", p=P))]
                if kind in ("in", "mid"):
                    nl = 0 if kind == "in" else layer + 1
                    for i, n in enumerate("qkv"):
                        todo += [(w_qkv[:, :, i * D:(i + 1) * D], A[f"L0_gnn_w{n}"][nl].rearrange("(a p) n -> p a n", p=P)),
                                 (row_qkv[:, i * D:(i + 1) * D], A[f"L0_gnn_b{n}"][nl:nl + 1, :])]
                    todo += [(g_col[:, 0, :], A["L0_gnn_ln1_g"][nl].rearrange("(a p) -> p a", p=P)),
                             (g_col[:, 1, :], A["L0_gnn_ln1_b"][nl].rearrange("(a p) -> p a", p=P))]
                for o_, i_ in todo:
                    sp.dma_start(o_, i_).then_inc(S["w_in_dma"], 16)

            def dense(kind):
                s, no = PS[kind], PASS_NO[kind]
                n_tok, n_used = count(kind, "turn") * BT, count(kind, "proj", "mlp") * BT

                def rows(t, it, c0=0, c1=None):
                    return t.rearrange("(t p) c -> p t c", p=TN)[:, bass.ds(it * BT, BT), c0:c1]

                def load_x(it):
                    sp.dma_start(x_in[:, :, :], rows(A["x"], it)).then_inc(s["x_late" if kind == "last" else "x_in"], 16)

                def load_h(it):
                    sp.dma_start(h_n[kind][:, :, :], rows(h_dram, it)).then_inc(s["x_in"], 16)

                def load_v(it):
                    sp.dma_start(own_v[:, :, :], rows(kv_in, it, D, ROW)).then_inc(s["x_in"], 16)

                def batch(it, last):
                    if not last:
                        if kind == "in":
                            hold(sp, s["tok"], it * n_tok + BT, S["sp_passed"])
                            load_x(it + 1)
                        if kind in ("mid", "last"):
                            hold(sp, s["tok"], it * n_tok + BT, S["sp_passed"])
                            load_v(it + 1)
                            hold(sp, s["bank_free"], it * n_used + BT + 3, S["sp_passed"])
                            load_h(it + 1)
                        if kind == "last":
                            hold(sp, s["stat"], it * (2 * BT) + 2 * BT, S["sp_passed"])
                            load_x(it + 1)
                    if kind in ("in", "mid"):
                        for j in range(BT):
                            hold(sp, s["kvc"], it * BT + j + 1, S["sp_passed"])
                            sp.dma_start(kv_out.rearrange("(t p) c -> p t c", p=TN)[:, bass.ds(it * BT + j, 1), :],
                                         kv_b[:, j:j + 1, :]).then_inc(S["kv_out"], 16)
                    hold(sp, s["done"], it + 1, S["sp_passed"])
                    if kind == "moe":
                        sp.dma_start(rows(out, it), h_b[:, :, :]).then_inc(S["out_done"], 16)
                        if not last:
                            load_h(it + 1)
                        hold(sp, S["out_done"], it * 16 + 16, s["out_free"])
                    else:
                        sp.dma_start(rows(h_dram, it), h_b[:, :, :]).then_inc(S["h_out"], 16)
                        if kind in ("in", "mid"):
                            hold(sp, S["kv_out"], it * (BT * 16) + (no * NBATCH + 1) * BT * 16, S["sp_passed"])
                        hold(sp, S["h_out"], it * 16 + (no * NBATCH + 1) * 16, s["out_free"])

                sp.sem_inc(s["out_free"], 1)
                if kind in ("mid", "last"):
                    load_v(0)
                if kind != "in":
                    load_h(0)
                if kind in ("in", "last"):
                    load_x(0)
                if kind in ("in", "mid"):
                    tables(no, True)
                with sp.Fori(0, NBATCH - 1) as it:
                    batch(it, False)
                batch(NBATCH - 1, True)

            def tables(layer, begin):
                def group(k, slot, first):
                    if not first:
                        hold(sp, S["agg"], k * VG + (layer * NV - (SLOTS - 1) * VG), S["sp_passed"])
                    t = S[f"tab{slot}"]
                    for hh in range(H):
                        sp.dma_start(pens[hh * GC:(hh + 1) * GC, slot, :, :],
                                     pen_lines[:, bass.ds(k * (GC * P), GC * P)].rearrange("a (c e) -> c a e", e=P)).then_inc(t, 16)
                    sp.dma_start(dt[:, slot, :], dl_line[:, bass.ds(k * (GC * P), GC * P)].to_broadcast([TN, GC * P])).then_inc(t, 16)
                if begin:
                    for k in range(SLOTS):
                        group(k, k, True)
                else:
                    in_slots(sp, group, begun=True)

            sp.wait_ge(S["prep_done"], 1)
            load_w("in", 0)
            kv_in = kv_out = kv_table
            dense("in")
            sp.wait_ge(S["pass_over"], 1)
            tables(0, False)
            sp.wait_ge(S["edges_over"], 1)
            load_w("mid", 0)
            kv_out = kv_table2
            dense("mid")
            kv_in = kv_table2
            sp.wait_ge(S["pass_over"], 2)
            tables(1, False)
            sp.wait_ge(S["edges_over"], 2)
            load_w("last", 1)
            dense("last")
            sp.wait_ge(S["pass_over"], 3)
            r = S["route_dma"]
            sp.dma_start(w_qkv[:, 0, 0:2 * NEXP].rearrange("p (a n) -> p a n", a=2), A["L0_ffn_Wr"].rearrange("(a p) n -> p a n", p=P)).then_inc(r, 16)
            sp.dma_start(row_qkv[:, 0:NEXP], A["L0_ffn_br"].rearrange("(a n) -> a n", a=1)).then_inc(r, 16)
            sp.dma_start(row_qkv[:, D:2 * D], A["L0_ffn_gamma"].rearrange("(a n) -> a n", a=1)).then_inc(r, 16)
            sp.dma_start(row_qkv[:, 2 * D:3 * D], A["L0_ffn_beta"].rearrange("(a n) -> a n", a=1)).then_inc(r, 16)
            sp.wait_ge(S["chosen"], 1)
            f = FE // P
            for i in range(TOPK):
                ex = sp.value_load(exp_ix[0:1, i:i + 1], min_val=0, max_val=NEXP - 1)
                sp.dma_start(w_up[:, :, i * FE:(i + 1) * FE], A["L0_ffn_W1"].rearrange("x (a p) n -> p (x a) n", p=P)[:, bass.ds(ex * 2, 2), :]).then_inc(r, 16)
                sp.dma_start(up_bias[:, i * f:(i + 1) * f], A["L0_ffn_b1"].rearrange("x (f p) -> p (x f)", p=P)[:, bass.ds(ex * f, f)]).then_inc(r, 16)
                sp.dma_start(w_down[:, i * f:(i + 1) * f, :], A["L0_ffn_W2"].rearrange("x (f p) n -> p (x f) n", p=P)[:, bass.ds(ex * f, f), :]).then_inc(r, 16)
                sp.dma_start(b2_rows[:, i, :], A["L0_ffn_b2"][bass.ds(ex, 1), :].to_broadcast([TN, D])).then_inc(r, 16)
            dense("moe")

        @block.gpsimd
        def _(pool):
            c = S["pool_const"]
            gps.iota(iota_f[:, :], pattern=[[1, P]], base=0, channel_multiplier=0, allow_small_or_imprecise_dtypes=True).then_inc(c, 1)
            gps.iota(iota_p[:, :], pattern=[[0, 1]], base=0, channel_multiplier=1, allow_small_or_imprecise_dtypes=True).then_inc(c, 1)
            gps.iota(iota_v, pattern=[[1, NV]], base=0, channel_multiplier=0, allow_small_or_imprecise_dtypes=True).then_inc(c, 1)
            gps.memset(ident[:, :], 0.0).then_inc(c, 1)
            pool.wait_ge(c, 4)
            gps.affine_select(out=ident[:, :], in_=ident[:, :], compare_op=ALU.not_equal, fill=1.0, base=0,
                              pattern=[[-1, P]], channel_multiplier=1).then_inc(c, 1)
            pool.wait_ge(S["blocks"], 1)
            pool.wait_ge(S["edges_copied"], 96)
            for a, rows in enumerate((src_rows, dst_rows)):
                for m in range(2):
                    gps.indirect_dma_start(out=e_i[:, a, m, :].bitcast(I32), out_offset=None, in_=rows,
                                           in_offset=bass.IndirectOffsetOnAxis(ap=small[0:HV, 12 + m:13 + m].bitcast(U32), axis=0)).then_inc(S["rows_in"], 16)

            def dense(kind):
                s, n_norm = PS[kind], count(kind, "norm")
                with pool.Fori(0, NBATCH) as it:
                    for k in range(n_norm):
                        hold(pool, s["stat"], it * (n_norm * BT) + (k + 1) * BT, S["pool_passed"])
                        gps.tensor_scalar(rs[:, :], mv[:, :, 1], EPS, 1.0, ALU.add, ALU.mult).then_inc(s["rs_step"], 1)
                        hold(pool, s["rs_step"], it * n_norm + k + 1, S["pool_passed"])
                        gps.tensor_tensor(rs[:, :], rs[:, :], half[0:TN, :], ALU.pow).then_inc(s["rs_ready"], 1)

            def gathers(layer):
                def group(k, slot, first):
                    if not first:
                        hold(pool, S["agg"], k * VG + (layer * NV - (SLOTS - 1) * VG - VG + 1), S["pool_passed"])
                    gps.tensor_copy(stage_ix[:, slot, :], src_ix[:, bass.ds(k * GC, GC)]).then_inc(S["ix_staged"], 1)
                    hold(pool, S["ix_staged"], k + (layer * NG + 1), S["pool_passed"])
                    for cc in range(GC):
                        if cc and cc % CH == 0 and not first:
                            hold(pool, S["agg"], k * VG + (layer * NV - SLOTS * VG + cc // CH + 1), S["pool_passed"])
                        gps.indirect_dma_start(out=chunk[:, slot, cc, :], out_offset=None, in_=table,
                                               in_offset=bass.IndirectOffsetOnAxis(ap=stage_ix[:, slot, cc:cc + 1], axis=0)).then_inc(gath[slot][cc // CH], 16)
                in_slots(pool, group)

            dense("in")
            pool.wait_ge(S["kv_out"], NT * 16)
            pool.wait_ge(S["pass_over"], 1)
            pool.wait_ge(S["h_out"], NBATCH * 16)
            table = kv_table
            gathers(0)
            dense("mid")
            pool.wait_ge(S["kv_out"], 2 * NT * 16)
            pool.wait_ge(S["pass_over"], 2)
            pool.wait_ge(S["h_out"], 2 * NBATCH * 16)
            table = kv_table2
            gathers(1)
            dense("last")
            dense("moe")

        @block.tensor
        def _(pe):
            pe.wait_ge(S["prep"], PREP_IND)
            for j in range(2):
                ten.matmul(bank[0][:, 0:NV], ones[0:LB, :], ind[:, j, :], start=(j == 0), stop=(j == 1))
            for m in range(2):
                for j in range(2):
                    mm = ten.matmul(bank[1][0:HV, m:m + 1], ind[:, j, m * HV:(m + 1) * HV], ones[0:LB, 0:1], start=(j == 0), stop=(j == 1))
            mm.then_inc(S["prep_pe"], 1)
            pe.wait_ge(S["pool_const"], 5)
            pe.wait_ge(S["penalties"], 1)
            for a, t in enumerate((e_src, e_next)):
                for m in range(2):
                    for j in range(CH):
                        mm = ten.transpose(bank[2 + 2 * a + m][:, j * HV:(j + 1) * HV], t[:, m, j * P:(j + 1) * P], ident[0:HV, 0:HV])
            mm.then_inc(S["turned_rows"], 1)
            ten.transpose(bank[0][0:H, 256:256 + P], lane_h[:, :], ident[:, :]).then_inc(S["turned_rows"], 1)

            def fold(kind):
                pe.wait_ge(S["w_in_dma"], 16 * W_TOTAL[kind])
                mm = None
                if kind in ("in", "mid"):
                    for c0, c1, b in ((0, 512, bank[4]), (512, 768, bank[5])):
                        for a in range(2):
                            mm = ten.matmul(b[0:1, 0:c1 - c0], g_col[:, 1, a:a + 1], w_qkv[:, a, c0:c1], start=(a == 0), stop=(a == 1))
                if kind in ("mid", "last"):
                    for f in range(FFN // P):
                        for a in range(2):
                            mm = ten.matmul(bank[6][:, f:f + 1], w_up[:, a, f * P:(f + 1) * P], g_col[:, 3, a:a + 1], start=(a == 0), stop=(a == 1))
                mm.then_inc(S["w_pe"], 1)

            def dense(kind):
                s = PS[kind]
                n_turn, n_mm = count(kind, "turn") * BT, count(kind, "proj", "mlp", "qkv") * BT
                n_used = count(kind, "proj", "mlp") * BT
                n_mlp = FFN // P * 2
                FREE = [2, 3, 3, 4, 5]
                with pe.Fori(0, NBATCH) as it:
                    turn = used = kvc = 0
                    for stage in PASSES[kind]:
                        if stage == "turn":
                            for j in range(BT):
                                pe.wait_ge(s["tok"], it * n_turn + turn + j + 1)
                                if j >= 2:
                                    pe.wait_ge(s["evac"], it * n_turn + turn + j - 1)
                                for a in range(2):
                                    mm = ten.transpose(bank[j % 2][:, a * TN:(a + 1) * TN], tok[:, j, a * P:(a + 1) * P], ident[0:TN, 0:TN])
                                mm.then_inc(s["turned"], 1)
                            turn += BT
                        elif stage == "proj":
                            for j in range(BT):
                                pe.wait_ge(s["evac"], it * n_turn + turn - BT + j + 1)
                                pe.wait_ge(s["bank_free"], it * n_used + used + FREE[j])
                                o_ = bank[4 + j % 3][0:TN, 0:D]
                                for a in range(2):
                                    mm = ten.matmul(o_, tok_T[:, a, j * TN:(j + 1) * TN], w_sq[:, a, :], start=(a == 0), stop=(a == 1))
                                mm.then_inc(s["mm"], 1)
                            used += BT
                        elif stage == "mlp":
                            pe.wait_ge(s["evac"], it * n_turn + turn)
                            for n in range(n_mlp):
                                f, (c0, cn) = n // 2, MLP_CUT[n % 2]
                                if n >= 4:
                                    pe.wait_ge(s["gelu"], it * n_mlp + n - 3)
                                for a in range(2):
                                    mm = ten.matmul(bank[n % 4][:, 0:cn], w_up[:, a, f * P:(f + 1) * P], tok_T[:, a, c0:c0 + cn], start=(a == 0), stop=(a == 1))
                                mm.then_inc(s["up"], 1)
                            pe.wait_ge(s["gelu"], it * n_mlp + n_mlp)
                            for j in range(BT):
                                pe.wait_ge(s["bank_free"], it * n_used + used + FREE[j])
                                o_ = bank[4 + j % 3][0:TN, 0:D]
                                for f in range(FFN // P):
                                    mm = ten.matmul(o_, up_T[:, f, j * TN:(j + 1) * TN], w_down[:, f, :], start=(f == 0), stop=(f == FFN // P - 1))
                                mm.then_inc(s["mm"], 1)
                            used += BT
                        elif stage == "qkv":
                            for j in range(BT):
                                pe.wait_ge(s["evac"], it * n_turn + turn - BT + j + 1)
                                if j >= 2:
                                    pe.wait_ge(s["kvc"], it * BT + j - 1)
                                for c0, c1, b in ((0, 512, bank[4 + 2 * (j % 2)]), (512, 768, bank[5 + 2 * (j % 2)])):
                                    ten.matmul(b[0:TN, 0:c1 - c0], ones[0:1, 0:TN], row_qkv[:, c0:c1], start=True, stop=False)
                                    for a in range(2):
                                        mm = ten.matmul(b[0:TN, 0:c1 - c0], tok_T[:, a, j * TN:(j + 1) * TN], w_qkv[:, a, c0:c1], start=False, stop=(a == 1))
                                mm.then_inc(s["mm"], 1)

            def edges(layer):
                def queries(k, slot, t, pairs, first=False):
                    gk = k + layer * NG
                    if 0 in pairs:
                        pe.wait_ge(S["onehot"], gk + 1)
                        if not first:
                            pe.wait_ge(S["ss_copied"], gk)
                    for b in pairs:
                        if not (first and b < 2):
                            pe.wait_ge(S["q_used"], gk * (GC // 2) + b - 1)
                        for cc in (2 * b, 2 * b + 1):
                            hot = dt[:, slot, cc * P:(cc + 1) * P]
                            for p3 in range(3):
                                mm = ten.matmul(b_q[b % 2][:, cc % 2 * D:(cc % 2 + 1) * D], hot, qs[:, bass.ds(t[b // 2] * (3 * QC) + p3 * QC, D)], start=(p3 == 0), stop=(p3 == 2))
                            for p3 in range(3):
                                mm = ten.matmul(b_ss[:, cc * H:(cc + 1) * H], hot, qs[:, bass.ds(t[b // 2] * (3 * QC) + (p3 * QC + D), H)], start=(p3 == 0), stop=(p3 == 2))
                        mm.then_inc(S["q_ready"], 1)

                def turn_hot(k, slot, v, first):
                    if not (first and v == 0):
                        pe.wait_ge(S["hot_copied"], k * VG + (layer * NV + v))
                    for c4 in range(CH):
                        cc = v * CH + c4
                        mm = ten.transpose(hot_T[:, c4, 0:TN], dt[:, slot, cc * P:(cc + 1) * P], ident_b[0:TN, 0:TN])
                    mm.then_inc(S["hot_turned"], 1)

                def maxima(k, n):
                    pe.wait_ge(S["ch_dve"], (k + layer * NG) * CH_DVE + {1: C_SP, 2: C_ENDS, 3: C_XY}[n])
                    if n == 1:
                        mm = ten.transpose(b_ch[:, 0:P], sp_e[:, :, :].rearrange("p h c -> p (h c)"), ident[:, :])
                    elif n == 2:
                        mm = ten.matmul(b_ch[0:H, 128:160], lane_h[:, :], ends[:, :, :].rearrange("p a c -> p (a c)"), start=True, stop=True)
                    else:
                        mm = ten.matmul(b_ch[:, 160:192], lane_hT[:, :], flows, start=True, stop=True)
                    mm.then_inc(S["ch_pe"], 1)

                def sums(k, slot, v, first=False):
                    gk = k + layer * NG
                    pe.wait_ge(S["hot_copied"], gk * VG + v + 1)
                    pe.wait_ge(S["w_ready"], gk * VG + v + 1)
                    if not (first and v < 2):
                        pe.wait_ge(S["agg_used"], gk * VG + v - 1)
                    for c4 in range(CH):
                        cc = v * CH + c4
                        mm = ten.matmul(b_acc[v % 2][0:TN, 0:WCOL], dhot[:, cc, :], chunk[:, slot, cc, WOFF:ROW], start=(c4 == 0), stop=(c4 == CH - 1))
                    mm.then_inc(S["agg"], 1)

                def step(k, slot, turn, first, left):
                    gk = k + layer * NG
                    if not first:
                        sums(k - 1, (slot - 1) % SLOTS, VG - 1)
                    first = first and layer == 0
                    if left:
                        t = tiles_of(mybir.EngineType.PE, (k + 1) * VG + 1, VG if left == 2 else VG - 1)
                        t1, t2 = (None,) + t[:VG - 1], t[VG - 1:]

                    def ahead(b):
                        if left:
                            queries(k + 1, (slot + 1) % SLOTS, t1, (b,))

                    turn_hot(k, slot, 0, first)
                    ahead(2)
                    pe.wait_ge(S["ch_dve"], gk * CH_DVE + C_MU)
                    ten.matmul(b_ch[0:TN, 192:192 + H], delta[:, :], r_diag[:, :], start=True, stop=True).then_inc(S["ch_pe"], 1)
                    ten.transpose(b_ch[:, 256:256 + P], f_lane[:, :], ident[:, :]).then_inc(S["ch_pe"], 1)
                    turn_hot(k, slot, 1, False)
                    ahead(3)
                    turn_hot(k, slot, 2, False)
                    ahead(4)
                    turn_hot(k, slot, 3, False)
                    ahead(5)
                    pe.wait_ge(S["ch_dve"], gk * CH_DVE + C_SELF)
                    sums(k, slot, 0, first)
                    ahead(6)
                    sums(k, slot, 1, first)
                    ahead(7)
                    sums(k, slot, 2)
                    if left == 2:
                        queries(k + 2, (slot + 2) % SLOTS, t2, (0,))
                    if left:
                        maxima(k + 1, 1)
                    if left == 2:
                        queries(k + 2, (slot + 2) % SLOTS, t2, (1,))
                    if left:
                        maxima(k + 1, 2)
                        maxima(k + 1, 3)
                    else:
                        sums(k, slot, VG - 1)

                queries(0, 0, tiles_of(mybir.EngineType.PE, 0, VG), range(GC // 2), layer == 0)
                maxima(0, 1)
                queries(1, 1, tiles_of(mybir.EngineType.PE, VG, 1), (0, 1))
                maxima(0, 2)
                maxima(0, 3)
                in_steps(pe, step)

            pe.wait_ge(S["prep_done"], 1)
            fold("in")
            pe.wait_ge(S["w_dve"], 1)
            dense("in")
            pe.wait_ge(S["pass_over"], 1)
            edges(0)
            fold("mid")
            pe.wait_ge(S["w_dve"], 2)
            dense("mid")
            pe.wait_ge(S["pass_over"], 2)
            edges(1)
            fold("last")
            pe.wait_ge(S["w_dve"], 3)
            dense("last")
            pe.wait_ge(S["pass_over"], 3)
            for a in range(2):
                for t in range(NT):
                    mm = ten.matmul(bank[0][:, a:a + 1], acc_t[:, t, a * P:(a + 1) * P], ones[0:TN, 0:1], start=(t == 0), stop=(t == NT - 1))
            mm.then_inc(S["route_pe"], 1)
            pe.wait_ge(S["route_dma"], 64)
            pe.wait_ge(S["route"], R_MEAN)
            for a in range(2):
                mm = ten.matmul(bank[1][0:1, 0:NEXP], small[:, a:a + 1], w_qkv[:, 0, a * NEXP:(a + 1) * NEXP], start=(a == 0), stop=(a == 1))
            mm.then_inc(S["route_pe"], 1)
            ten.matmul(bank[7][0:TN, :], ones[0:1, 0:TN], row_qkv[:, D:3 * D], start=True, stop=True).then_inc(S["route_pe"], 1)
            pe.wait_ge(S["route"], R_TOPW)
            ten.matmul(bank[2][:, 0:TOPK], ones[0:1, :], small[0:1, 62:64], start=True, stop=True).then_inc(S["route_pe"], 1)
            pe.wait_ge(S["route"], R_WEIGHTS)
            dense("moe")

        @block.scalar
        def _(act):
            def dense(kind):
                s = PS[kind]
                n_turn, n_mm = count(kind, "turn") * BT, count(kind, "proj", "mlp", "qkv") * BT
                n_mlp = FFN // P * 2
                with act.Fori(0, NBATCH) as it:
                    turn = mm = 0
                    for stage in PASSES[kind]:
                        if stage == "turn":
                            for j in range(BT):
                                act.wait_ge(s["turned"], it * n_turn + turn + j + 1)
                                sca.activation(tok_T[:, :, j * TN:(j + 1) * TN], bank[j % 2][:, 0:2 * TN].rearrange("p (a n) -> p a n", a=2), ACT.Copy).then_inc(s["evac"], 1)
                            turn += BT
                        elif stage == "mlp":
                            for n in range(n_mlp):
                                f, (c0, cn) = n // 2, MLP_CUT[n % 2]
                                act.wait_ge(s["up"], it * n_mlp + n + 1)
                                sca.activation(up_T[:, f, c0:c0 + cn], bank[n % 4][:, 0:cn], ACT.Gelu, bias=up_bias[:, f:f + 1]).then_inc(s["gelu"], 1)
                        elif stage == "qkv":
                            act.wait_ge(s["out_free"], it + 1)
                            for j in range(BT):
                                act.wait_ge(s["mm"], it * n_mm + mm + j + 1)
                                b0, b1 = bank[4 + 2 * (j % 2)], bank[5 + 2 * (j % 2)]
                                sca.activation(qf[:, j, 0:D], b0[0:TN, 0:D], ACT.Copy)
                                sca.activation(kv_b[:, j, 0:D], b0[0:TN, D:2 * D], ACT.Copy)
                                sca.activation(kv_b[:, j, D:ROW].rearrange("p (d h) -> p h d", h=H),
                                               b1[0:TN, 0:D].rearrange("p (h d) -> p h d", h=H), ACT.Copy).then_inc(s["kvc"], 1)
                        if stage in ("proj", "mlp"):
                            mm += BT

            def edges(layer):
                def copy_self(k, slot):
                    act.wait_ge(S["q_ready"], (k + layer * NG) * (GC // 2) + GC // 2)
                    sca.activation(ss_e[:, slot, :, :].rearrange("p h c -> p c h"), b_ss[:, 0:P].rearrange("p (c h) -> p c h", h=H), ACT.Copy).then_inc(S["ss_copied"], 1)

                def step(k, slot, turn, first, left):
                    gk = k + layer * NG

                    def copy_hot(v):
                        act.wait_ge(S["hot_turned"], gk * VG + v + 1)
                        sca.activation(dhot[:, v * CH:(v + 1) * CH, :], hot_T[:, :, 0:TN], ACT.Copy).then_inc(S["hot_copied"], 1)
                    c = S["ch_act"]
                    act.wait_ge(S["ch_dve"], gk * CH_DVE + C_DM)
                    sca.activation(m_new[:, 2:3], m_new[:, 1:2], ACT.Exp).then_inc(c, 1)
                    copy_hot(0)
                    copy_hot(1)
                    act.wait_ge(S["ch_dve"], gk * CH_DVE + C_ARG)
                    a0 = arg[:, 0, :].rearrange("p (h c) -> p c h", h=H)
                    if not (first and layer == 0):
                        act.wait_ge(S["w_ready"], gk * VG)
                    sca.activation(b_p[:, 0:P].rearrange("p (c h) -> p c h", h=H), a0, ACT.Exp).then_inc(c, 1)
                    sca.activation(chunk[:, slot, :, WOFF:WOFF + H], a0, ACT.Exp).then_inc(c, 1)
                    sca.activation(own_e[:, :], arg[:, 1, :], ACT.Exp).then_inc(c, 1)
                    copy_hot(2)
                    copy_hot(3)
                    if left == 2:
                        nn = (slot + 2) % SLOTS
                        act.wait_ge(S[f"tab{nn}"], turn(2) * ((H + 1) * 16) + (layer * USES[nn] + 1) * (H + 1) * 16)
                        sca.activation(dt[:, nn, :], dt[:, nn, :], ACT.Abs, bias=minus_p[0:TN, :]).then_inc(S["dl_abs"], 1)
                        act.wait_ge(S["dl_abs"], k + (layer * (NG - 2) + 1))
                        sca.activation(dt[:, nn, :], dt[:, nn, :], ACT.Relu, bias=ones[0:TN, 0:1], scale=-1.0).then_inc(S["onehot"], 1)
                    if left:
                        copy_self(k + 1, (slot + 1) % SLOTS)

                copy_self(0, 0)
                in_steps(act, step)

            dense("in")
            edges(0)
            dense("mid")
            edges(1)
            dense("last")
            for n, (at, i_, w, b_) in enumerate(((R_E1, 8, NEXP, 58), (R_E2, 16, NEXP, 58), (R_E3, 60, TOPK, 58))):
                act.wait_ge(S["route"], at)
                sca.activation(small[0:1, i_:i_ + w], small[0:1, i_:i_ + w], ACT.Exp, bias=small[0:1, b_:b_ + 1]).then_inc(S["route_act"], 1)
            dense("moe")

        @block.vector
        def _(v):
            tt, ts = vec.tensor_tensor, vec.tensor_scalar
            vec.memset(fill_m1.bitcast(I32), -1).then_inc(S["pads"], 1)
            vec.memset(fill_0.bitcast(I32), 0).then_inc(S["pads"], 1)
            vec.memset(small[0:1, 10:11], -2.0).then_inc(S["pads"], 1)
            st = Steps(S["prep"])

            def do(ins):
                st.did(ins)
                st.sync(v)

            vec.memset(half[:, :], -0.5)
            st.did(vec.memset(ones[:, :], 1.0))
            vec.memset(g_run[:, :], -BIG)
            do(vec.memset(h_run[:, :], -BIG))
            v.wait_ge(S["pool_const"], 5)
            st.did(ts(minus_p[:, :], iota_p[:, :], -1.0, None, ALU.mult))
            do(vec.tensor_copy(ident_b[:, :], ident[:, :]))
            by_lane = ident[:, :].rearrange("p (h c) -> p h c", h=H)
            do(vec.tensor_reduce(lane_h[:, :], by_lane, AX.X, ALU.add))
            for a in range(2):
                do(vec.tensor_reduce(lane_c[:, a, :], by_lane.rearrange("p h c -> p c h"), AX.X, ALU.add))
            v.wait_ge(S["last_in"], 48)
            do(vec.tensor_copy(small[0:LB, 2:4], small[0:LB, 0:2].bitcast(I32)))
            do(ts(small[:, 20:20 + NT - 1], iota_f[:, 1:NT], float(TN), None, ALU.mult))
            for j in range(2):
                do(ts(e_src[0:LB, 0, 0:NT - 1], small[0:LB, 20:20 + NT - 1], small[0:LB, 2 + j:3 + j], None, ALU.is_le))
                do(vec.tensor_reduce(small[0:LB, 4 + j:5 + j], e_src[0:LB, 0, 0:NT - 1], AX.X, ALU.add))
                do(ts(small[0:LB, 6 + j:7 + j], small[0:LB, 4 + j:5 + j], iota_p[0:LB, :], float(j * LB), ALU.add, ALU.add))
                do(ts(ind[:, j, :], iota_v[0:LB, :], small[0:LB, 6 + j:7 + j], None, ALU.is_gt))
            assert st.n == PREP_IND, st.n
            v.wait_ge(S["prep_pe"], 1)
            do(vec.tensor_copy(small[0:HV, 16:18], bank[1][0:HV, 0:2]))
            vec.tensor_copy(small[0:HV, 12:14].bitcast(U32), small[0:HV, 16:18]).then_inc(S["blocks"], 1)
            for m in range(2):
                do(ts(small[0:HV, 18 + m:19 + m], small[0:HV, 16 + m:17 + m], iota_p[0:HV, :], -1.0, ALU.subtract, ALU.mult))
                do(ts(small[0:HV, 18 + m:19 + m], small[0:HV, 18 + m:19 + m], float(m * HV), float(NT - 1), ALU.add, ALU.min))
                do(ts(small[0:HV, 18 + m:19 + m], small[0:HV, 18 + m:19 + m], float(TN), None, ALU.mult))
            do(tt(iota_v[0:1, :], iota_v[0:1, :], bank[0][0:1, 0:NV], ALU.subtract))
            do(ts(iota_v[0:1, :], iota_v[0:1, :], float(NT - 1), None, ALU.min))
            do(vec.tensor_copy(t_row[:, :], iota_v[0:1, :]))
            v.wait_ge(S["rows_in"], 64)
            st.did(vec.tensor_copy(e_src, e_i[:, 0, :, :].bitcast(I32)))
            do(vec.tensor_copy(e_dst, e_i[:, 1, :, :].bitcast(I32)))
            for m in range(2):
                do(ts(e_dl[:, m, :], e_dst[:, m, :], small[0:HV, 18 + m:19 + m], None, ALU.subtract))
            do(ts(e_val, e_dl, 0.0, None, ALU.is_ge))
            do(ts(e_key, e_dl, float(TN), None, ALU.is_lt))
            do(tt(e_val, e_val, e_key, ALU.mult))
            for t, s_ in ((e_key, e_dst), (e_dl, e_dl)):
                do(vec.scalar_tensor_tensor(out=t, in0=s_, scalar=1.0, in1=e_val, op0=ALU.add, op1=ALU.mult))
                do(ts(t, t, -1.0, None, ALU.add))
            vec.tensor_copy(b_dl, e_dl).then_inc(S["keys"], 1)
            v.wait_ge(S["lines_in"], 16 * (2 + 3 * H))
            st.did(tt(e_prev, e_key, e_prev, ALU.is_equal))
            do(tt(e_next, e_key, e_next, ALU.is_equal))
            st.did(ts(b_pf, e_prev, BIG, -BIG, ALU.mult, ALU.add))
            do(ts(b_pb, e_next, BIG, -BIG, ALU.mult, ALU.add))
            do(ts(e_next, e_next, -1.0, 1.0, ALU.mult, ALU.add))
            tt(e_next, e_next, e_val, ALU.mult).then_inc(S["penalties"], 1)
            v.wait_ge(S["turned_rows"], 2)
            for a, (t, dst) in enumerate(((e_src, src_ix), (e_next, last_col))):
                for m in range(2):
                    st.did(vec.tensor_copy(dst[:, :].rearrange("p (v j) -> p j v", j=CH)[:, :, m * HV:(m + 1) * HV],
                                           bank[2 + 2 * a + m][:, 0:CH * HV].rearrange("p (j v) -> p j v", j=CH)))
            st.did(vec.tensor_copy(lane_hT[:, :], bank[0][0:H, 256:256 + P]))
            v.wait_ge(S["lines_in"], 16 * (2 + 4 * H))
            do(tt(k_first, k_first, k_last, ALU.is_equal))
            do(ts(k_first, k_first, BIG, -BIG, ALU.mult, ALU.add))
            at_group = kp[:, 0:NC].rearrange("p (g c) -> p g c", c=GC)[:, :, 0]
            do(ts(dl0[:, :], at_group, 0.0, None, ALU.is_equal))
            do(ts(k_last[:, 0:NG], a_f[:, 0:NG], 1.0, None, ALU.add))
            do(tt(dl0[:, :], dl0[:, :], k_last[:, 0:NG], ALU.mult))
            do(ts(dl0[:, :], dl0[:, :], -1.0, None, ALU.add))
            do(tt(a_f[:, :], k_first, kp[:, 0:NC], ALU.min))
            do(tt(a_b[:, :].rearrange("p (g c) -> p g c", c=GC)[:, :, ::-1], k_first.rearrange("p (g c) -> p g c", c=GC),
                  kp[:, 1:NC + 1].rearrange("p (g c) -> p g c", c=GC), ALU.min))
            v.sem_inc(S["prep_done"], 1)

            def fold(kind):
                w = S["w_step"]
                n0 = {"in": 0, "mid": W_STEPS["in"], "last": W_STEPS["in"] + W_STEPS["mid"]}[kind]
                ws = Steps(w, n0)
                v.wait_ge(S["w_pe"], PASS_NO[kind] + 1)
                sc = DH ** -0.5
                if kind in ("in", "mid"):
                    ws.did(tt(row_qkv[:, 0:512], row_qkv[:, 0:512], bank[4][0:1, 0:512], ALU.add))
                    ws.did(tt(row_qkv[:, 512:768], row_qkv[:, 512:768], bank[5][0:1, 0:256], ALU.add))
                    for a in range(2):
                        ws.did(ts(w_qkv[:, a, 0:D], w_qkv[:, a, 0:D], g_col[:, 0, a:a + 1], sc, ALU.mult, ALU.mult))
                        ws.did(ts(w_qkv[:, a, D:3 * D], w_qkv[:, a, D:3 * D], g_col[:, 0, a:a + 1], None, ALU.mult))
                    ws.sync(v)
                    ws.did(ts(row_qkv[:, 0:D], row_qkv[:, 0:D], sc, None, ALU.mult))
                if kind in ("mid", "last"):
                    ws.did(tt(up_bias[:, :], up_bias[:, :], bank[6][:, 0:FFN // P], ALU.add))
                    for a in range(2):
                        ws.did(ts(w_up[:, a, :], w_up[:, a, :], g_col[:, 2, a:a + 1], None, ALU.mult))
                ws.sync(v)
                assert ws.n == W_STEPS[kind], ws.n
                v.sem_inc(S["w_dve"], 1)

            def dense(kind):
                s = PS[kind]
                n_tok, n_mm = count(kind, "turn") * BT, count(kind, "proj", "mlp", "qkv") * BT
                n_used = count(kind, "proj", "mlp") * BT
                n_norm = count(kind, "norm")
                n_x = {"in": 16, "mid": 32, "last": 32, "moe": 16}[kind]
                def tiles_of_batch(it):
                    return acc[:, bass.ds(it * (BT * WCOL), BT * WCOL)].rearrange("p (j w) -> p j w", j=BT)

                def norm(it, no, src, dst, ready, st, begun=False):
                    if not begun:
                        for j in range(BT):
                            st.did(vec.bn_stats(stat[:, j, :], src[:, j, :]))
                    hold(v, st.sem, st.base + st.n, S["dve_passed"])
                    for j in range(BT):
                        vec.bn_aggr(mv[:, j, :], stat[:, j, :]).then_inc(s["stat"], 1)
                    v.wait_ge(s["stat"], it * (n_norm * BT) + (no + 1) * BT)
                    v.wait_ge(s["rs_ready"], it * n_norm + no + 1)
                    for j in range(BT):
                        ins = ts(dst[:, j, 0:D], src[:, j, :], mv[:, j, 0:1], rs[:, j:j + 1], ALU.subtract, ALU.mult)
                        if ready is None:
                            st.did(ins)
                        else:
                            ins.then_inc(ready, 1)

                def bias(t, b):
                    return tt(t, t, b.rearrange("p (a c) -> p a c", a=1).to_broadcast([TN, BT, D]), ALU.add)

                def head(it):
                    st = Steps(s["head"], it * H_STEPS[kind])
                    if kind != "moe":
                        v.wait_ge(s["x_in"], it * n_x + n_x)
                    tiles = tiles_of_batch(it)
                    if kind == "in":
                        norm(it, 0, x_in, tok, s["tok"], st)
                    elif kind == "moe":
                        for j in range(BT):
                            vec.tensor_copy(tok[:, j, :], tiles[:, j, 0:D]).then_inc(s["tok"], 1)
                        v.wait_ge(s["tok"], it * n_tok + BT)
                        st.did(bias(tiles[:, :, 0:D], bias_down))
                    else:
                        z, own = tiles[:, :, 0:H], tiles[:, :, H:2 * H]
                        val = tiles[:, :, 2 * H:WCOL].rearrange("p j (d h) -> p j d h", h=H)
                        den = small[0:TN, 0:BT * H].rearrange("p (j h) -> p j h", h=H)
                        mine = own_v.rearrange("p j (d h) -> p j d h", h=H)
                        st.did(tt(den, z, own, ALU.add)); st.sync(v)
                        st.did(ts(den, den, 1e-30, None, ALU.max)); st.sync(v)
                        st.did(vec.reciprocal(den, den))
                        st.did(tt(mine, mine, own.rearrange("p j (a h) -> p j a h", a=1).to_broadcast([TN, BT, DH, H]), ALU.mult)); st.sync(v)
                        st.did(tt(mine, mine, val, ALU.add)); st.sync(v)
                        for j in range(BT):
                            tt(tok[:, j, :].rearrange("p (h d) -> p d h", h=H), own_v[:, j, :].rearrange("p (d h) -> p d h", h=H),
                               den[:, j:j + 1, :].to_broadcast([TN, DH, H]), ALU.mult).then_inc(s["tok"], 1)
                        st.did(bias(h_n[kind], bias_sq))
                    assert st.n == H_STEPS[kind], (kind, st.n)

                def batch(it, last):
                    st = Steps(s["dve"], it * D_STEPS[kind])
                    mm = used = 0
                    norms, turns = int(kind == "in"), 1
                    tiles = tiles_of_batch(it)
                    stages = PASSES[kind][1:]

                    def next_head():
                        if not last:
                            v.wait_ge(s["evac"], it * n_tok + n_tok)
                            head(it + 1)
                    v.wait_ge(s["out_free"], it + 1)
                    if kind == "moe":
                        next_head()
                    for k, stage in enumerate(stages):
                        if stage in ("proj", "mlp"):
                            if k == 1 and kind != "in":
                                v.wait_ge(s["head"], it * H_STEPS[kind] + H_STEPS[kind])
                            x = tiles[:, :, 0:D] if kind == "moe" else h_b
                            normed_next = stages[k + 1] == "norm"

                            def stats(j):
                                if normed_next:
                                    hold(v, s["bank_free"], it * n_used + used + j + 4, S["dve_passed"])
                                    st.did(vec.bn_stats(stat[:, j, :], x[:, j, :]))
                            for j in range(BT):
                                v.wait_ge(s["mm"], it * n_mm + mm + j + 1)
                                r = bank[4 + j % 3][0:TN, 0:D]
                                if kind == "in":
                                    ins = tt(h_b[:, j, :], r, bias_sq, ALU.add)
                                elif kind == "moe":
                                    ins = tt(tiles[:, j, 0:D], tiles[:, j, 0:D], r, ALU.add)
                                elif stage == "proj":
                                    ins = tt(h_b[:, j, :], h_n[kind][:, j, :], r, ALU.add)
                                else:
                                    ins = tt(h_b[:, j, :], h_b[:, j, :], r, ALU.add)
                                ins.then_inc(s["bank_free"], 1)
                                if j:
                                    stats(j - 1)
                            stats(BT - 1)
                            mm += BT
                            used += BT
                            hold(v, s["bank_free"], it * n_used + used + 3, S["dve_passed"])
                        elif stage == "norm":
                            feeds = k + 1 < len(stages)
                            src = tiles[:, :, 0:D] if kind == "moe" else h_b
                            dst = tok if feeds else h_b if kind == "moe" else tiles
                            norm(it, norms, src, dst, s["tok"] if feeds else None, st, begun=True)
                            norms += 1
                            if feeds:
                                turns += 1
                                if "mlp" in stages[k:]:
                                    v.wait_ge(s["tok"], it * n_tok + turns * BT)
                                    st.did(bias(h_b, bias_down)); st.sync(v)
                                    if kind == "last":
                                        v.wait_ge(s["x_late"], it * 16 + 16)
                                        st.did(tt(h_b[:, :, :], h_b[:, :, :], x_in[:, :, :], ALU.add)); st.sync(v)
                                if turns == n_tok // BT:
                                    next_head()
                            else:
                                st.sync(v)
                        elif stage == "qkv":
                            for j in range(BT):
                                v.wait_ge(s["kvc"], it * BT + j + 1)
                                st.did(tt(qr[:, j, 0:D], qf[:, j, 0:D], kv_b[:, j, 0:D], ALU.mult)); st.sync(v)
                                st.did(vec.tensor_reduce(qf[:, j, D:QC], qr[:, j, 0:D].rearrange("p (h d) -> p h d", h=H), AX.X, ALU.add))
                            st.sync(v)
                            q3 = qs[:, bass.ds(it * (BT * 3 * QC), BT * 3 * QC)].rearrange("p (j r c) -> p j r c", j=BT, r=3)
                            st.did(vec.tensor_copy(q3[:, :, 0, :], qf)); st.sync(v)
                            st.did(tt(qr, qf, q3[:, :, 0, :], ALU.subtract)); st.sync(v)
                            st.did(vec.tensor_copy(q3[:, :, 1, :], qr)); st.sync(v)
                            st.did(tt(q3[:, :, 2, :], qr, q3[:, :, 1, :], ALU.subtract)); st.sync(v)
                    if kind == "moe":
                        v.wait_ge(s["x_in"], it * n_x + n_x)
                        gain, shift = bank[7][0:TN, 0:D], bank[7][0:TN, D:2 * D]
                        for x, op in ((gain, ALU.mult), (shift, ALU.add)):
                            for j in range(BT):
                                st.did(tt(h_b[:, j, :], h_b[:, j, :], x, op))
                            st.sync(v)
                        st.did(tt(h_b[:, :, :], h_b[:, :, :], h_n[kind][:, :, :], ALU.add)); st.sync(v)
                    assert st.n == D_STEPS[kind], (kind, st.n)
                    v.sem_inc(s["done"], 1)

                v.sem_inc(s["bank_free"], 3)
                head(0)
                with v.Fori(0, NBATCH - 1) as it:
                    batch(it, False)
                batch(NBATCH - 1, True)
                v.sem_inc(S["pass_over"], 1)

            def edges(layer):
                es = Steps(S["edge_step"], layer * 2)

                def onehot(k, slot, turn):
                    v.wait_ge(S[f"tab{slot}"], turn * ((H + 1) * 16) + (layer * USES[slot] + 1) * (H + 1) * 16)
                    ts(dt[:, slot, :], dt[:, slot, :], iota_p[0:TN, :], None, ALU.is_equal).then_inc(S["onehot"], 1)

                def scores(k, slot, turn, b):
                    gk = k + layer * NG
                    if b % 2 == 0:
                        v.wait_ge(gath[slot][b // 2], turn * (CH * 16) + (layer * USES[slot] + 1) * CH * 16)
                    v.wait_ge(S["q_ready"], gk * (GC // 2) + b + 1)
                    pair = chunk[:, slot, 2 * b:2 * b + 2, 0:D]
                    tt(pair, pair, b_q[b % 2][:, :].rearrange("p (c w) -> p c w", c=2), ALU.mult).then_inc(S["q_used"], 1)

                def sum_scores(k, slot, b):
                    gk = k + layer * NG
                    v.wait_ge(S["q_used"], gk * (GC // 2) + b + 1)
                    c0 = 2 * b - 2
                    vec.tensor_reduce(s_e[:, slot, :, c0:c0 + CH].rearrange("p h c -> p c h"),
                                      chunk[:, slot, c0:c0 + CH, 0:D].rearrange("p c (h d) -> p c h d", h=H), AX.X, ALU.add).then_inc(S["score"], 1)

                def pe(k, n):
                    v.wait_ge(S["ch_pe"], (k + layer * NG) * CH_PE + n)

                def scores_max(k, slot, st):
                    v.wait_ge(S["score"], (k + layer * NG) * VG + VG)
                    v.wait_ge(S["ss_copied"], k + (layer * NG + 1))
                    st.did(tt(sp_e[:, :, :], s_e[:, slot, :, :], ss_e[:, slot, :, :], ALU.max))
                    assert st.n == C_SP

                def in_chunks(k, slot, st):
                    pf, pb, sT = pens[:, slot, 0, :], pens[:, slot, 1, :], b_ch[:, 0:P]
                    pe(k, 1)
                    st.did(vec.tensor_tensor_scan(f_lane[:, 1:P], pf[:, 1:P], sT[:, 1:P], sT[:, 0:1], ALU.add, ALU.max))
                    st.did(vec.tensor_tensor_scan(b_lane[:, ::-1][:, 1:P], pb[:, ::-1][:, 1:P], sT[:, ::-1][:, 1:P], sT[:, P - 1:P], ALU.add, ALU.max))
                    st.did(vec.tensor_copy(g_run[:, 0:1], g_run[:, GC:GC + 1]))
                    st.sync(v, st.n - 1)
                    st.did(ts(ends[:, 0, :], lane_c[:, 0, :], f_lane[:, P - 1:P], None, ALU.mult))
                    st.did(ts(ends[:, 1, :], lane_c[:, 0, :], b_lane[:, 0:1], None, ALU.mult))
                    assert st.n == C_ENDS

                def over_chunks(k, st):
                    st.sync(v)
                    pe(k, 2)
                    c0 = k * GC
                    st.did(vec.tensor_tensor_scan(g_run[:, 1:GC + 1], a_f[:, bass.ds(c0, GC)], b_ch[0:H, 128:128 + GC], g_run[:, 0:1], ALU.add, ALU.max))
                    st.did(vec.tensor_tensor_scan(h_run[:, 0:GC][:, ::-1], a_b[:, bass.ds(c0, GC)], b_ch[0:H, 128 + GC:128 + 2 * GC][:, ::-1], -BIG, ALU.add, ALU.max))
                    assert st.n == C_XY
                    st.sync(v)
                    st.did(tt(m_new[:, 0:1], h_run[:, 0:1], g_run[:, 0:1], ALU.max))
                    st.sync(v)
                    st.did(tt(m_new[:, 1:2], g_run[:, 0:1], m_new[:, 0:1], ALU.subtract))
                    assert st.n == C_DM

                def step(k, slot, turn, first, left):
                    gk = k + layer * NG
                    nxt = (slot + 1) % SLOTS
                    st = Steps(S["ch_dve"], gk * CH_DVE)
                    st.n = C_DM
                    head = Steps(S["ch_dve"], (gk + 1) * CH_DVE)
                    def do(ins):
                        st.did(ins)
                        st.sync(v)

                    def ahead(b):
                        if left:
                            scores(k + 1, nxt, turn(1), b)

                    def ahead_sum(b):
                        if left:
                            sum_scores(k + 1, nxt, b)

                    def weigh(q):
                        val = chunk[:, slot, q * CH:(q + 1) * CH, D:ROW].rearrange("p c (d h) -> p c d h", h=H)
                        w = b_p[:, q * CH * H:(q + 1) * CH * H].rearrange("p (c a h) -> p c a h", c=CH, a=1).to_broadcast([P, CH, DH, H])
                        tt(val, val, w, ALU.mult).then_inc(S["w_ready"], 1)

                    def add(q, t):
                        v.wait_ge(S["agg"], gk * VG + q + 1)
                        if q == 0:
                            st.sync(v)
                        else:
                            v.wait_ge(S["agg_used"], gk * VG + q)
                        at = acc[:, bass.ds(t[max(q, 0)] * WCOL, WCOL)]
                        tt(at, at, b_acc[q % 2][0:TN, 0:WCOL], ALU.add).then_inc(S["agg_used"], 1)

                    pf, pb, sT = pens[:, slot, 0, :], pens[:, slot, 1, :], b_ch[:, 0:P]
                    st.did(ts(delta[:, :], iota_f[0:H, 0:TN], dl0[:, bass.ds(k, 1)], None, ALU.is_equal))
                    ahead(0)
                    pe(k, 3)
                    st.did(tt(xy_m[:, :, :], lane_c[:, :, :], b_ch[:, 160:192].rearrange("p (a c) -> p a c", a=2), ALU.mult))
                    v.wait_ge(S["ch_act"], gk * CH_ACT + 1)
                    st.did(ts(m_new[:, 3:4], m_new[:, 2:3], -1.0, None, ALU.add))
                    st.sync(v, st.n - 1)
                    st.did(vec.tensor_reduce(xy_l[:, :], xy_m[:, :, :], AX.X, ALU.add))
                    st.sync(v, st.n - 1)
                    st.did(ts(r_diag[:, :], ident[0:H, 0:H], m_new[:, 3:4], None, ALU.mult))
                    st.sync(v, st.n - 1)
                    st.did(vec.tensor_tensor_scan(f_lane[:, :], pf, sT, xy_l[:, 0:1], ALU.add, ALU.max))
                    do(vec.tensor_tensor_scan(b_lane[:, ::-1], pb[:, ::-1], sT[:, ::-1], xy_l[:, 1:2], ALU.add, ALU.max))
                    st.did(tt(f_lane[:, :], f_lane[:, :], b_lane[:, :], ALU.max))
                    assert st.n == C_MU
                    ahead(1)
                    ahead_sum(1)
                    t = tiles_of(mybir.EngineType.DVE, k * VG, VG) if first else tiles_of(mybir.EngineType.DVE, k * VG - 1, VG + 1)
                    if not first:
                        add(-1, t)
                        t = t[1:]
                    pe(k, 5)
                    st.did(ts(a_fac[:, :], b_ch[0:TN, 192:192 + H], 1.0, None, ALU.add))
                    mu = b_ch[:, 256:256 + P]
                    st.did(tt(arg[:, 0, :], s_e[:, slot, :, :].rearrange("p h c -> p (h c)"), mu, ALU.subtract))
                    st.did(tt(arg[:, 1, :], ss_e[:, slot, :, :].rearrange("p h c -> p (h c)"), mu, ALU.subtract))
                    assert st.n == C_ARG
                    st.sync(v, C_ARG - 2)
                    if not first:
                        v.wait_ge(S["agg_used"], gk * VG)
                    at = acc[:, bass.ds(t[0] * WCOL, WCOL)].rearrange("p (x h) -> p x h", h=H)
                    st.did(tt(at, at, a_fac[:, :].rearrange("p (a h) -> p a h", a=1).to_broadcast([TN, WCOL // H, H]), ALU.mult))
                    ahead(2)
                    ahead(3)
                    v.wait_ge(S["ch_act"], gk * CH_ACT + CH_ACT)
                    st.did(tt(chunk[:, slot, :, WOFF + H:WOFF + 2 * H], own_e[:, :].rearrange("p (h c) -> p c h", h=H),
                              last_col[:, bass.ds(k * GC, GC)].rearrange("p (c a) -> p c a", a=1).to_broadcast([P, GC, H]), ALU.mult))
                    assert st.n == C_SELF == CH_DVE
                    ahead_sum(3)
                    weigh(0)
                    ahead(4)
                    weigh(1)
                    ahead(5)
                    add(0, t)
                    ahead_sum(5)
                    weigh(2)
                    ahead(6)
                    add(1, t)
                    weigh(3)
                    ahead(7)
                    ahead_sum(7)
                    if left:
                        scores_max(k + 1, nxt, head)
                    add(2, t)
                    if left:
                        in_chunks(k + 1, nxt, head)
                    if left:
                        over_chunks(k + 1, head)
                    else:
                        add(3, t)
                        v.wait_ge(S["agg_used"], gk * VG + VG)

                onehot(0, 0, 0)
                onehot(1, 1, 0)
                es.did(vec.memset(acc[:, :], 0.0))
                es.did(vec.memset(g_run[:, GC:GC + 1], -BIG))
                es.sync(v)
                for b in range(GC // 2):
                    scores(0, 0, 0, b)
                    if b % 2:
                        sum_scores(0, 0, b)
                head = Steps(S["ch_dve"], layer * NG * CH_DVE)
                scores_max(0, 0, head)
                in_chunks(0, 0, head)
                over_chunks(0, head)
                in_steps(v, step)
                v.sem_inc(S["edges_over"], 1)

            fold("in")
            dense("in")
            edges(0)
            fold("mid")
            dense("mid")
            edges(1)
            fold("last")
            dense("last")

            st = Steps(S["route"])

            def col(c, n=NEXP):
                return small[0:1, c:c + n]

            def softmax_top(x, e_no, n=NEXP):
                do(vec.tensor_reduce(col(58, 1), col(x, n), AX.X, ALU.max))
                do(ts(col(58, 1), col(58, 1), -1.0, None, ALU.mult))
                assert st.n == (R_E1, R_E2, R_E3)[e_no], (e_no, st.n)
                v.wait_ge(S["route_act"], e_no + 1)
                do(vec.tensor_reduce(col(59, 1), col(x, n), AX.X, ALU.add))
                do(vec.reciprocal(col(59, 1), col(59, 1)))

            v.wait_ge(S["route_pe"], 1)
            do(ts(small[:, 0:2], bank[0][:, 0:2], 1.0 / N, None, ALU.mult))
            assert st.n == R_MEAN
            v.wait_ge(S["route_pe"], 2)
            do(tt(col(8), bank[1][0:1, 0:NEXP], row_qkv[:, 0:NEXP], ALU.add))
            softmax_top(8, 0)
            do(ts(col(8), col(8), col(59, 1), None, ALU.mult))
            do(ts(col(16), col(8), float(N), None, ALU.mult))
            do(ts(col(24), col(16), CAPACITY, None, ALU.is_gt))
            do(ts(col(16), col(16), CAPACITY, None, ALU.max))
            do(vec.reciprocal(col(16), col(16)))
            do(ts(col(16), col(16), CAPACITY, -1.0, ALU.mult, ALU.add))
            do(tt(col(16), col(16), col(24), ALU.mult))
            do(ts(col(16), col(16), 1.0, None, ALU.add))
            do(tt(col(16), col(16), col(8), ALU.mult))
            softmax_top(16, 1)
            do(ts(col(16), col(16), col(59, 1), None, ALU.mult))
            for i in range(TOPK):
                do(vec.tensor_reduce(col(60 + i, 1), col(16), AX.X, ALU.max))
                do(ts(col(24), col(16), col(60 + i, 1), None, ALU.is_equal))
                do(ts(col(32), col(24), -99.0, 99.0, ALU.mult, ALU.add))
                do(tt(col(24), col(24), iota_f[0:1, 0:NEXP], ALU.mult))
                do(tt(col(32), col(32), col(24), ALU.add))
                do(vec.tensor_reduce(col(40 + i, 1), col(32), AX.X, ALU.min))
                do(ts(col(24), iota_f[0:1, 0:NEXP], col(40 + i, 1), -10.0, ALU.is_equal, ALU.mult))
                do(tt(col(16), col(16), col(24), ALU.add))
            vec.tensor_copy(exp_ix[:, :], col(40, TOPK)).then_inc(S["chosen"], 1)
            softmax_top(60, 2, TOPK)
            do(ts(col(62, TOPK), col(60, TOPK), col(59, 1), None, ALU.mult))
            assert st.n == R_TOPW, st.n
            v.wait_ge(S["route_pe"], 4)
            do(vec.tensor_copy(small[:, 4:6], bank[2][:, 0:TOPK]))
            v.wait_ge(S["route_dma"], 16 * (4 + 4 * TOPK))
            f = FE // P
            for i in range(TOPK):
                st.did(ts(w_down[:, i * f:(i + 1) * f, :], w_down[:, i * f:(i + 1) * f, :], small[:, 4 + i:5 + i], None, ALU.mult))
            do(ts(bias_down[:, :], b2_rows[:, 0, :], small[0:TN, 4:5], None, ALU.mult))
            do(vec.scalar_tensor_tensor(out=bias_down[:, :], in0=b2_rows[:, 1, :], scalar=small[0:TN, 5:6], in1=bias_down[:, :], op0=ALU.mult, op1=ALU.add))
            assert st.n == R_WEIGHTS, st.n
            dense("moe")


_INS = ["x", "src", "dst"] + [f"L0_gnn_{n}" for n in (
    "w_in", "b_in", "ln1_g", "ln1_b", "ln2_g", "ln2_b", "wq", "bq", "wk", "bk", "wv", "bv", "wo", "bo", "w1", "b1", "w2", "b2")] + [
    f"L0_ffn_{n}" for n in ("Wr", "br", "W1", "b1", "W2", "b2", "gamma", "beta")]


def kernel(**inputs):
    import numpy as _np
    import concourse.bacc as _bacc
    from concourse import mybir as _mybir
    from concourse.bass_utils import run_bass_kernel_spmd as _run

    nc = _bacc.Bacc("TRN2", target_bir_lowering=False, num_devices=1)
    arrays, args = {}, {}
    for name in _INS:
        a = _np.ascontiguousarray(inputs[name])
        arrays[f"in_{name}_dram"] = a
        args[name] = nc.dram_tensor(f"in_{name}_dram", a.shape, _mybir.dt.from_np(a.dtype), kind="ExternalInput").ap()
    out = nc.dram_tensor("out_0_dram", (N, D), _mybir.dt.float32, kind="ExternalOutput").ap()
    program(nc, args, out)
    r = _run(nc, [arrays], core_ids=[0])
    return r.results[0]["out_0_dram"]
```
